# Optimizing a Trainium2 kernel written in Bass

```python
import numpy as np
import jax
import jax.numpy as jnp

def _softmax(x, axis=-1):
    return jax.nn.softmax(x, axis=axis)

def _gelu(x):
    return jax.nn.gelu(x, approximate=True)

def _silu(x):
    return jax.nn.silu(x)

def _sigmoid(x):
    return jax.nn.sigmoid(x)

def _layernorm(x, axis=-1, eps=1e-05):
    m = jnp.mean(x, axis=axis, keepdims=True)
    v = jnp.var(x, axis=axis, keepdims=True)
    return (x - m) / jnp.sqrt(v + eps)

def _scatter_add(tgt, idx, src, axis=0):
    return tgt.at[idx].add(src)

def _segment_sum(src, seg, n):
    return jax.ops.segment_sum(src, seg, n)
kernel_name = 'mk_flamingo_gated_d4_seqx_r8_f17b95'

def setup_inputs(seed: int=0):
    np.random.seed(seed)
    _w = jnp.asarray

    def _rec_inputs():
        import jax
        import jax.numpy as jnp
        _rk = jax.random.key(seed)
        x = -0.000125 + 0.9999 * jax.random.normal(jax.random.fold_in(_rk, 1), (16, 64, 128), jnp.float32)
        _lenS = 64 - jax.random.randint(jax.random.fold_in(_rk, 7), (16,), 0, max(1, 64 // 4) + 1, jnp.int32)
        _lenS2 = 64 - jax.random.randint(jax.random.fold_in(_rk, 8), (16,), 0, max(1, 64 // 4) + 1, jnp.int32)
        _ctx_1024P = jax.random.normal(jax.random.fold_in(_rk, 11), (16, 16, 128), jnp.float32)
        _ctx_1024c = jax.random.dirichlet(jax.random.fold_in(_rk, 511), 0.3 * jnp.ones((16,), jnp.float32), (16, 64))
        _ctx_1024t = jnp.einsum('bsk,bkd->bsd', _ctx_1024c, _ctx_1024P)
        _ctx_1024t = _ctx_1024t * jax.lax.rsqrt(jnp.mean(jnp.square(_ctx_1024t)) + 1e-12) * 0.953939
        ctx_1024 = -1.52775e-05 + 0.999936 * (_ctx_1024t + 0.3 * jax.random.normal(jax.random.fold_in(_rk, 611), (16, 64, 128), jnp.float32))
        _validS = jnp.arange(64)[None, :] < _lenS[:, None]
        _validS2 = jnp.arange(64)[None, :] < _lenS2[:, None]
        _causal = jnp.tril(jnp.ones((64, 64), dtype=bool))
        mask_BxS_ff1 = jnp.where(jnp.ones((16, 64), dtype=bool), 1.0, 0.0).astype(jnp.float32)
        mask_BxS2_ik0 = jnp.where(jnp.broadcast_to(_validS2[:, :], (16, 64)), 0, 1).astype(jnp.int32)
        _g = jax.random.normal(jax.random.fold_in(_rk, 9001), (2, 4), jnp.float32)
        _g = jnp.sign(_g) * jnp.maximum(jnp.abs(_g), 1.0) + (_g == 0) * 1.0
        g_xattn = _g[0]
        g_ffn = _g[1]
        return (x, ctx_1024, mask_BxS_ff1, mask_BxS2_ik0, g_xattn, g_ffn)
    x, ctx_1024, mask_BxS_ff1, mask_BxS2_ik0, g_xattn, g_ffn = _rec_inputs()

    def _L0_xattn_setup():
        import jax, jax.numpy as jnp
        import numpy as np
        DECAY = 0.9
        key = jax.random.key(seed)
        k1, k2, k3 = jax.random.split(key, 3)
        B, S, D = (8, 512, 128)
        q = jax.random.normal(k1, (B, S, D), dtype=jnp.float32)
        k = jax.random.normal(k2, (B, S, D), dtype=jnp.float32)
        v = jax.random.normal(k3, (B, S, D), dtype=jnp.float32)
        return {'q': q, 'k': k, 'v': v}
    _L0_xattn_all = _L0_xattn_setup()
    _L0_xattn_in = {k: v for k, v in _L0_xattn_all.items() if k in ()}
    del _L0_xattn_all

    def _L0_ffn_setup():
        import jax, jax.numpy as jnp
        import numpy as np
        NUM_EXPERTS = 8
        TOP_K = 2
        D = 128
        H = 4 * D
        B, S = (4, 256)
        key = jax.random.key(seed)
        ks = jax.random.split(key, 8)
        s = 0.02
        return {'x': jax.random.normal(ks[0], (B, S, D), dtype=jnp.float32), 'gate_w': jax.random.normal(ks[1], (NUM_EXPERTS, D), dtype=jnp.float32) * s, 'gate_b': jnp.zeros((NUM_EXPERTS,), dtype=jnp.float32), 'w1': jax.random.normal(ks[2], (NUM_EXPERTS, D, H), dtype=jnp.float32) * s, 'b1': jnp.zeros((NUM_EXPERTS, H), dtype=jnp.float32), 'w2': jax.random.normal(ks[3], (NUM_EXPERTS, H, D), dtype=jnp.float32) * s, 'b2': jnp.zeros((NUM_EXPERTS, D), dtype=jnp.float32)}
    _L0_ffn_all = _L0_ffn_setup()
    _L0_ffn_in = {k: v for k, v in _L0_ffn_all.items() if k in ('gate_w', 'gate_b', 'w1', 'b1', 'w2', 'b2')}
    del _L0_ffn_all

    def _L1_xattn_setup():
        import jax, jax.numpy as jnp
        import numpy as np
        B, SQ, SKV, D, H = (2, 256, 256, 128, 16)
        HD = D // H
        ROPE_BASE = 10000.0

        def _rope_interleaved(x):
            s, hd = (x.shape[1], x.shape[-1])
            dim = hd // 2
            freqs = jnp.exp(-jnp.arange(dim, dtype=x.dtype) * jnp.log(jnp.asarray(ROPE_BASE, x.dtype)) / dim)
            ang = jnp.arange(s, dtype=x.dtype)[:, None] * freqs[None, :]
            cos = jnp.cos(ang)[None, :, None, :]
            sin = jnp.sin(ang)[None, :, None, :]
            xe, xo = (x[..., ::2], x[..., 1::2])
            re = xe * cos - xo * sin
            ro = xe * sin + xo * cos
            return jnp.stack([re, ro], axis=-1).reshape(x.shape)
        key = jax.random.key(seed)
        ks = jax.random.split(key, 6)
        s = 1.0 / np.sqrt(D)
        return {'x_q': jax.random.normal(ks[0], (B, SQ, D), jnp.float32), 'x_kv': jax.random.normal(ks[1], (B, SKV, D), jnp.float32), 'wq': jax.random.normal(ks[2], (D, D), jnp.float32) * s, 'bq': jnp.zeros((D,), jnp.float32), 'wk': jax.random.normal(ks[3], (D, D), jnp.float32) * s, 'bk': jnp.zeros((D,), jnp.float32), 'wv': jax.random.normal(ks[4], (D, D), jnp.float32) * s, 'bv': jnp.zeros((D,), jnp.float32), 'wo': jax.random.normal(ks[5], (D, D), jnp.float32) * s, 'bo': jnp.zeros((D,), jnp.float32)}
    _L1_xattn_all = _L1_xattn_setup()
    _L1_xattn_in = {k: v for k, v in _L1_xattn_all.items() if k in ('wq', 'bq', 'wk', 'bk', 'wv', 'bv', 'wo', 'bo')}
    del _L1_xattn_all

    def _L1_ffn_setup():
        import jax, jax.numpy as jnp
        import numpy as np
        E = 8
        TOPK = 2

        def _moe_forward(x, Wg, W1, W2, W3):
            B, S, D = x.shape
            xt = x.reshape(-1, D)
            T = xt.shape[0]
            logits = xt @ Wg.T
            scores = jax.nn.softmax(logits, axis=-1)
            w, idx = jax.lax.top_k(scores, TOPK)
            w = w / (w.sum(axis=-1, keepdims=True) + 1e-20)
            cw = jnp.zeros((T, E), xt.dtype).at[jnp.arange(T)[:, None], idx].add(w)
            h = jax.nn.silu(jnp.einsum('td,ehd->teh', xt, W1)) * jnp.einsum('td,ehd->teh', xt, W3)
            out = jnp.einsum('teh,edh->ted', h, W2)
            y = jnp.einsum('te,ted->td', cw, out)
            return y.reshape(B, S, D)
        key = jax.random.key(seed)
        k0, k1, k2, k3, k4 = jax.random.split(key, 5)
        B, S, D, H = (1, 256, 128, 352)
        scale = 0.02
        x = jax.random.normal(k0, (B, S, D), jnp.float32)
        Wg = jax.random.normal(k1, (E, D), jnp.float32) * scale
        W1 = jax.random.normal(k2, (E, H, D), jnp.float32) * scale
        W2 = jax.random.normal(k3, (E, D, H), jnp.float32) * scale
        W3 = jax.random.normal(k4, (E, H, D), jnp.float32) * scale
        return {'x': x, 'Wg': Wg, 'W1': W1, 'W2': W2, 'W3': W3}
    _L1_ffn_all = _L1_ffn_setup()
    _L1_ffn_in = {k: v for k, v in _L1_ffn_all.items() if k in ('Wg', 'W1', 'W2', 'W3')}
    del _L1_ffn_all

    def _L2_xattn_setup():
        import jax, jax.numpy as jnp
        import numpy as np
        B, F, T, D = (8, 32, 32, 128)
        NEG = -1e+30
        key = jax.random.key(seed)
        ks = jax.random.split(key, 10)
        s = 1.0 / np.sqrt(D)
        return {'features': jax.random.normal(ks[0], (B, F, D), jnp.float32), 'masks': jnp.ones((B, F), jnp.float32), 'textual_features': jax.random.normal(ks[1], (B, T, D), jnp.float32), 'q_masks': jax.random.randint(ks[2], (B, T), 0, 2, jnp.int32), 'Ws': jax.random.normal(ks[3], (D, D), jnp.float32) * s, 'W': jax.random.normal(ks[4], (D, D), jnp.float32) * s, 'w': jax.random.normal(ks[5], (D, 1), jnp.float32) * s, 'b': jax.random.normal(ks[6], (1, D), jnp.float32) * s, 'Wcw': jax.random.normal(ks[7], (1, D), jnp.float32) * s, 'bcw': jnp.zeros((1,), jnp.float32), 'Wcb': jax.random.normal(ks[8], (1, D), jnp.float32) * s, 'bcb': jnp.zeros((1,), jnp.float32)}
    _L2_xattn_all = _L2_xattn_setup()
    _L2_xattn_in = {k: v for k, v in _L2_xattn_all.items() if k in ('Ws', 'W', 'w', 'b', 'Wcw', 'bcw', 'Wcb', 'bcb')}
    del _L2_xattn_all

    def _L2_ffn_setup():
        import jax, jax.numpy as jnp
        import numpy as np
        TOPK = 4
        N_GROUPS = 4
        TOPK_GROUPS = 2
        ROUTE_SCALE = 2.5

        def _gate(x2, Wg):
            T = x2.shape[0]
            E = Wg.shape[0]
            scores = x2 @ Wg.T
            s = jax.nn.sigmoid(scores)
            g = s.reshape(T, N_GROUPS, E // N_GROUPS)
            group_scores = g.max(axis=-1)
            _, gidx = jax.lax.top_k(group_scores, TOPK_GROUPS)
            group_mask = jnp.any(jax.nn.one_hot(gidx, N_GROUPS, dtype=jnp.bool_), axis=1)
            masked = jnp.where(group_mask[:, :, None], g, -jnp.inf).reshape(T, E)
            _, idx = jax.lax.top_k(masked, TOPK)
            w = jnp.take_along_axis(s, idx, axis=1)
            w = w / jnp.sum(w, axis=-1, keepdims=True)
            w = w * ROUTE_SCALE
            return (w.astype(x2.dtype), idx)
        key = jax.random.key(seed)
        ks = jax.random.split(key, 6)
        B, S, D, I, E = (2, 256, 128, 128, 16)
        scale = 0.02
        return {'x': jax.random.normal(ks[0], (B, S, D), dtype=jnp.float32), 'Wg': jax.random.normal(ks[1], (E, D), dtype=jnp.float32) * scale, 'W1': jax.random.normal(ks[2], (E, I, D), dtype=jnp.float32) * scale, 'b1': jnp.zeros((E, I), dtype=jnp.float32), 'W2': jax.random.normal(ks[3], (E, D, I), dtype=jnp.float32) * scale, 'b2': jnp.zeros((E, D), dtype=jnp.float32), 'W3': jax.random.normal(ks[4], (E, I, D), dtype=jnp.float32) * scale, 'b3': jnp.zeros((E, I), dtype=jnp.float32)}
    _L2_ffn_all = _L2_ffn_setup()
    _L2_ffn_in = {k: v for k, v in _L2_ffn_all.items() if k in ('Wg', 'W1', 'b1', 'W2', 'b2', 'W3', 'b3')}
    del _L2_ffn_all

    def _L3_xattn_setup():
        import jax, jax.numpy as jnp
        import numpy as np
        D_MODEL = 128
        N_HEADS = 16
        D_K = D_MODEL // N_HEADS
        ROPE_BASE = 10000.0

        def rope_cos_sin(seq_len, d_k, base=ROPE_BASE, dtype=jnp.float32):
            inv_freq = 1.0 / base ** (jnp.arange(0, d_k, 2, dtype=dtype) / d_k)
            pos = jnp.arange(seq_len, dtype=dtype)
            freqs = jnp.outer(pos, inv_freq)
            return (jnp.cos(freqs), jnp.sin(freqs))

        def apply_rope(x, cos, sin):
            x1 = x[..., 0::2]
            x2 = x[..., 1::2]
            c = cos[None, None]
            s = sin[None, None]
            r1 = x1 * c - x2 * s
            r2 = x1 * s + x2 * c
            return jnp.stack([r1, r2], axis=-1).reshape(x.shape)
        key = jax.random.key(seed)
        ks = jax.random.split(key, 7)
        B, T = (2, 256)
        q = jax.random.normal(ks[0], (B, T, D_MODEL), dtype=jnp.float32)
        k = jax.random.normal(ks[1], (B, T, D_MODEL), dtype=jnp.float32)
        v = jax.random.normal(ks[2], (B, T, D_MODEL), dtype=jnp.float32)
        scale = 1.0 / np.sqrt(D_MODEL)
        W_q = jax.random.normal(ks[3], (D_MODEL, D_MODEL), dtype=jnp.float32) * scale
        W_k = jax.random.normal(ks[4], (D_MODEL, D_MODEL), dtype=jnp.float32) * scale
        W_v = jax.random.normal(ks[5], (D_MODEL, D_MODEL), dtype=jnp.float32) * scale
        W_o = jax.random.normal(ks[6], (D_MODEL, D_MODEL), dtype=jnp.float32) * scale
        return {'q': q, 'k': k, 'v': v, 'W_q': W_q, 'W_k': W_k, 'W_v': W_v, 'W_o': W_o}
    _L3_xattn_all = _L3_xattn_setup()
    _L3_xattn_in = {k: v for k, v in _L3_xattn_all.items() if k in ('W_q', 'W_k', 'W_v', 'W_o')}
    del _L3_xattn_all

    def _L3_ffn_setup():
        import jax, jax.numpy as jnp
        import numpy as np
        H, F, E_SHARED, E_ROUTED, K = (128, 512, 1, 8, 2)

        def _expert(x, w_up, w_down):
            h = jax.nn.gelu(jnp.einsum('bsh,hf->bsf', x, w_up), approximate=False)
            return jnp.einsum('bsf,fh->bsh', h, w_down)
        key = jax.random.key(seed)
        ks = jax.random.split(key, 6)
        x = jax.random.normal(ks[0], (4, 256, H), dtype=jnp.float32)
        s = 0.02
        shared_up = jax.random.normal(ks[1], (E_SHARED, H, F), dtype=jnp.float32) * s
        shared_down = jax.random.normal(ks[2], (E_SHARED, F, H), dtype=jnp.float32) * s
        routed_up = jax.random.normal(ks[3], (E_ROUTED, H, F), dtype=jnp.float32) * s
        routed_down = jax.random.normal(ks[4], (E_ROUTED, F, H), dtype=jnp.float32) * s
        router_w = jax.random.normal(ks[5], (H, E_ROUTED), dtype=jnp.float32) * s
        return {'x': x, 'shared_up': shared_up, 'shared_down': shared_down, 'routed_up': routed_up, 'routed_down': routed_down, 'router_w': router_w}
    _L3_ffn_all = _L3_ffn_setup()
    _L3_ffn_in = {k: v for k, v in _L3_ffn_all.items() if k in ('shared_up', 'shared_down', 'routed_up', 'routed_down', 'router_w')}
    del _L3_ffn_all
    return {'x': x, 'ctx_1024': ctx_1024, 'mask_BxS_ff1': mask_BxS_ff1, 'mask_BxS2_ik0': mask_BxS2_ik0, 'g_xattn': g_xattn, 'g_ffn': g_ffn, 'L0_ffn_gate_w': _L0_ffn_in['gate_w'], 'L0_ffn_gate_b': _L0_ffn_in['gate_b'], 'L0_ffn_w1': _L0_ffn_in['w1'], 'L0_ffn_b1': _L0_ffn_in['b1'], 'L0_ffn_w2': _L0_ffn_in['w2'], 'L0_ffn_b2': _L0_ffn_in['b2'], 'L1_xattn_wq': _L1_xattn_in['wq'], 'L1_xattn_bq': _L1_xattn_in['bq'], 'L1_xattn_wk': _L1_xattn_in['wk'], 'L1_xattn_bk': _L1_xattn_in['bk'], 'L1_xattn_wv': _L1_xattn_in['wv'], 'L1_xattn_bv': _L1_xattn_in['bv'], 'L1_xattn_wo': _L1_xattn_in['wo'], 'L1_xattn_bo': _L1_xattn_in['bo'], 'L1_ffn_Wg': _L1_ffn_in['Wg'], 'L1_ffn_W1': _L1_ffn_in['W1'], 'L1_ffn_W2': _L1_ffn_in['W2'], 'L1_ffn_W3': _L1_ffn_in['W3'], 'L2_xattn_Ws': _L2_xattn_in['Ws'], 'L2_xattn_W': _L2_xattn_in['W'], 'L2_xattn_w': _L2_xattn_in['w'], 'L2_xattn_b': _L2_xattn_in['b'], 'L2_xattn_Wcw': _L2_xattn_in['Wcw'], 'L2_xattn_bcw': _L2_xattn_in['bcw'], 'L2_xattn_Wcb': _L2_xattn_in['Wcb'], 'L2_xattn_bcb': _L2_xattn_in['bcb'], 'L2_ffn_Wg': _L2_ffn_in['Wg'], 'L2_ffn_W1': _L2_ffn_in['W1'], 'L2_ffn_b1': _L2_ffn_in['b1'], 'L2_ffn_W2': _L2_ffn_in['W2'], 'L2_ffn_b2': _L2_ffn_in['b2'], 'L2_ffn_W3': _L2_ffn_in['W3'], 'L2_ffn_b3': _L2_ffn_in['b3'], 'L3_xattn_W_q': _L3_xattn_in['W_q'], 'L3_xattn_W_k': _L3_xattn_in['W_k'], 'L3_xattn_W_v': _L3_xattn_in['W_v'], 'L3_xattn_W_o': _L3_xattn_in['W_o'], 'L3_ffn_shared_up': _L3_ffn_in['shared_up'], 'L3_ffn_shared_down': _L3_ffn_in['shared_down'], 'L3_ffn_routed_up': _L3_ffn_in['routed_up'], 'L3_ffn_routed_down': _L3_ffn_in['routed_down'], 'L3_ffn_router_w': _L3_ffn_in['router_w']}

def reference(x, ctx_1024, mask_BxS_ff1, mask_BxS2_ik0, g_xattn, g_ffn, L0_ffn_gate_w, L0_ffn_gate_b, L0_ffn_w1, L0_ffn_b1, L0_ffn_w2, L0_ffn_b2, L1_xattn_wq, L1_xattn_bq, L1_xattn_wk, L1_xattn_bk, L1_xattn_wv, L1_xattn_bv, L1_xattn_wo, L1_xattn_bo, L1_ffn_Wg, L1_ffn_W1, L1_ffn_W2, L1_ffn_W3, L2_xattn_Ws, L2_xattn_W, L2_xattn_w, L2_xattn_b, L2_xattn_Wcw, L2_xattn_bcw, L2_xattn_Wcb, L2_xattn_bcb, L2_ffn_Wg, L2_ffn_W1, L2_ffn_b1, L2_ffn_W2, L2_ffn_b2, L2_ffn_W3, L2_ffn_b3, L3_xattn_W_q, L3_xattn_W_k, L3_xattn_W_v, L3_xattn_W_o, L3_ffn_shared_up, L3_ffn_shared_down, L3_ffn_routed_up, L3_ffn_routed_down, L3_ffn_router_w):
    import jax
    import jax.numpy as jnp

    def _L0_xattn_ref(q, k, v):
        import jax, jax.numpy as jnp
        import numpy as np
        DECAY = 0.9
        kv = jnp.swapaxes(k * v, 0, 1)

        def step(r, kv_t):
            r = DECAY * r + kv_t
            return (r, r)
        r0 = jnp.zeros(q.shape[:1] + q.shape[2:], dtype=q.dtype)
        _, rs = jax.lax.scan(step, r0, kv)
        return q * jnp.swapaxes(rs, 0, 1)

    def _L0_ffn_ref(x, gate_w, gate_b, w1, b1, w2, b2):
        import jax, jax.numpy as jnp
        import numpy as np
        NUM_EXPERTS = 8
        TOP_K = 2
        D = 128
        H = 4 * D
        B, S = (4, 256)
        orig_shape = x.shape
        xf = x.reshape(-1, orig_shape[-1])
        gates = xf @ gate_w.T + gate_b
        weights, indices = jax.lax.top_k(gates, TOP_K)
        weights = jax.nn.softmax(weights, axis=-1)
        out = jnp.zeros_like(xf)
        for e in range(NUM_EXPERTS):
            w_e = jnp.sum(weights * (indices == e), axis=-1, keepdims=True)
            h = jax.nn.gelu(xf @ w1[e] + b1[e], approximate=False)
            out = out + w_e * (h @ w2[e] + b2[e])
        return out.reshape(orig_shape)

    def _L1_xattn_ref(x_q, x_kv, wq, bq, wk, bk, wv, bv, wo, bo):
        import jax, jax.numpy as jnp
        import numpy as np
        B, SQ, SKV, D, H = (2, 256, 256, 128, 16)
        HD = D // H
        ROPE_BASE = 10000.0

        def _rope_interleaved(x):
            s, hd = (x.shape[1], x.shape[-1])
            dim = hd // 2
            freqs = jnp.exp(-jnp.arange(dim, dtype=x.dtype) * jnp.log(jnp.asarray(ROPE_BASE, x.dtype)) / dim)
            ang = jnp.arange(s, dtype=x.dtype)[:, None] * freqs[None, :]
            cos = jnp.cos(ang)[None, :, None, :]
            sin = jnp.sin(ang)[None, :, None, :]
            xe, xo = (x[..., ::2], x[..., 1::2])
            re = xe * cos - xo * sin
            ro = xe * sin + xo * cos
            return jnp.stack([re, ro], axis=-1).reshape(x.shape)
        b, sq, _ = x_q.shape
        skv = x_kv.shape[1]
        q = (jnp.einsum('bsd,ed->bse', x_q, wq) + bq).reshape(b, sq, H, HD)
        k = (jnp.einsum('bsd,ed->bse', x_kv, wk) + bk).reshape(b, skv, H, HD)
        v = (jnp.einsum('bsd,ed->bse', x_kv, wv) + bv).reshape(b, skv, H, HD)
        q = _rope_interleaved(q)
        k = _rope_interleaved(k)
        scores = jnp.einsum('bqhd,bkhd->bhqk', q, k) / jnp.sqrt(jnp.asarray(HD, q.dtype))
        attn = jax.nn.softmax(scores, axis=-1)
        ctx = jnp.einsum('bhqk,bkhd->bqhd', attn, v).reshape(b, sq, D)
        return jnp.einsum('bsd,ed->bse', ctx, wo) + bo

    def _L1_ffn_ref(x, Wg, W1, W2, W3):
        import jax, jax.numpy as jnp
        import numpy as np
        E = 8
        TOPK = 2

        def _moe_forward(x, Wg, W1, W2, W3):
            B, S, D = x.shape
            xt = x.reshape(-1, D)
            T = xt.shape[0]
            logits = xt @ Wg.T
            scores = jax.nn.softmax(logits, axis=-1)
            w, idx = jax.lax.top_k(scores, TOPK)
            w = w / (w.sum(axis=-1, keepdims=True) + 1e-20)
            cw = jnp.zeros((T, E), xt.dtype).at[jnp.arange(T)[:, None], idx].add(w)
            h = jax.nn.silu(jnp.einsum('td,ehd->teh', xt, W1)) * jnp.einsum('td,ehd->teh', xt, W3)
            out = jnp.einsum('teh,edh->ted', h, W2)
            y = jnp.einsum('te,ted->td', cw, out)
            return y.reshape(B, S, D)
        return _moe_forward(x, Wg, W1, W2, W3)

    def _L2_xattn_ref(features, masks, textual_features, q_masks, Ws, W, w, b, Wcw, bcw, Wcb, bcb):
        import jax, jax.numpy as jnp
        import numpy as np
        B, F, T, D = (8, 32, 32, 128)
        NEG = -1e+30
        txt_proj = jnp.einsum('btd,de->bte', textual_features, Ws)
        feat_proj = jnp.einsum('bfd,de->bfe', features, W)
        h = jnp.tanh(txt_proj[:, None, :, :] + feat_proj[:, :, None, :] + b[None, None, :, :][..., 0, :])
        rho = jnp.einsum('bftd,d->bft', h, w[:, 0])
        qm = q_masks.astype(jnp.float32)
        rho = rho + (1.0 - qm)[:, None, :] * NEG
        att = jax.nn.softmax(rho, axis=-1)
        txt_h = jnp.einsum('bft,btd->bfd', att, textual_features)
        w_s = jnp.tanh(jnp.einsum('bfd,od->bfo', txt_h, Wcw) + bcw)
        b_s = jnp.tanh(jnp.einsum('bfd,od->bfo', txt_h, Wcb) + bcb)
        return w_s * features + b_s

    def _L2_ffn_ref(x, Wg, W1, b1, W2, b2, W3, b3):
        import jax, jax.numpy as jnp
        import numpy as np
        TOPK = 4
        N_GROUPS = 4
        TOPK_GROUPS = 2
        ROUTE_SCALE = 2.5

        def _gate(x2, Wg):
            T = x2.shape[0]
            E = Wg.shape[0]
            scores = x2 @ Wg.T
            s = jax.nn.sigmoid(scores)
            g = s.reshape(T, N_GROUPS, E // N_GROUPS)
            group_scores = g.max(axis=-1)
            _, gidx = jax.lax.top_k(group_scores, TOPK_GROUPS)
            group_mask = jnp.any(jax.nn.one_hot(gidx, N_GROUPS, dtype=jnp.bool_), axis=1)
            masked = jnp.where(group_mask[:, :, None], g, -jnp.inf).reshape(T, E)
            _, idx = jax.lax.top_k(masked, TOPK)
            w = jnp.take_along_axis(s, idx, axis=1)
            w = w / jnp.sum(w, axis=-1, keepdims=True)
            w = w * ROUTE_SCALE
            return (w.astype(x2.dtype), idx)
        shape = x.shape
        D = shape[-1]
        x2 = x.reshape(-1, D)
        weights, indices = _gate(x2, Wg)
        E = Wg.shape[0]
        y = jnp.zeros_like(x2)
        for e in range(E):
            we = jnp.sum(weights * (indices == e), axis=-1)
            h = jax.nn.silu(x2 @ W1[e].T + b1[e]) * (x2 @ W3[e].T + b3[e])
            y = y + (h @ W2[e].T + b2[e]) * we[:, None]
        return y.reshape(shape)

    def _L3_xattn_ref(q, k, v, W_q, W_k, W_v, W_o):
        import jax, jax.numpy as jnp
        import numpy as np
        D_MODEL = 128
        N_HEADS = 16
        D_K = D_MODEL // N_HEADS
        ROPE_BASE = 10000.0

        def rope_cos_sin(seq_len, d_k, base=ROPE_BASE, dtype=jnp.float32):
            inv_freq = 1.0 / base ** (jnp.arange(0, d_k, 2, dtype=dtype) / d_k)
            pos = jnp.arange(seq_len, dtype=dtype)
            freqs = jnp.outer(pos, inv_freq)
            return (jnp.cos(freqs), jnp.sin(freqs))

        def apply_rope(x, cos, sin):
            x1 = x[..., 0::2]
            x2 = x[..., 1::2]
            c = cos[None, None]
            s = sin[None, None]
            r1 = x1 * c - x2 * s
            r2 = x1 * s + x2 * c
            return jnp.stack([r1, r2], axis=-1).reshape(x.shape)
        B, T_q, _ = q.shape
        T_k = k.shape[1]
        Q = (q @ W_q.T).reshape(B, T_q, N_HEADS, D_K).transpose(0, 2, 1, 3)
        K = (k @ W_k.T).reshape(B, T_k, N_HEADS, D_K).transpose(0, 2, 1, 3)
        V = (v @ W_v.T).reshape(B, T_k, N_HEADS, D_K).transpose(0, 2, 1, 3)
        cos_q, sin_q = rope_cos_sin(T_q, D_K)
        cos_k, sin_k = rope_cos_sin(T_k, D_K)
        Q = apply_rope(Q, cos_q, sin_q)
        K = apply_rope(K, cos_k, sin_k)
        scale = jnp.sqrt(jnp.asarray(D_K, dtype=Q.dtype))
        scores = jnp.einsum('bhqd,bhkd->bhqk', Q, K) / scale
        attn = jax.nn.softmax(scores, axis=-1)
        out = jnp.einsum('bhqk,bhkd->bhqd', attn, V)
        out = out.transpose(0, 2, 1, 3).reshape(B, T_q, D_MODEL)
        return out @ W_o.T

    def _L3_ffn_ref(x, shared_up, shared_down, routed_up, routed_down, router_w):
        import jax, jax.numpy as jnp
        import numpy as np
        H, F, E_SHARED, E_ROUTED, K = (128, 512, 1, 8, 2)

        def _expert(x, w_up, w_down):
            h = jax.nn.gelu(jnp.einsum('bsh,hf->bsf', x, w_up), approximate=False)
            return jnp.einsum('bsf,fh->bsh', h, w_down)
        shared_out = jnp.zeros_like(x)
        for i in range(E_SHARED):
            shared_out = shared_out + _expert(x, shared_up[i], shared_down[i])
        probs = jax.nn.softmax(jnp.einsum('bsh,he->bse', x, router_w), axis=-1)
        top_k_prob, top_k_idx = jax.lax.top_k(probs, K)
        onehot = jax.nn.one_hot(top_k_idx, E_ROUTED, dtype=x.dtype)
        gates = jnp.einsum('bsk,bske->bse', top_k_prob, onehot)
        routed_out = jnp.zeros_like(x)
        for e in range(E_ROUTED):
            y = _expert(x, routed_up[e], routed_down[e])
            routed_out = routed_out + gates[..., e:e + 1] * y
        return shared_out + routed_out + x
    x = x + jnp.tanh(g_xattn[0]) * _L0_xattn_ref(_layernorm(x, axis=-1), ctx_1024, ctx_1024)
    x = x + jnp.tanh(g_ffn[0]) * _L0_ffn_ref(_layernorm(x, axis=-1), L0_ffn_gate_w, L0_ffn_gate_b, L0_ffn_w1, L0_ffn_b1, L0_ffn_w2, L0_ffn_b2)
    x = x + jnp.tanh(g_xattn[1]) * _L1_xattn_ref(_layernorm(x, axis=-1), ctx_1024, L1_xattn_wq, L1_xattn_bq, L1_xattn_wk, L1_xattn_bk, L1_xattn_wv, L1_xattn_bv, L1_xattn_wo, L1_xattn_bo)
    x = x + jnp.tanh(g_ffn[1]) * _L1_ffn_ref(_layernorm(x, axis=-1), L1_ffn_Wg, L1_ffn_W1, L1_ffn_W2, L1_ffn_W3)
    x = x + jnp.tanh(g_xattn[2]) * _L2_xattn_ref(_layernorm(x, axis=-1), mask_BxS_ff1, ctx_1024, mask_BxS2_ik0, L2_xattn_Ws, L2_xattn_W, L2_xattn_w, L2_xattn_b, L2_xattn_Wcw, L2_xattn_bcw, L2_xattn_Wcb, L2_xattn_bcb)
    x = x + jnp.tanh(g_ffn[2]) * _L2_ffn_ref(_layernorm(x, axis=-1), L2_ffn_Wg, L2_ffn_W1, L2_ffn_b1, L2_ffn_W2, L2_ffn_b2, L2_ffn_W3, L2_ffn_b3)
    x = x + jnp.tanh(g_xattn[3]) * _L3_xattn_ref(_layernorm(x, axis=-1), ctx_1024, ctx_1024, L3_xattn_W_q, L3_xattn_W_k, L3_xattn_W_v, L3_xattn_W_o)
    x = x + jnp.tanh(g_ffn[3]) * _L3_ffn_ref(_layernorm(x, axis=-1), L3_ffn_shared_up, L3_ffn_shared_down, L3_ffn_routed_up, L3_ffn_routed_down, L3_ffn_router_w)
    return x

_drawn_inputs = setup_inputs


def setup_inputs(seed=0):
    import zlib

    import numpy as np

    out = dict(_drawn_inputs(seed))
    spreads = {'L0_ffn_gate_b': (0.0, 0.8),
     'L0_ffn_b1': (0.0, 0.8),
     'L0_ffn_b2': (0.0, 0.8),
     'L1_xattn_bq': (0.0, 0.8),
     'L1_xattn_bk': (0.0, 0.8),
     'L1_xattn_bv': (0.0, 0.731),
     'L1_xattn_bo': (0.0, 0.733),
     'L2_ffn_b1': (0.0, 0.8),
     'L2_ffn_b2': (0.0, 0.69),
     'L2_ffn_b3': (0.0, 0.8)}
    factors = {'g_ffn': 8.0,
     'L0_ffn_gate_w': 8.0,
     'L0_ffn_w1': 8.0,
     'L0_ffn_w2': 8.0,
     'L1_ffn_Wg': 8.0,
     'L1_ffn_W1': 8.0,
     'L1_ffn_W2': 8.0,
     'L1_ffn_W3': 8.0,
     'L2_xattn_Ws': 4.755,
     'L2_xattn_W': 8.0,
     'L2_xattn_w': 4.83,
     'L2_xattn_b': 39.399,
     'L2_ffn_Wg': 5.671,
     'L2_ffn_W1': 8.0,
     'L2_ffn_W2': 8.0,
     'L2_ffn_W3': 8.0,
     'L3_xattn_W_q': 3.215,
     'L3_xattn_W_k': 3.101,
     'L3_ffn_shared_up': 8.0,
     'L3_ffn_shared_down': 8.0,
     'L3_ffn_routed_up': 8.0,
     'L3_ffn_routed_down': 8.0,
     'L3_ffn_router_w': 8.0}
    for name, (base, spread) in spreads.items():
        noise = np.random.default_rng([zlib.crc32(name.encode()), seed]).standard_normal(out[name].shape)
        drawn = base * np.exp(spread * noise) if base else spread * noise
        out[name] = jnp.asarray(drawn.astype(out[name].dtype))
    for name, factor in factors.items():
        out[name] = (out[name] * factor).astype(out[name].dtype)
    return out
```

```python
from contextlib import ExitStack

import numpy as np

import concourse.bass as bass
from concourse import mybir

F32 = mybir.dt.float32
F32R = mybir.dt.float32r
BF16 = mybir.dt.bfloat16
I32 = mybir.dt.int32
ACT = mybir.ActivationFunctionType
ALU = mybir.AluOpType
AX = mybir.AxisListType.X

P = 128
B, S = 16, 64
T = B * S
TILES = T // P
HALF = T // 2
HT = TILES // 2
HEADS, HD = 16, 8
PAIRS = B // 2
EPS = 1e-5
DECAY = 0.9
NEG = -1e30


class Moe:

    def __init__(self, layer, experts, hidden, gated, unroll, topk, routed=None, biases=0):
        self.biases = biases
        self.layer, self.experts, self.gated, self.unroll, self.topk = layer, experts, gated, unroll, topk
        self.routed = routed or experts
        self.chunks = [(f, min(P, hidden - f)) for f in range(0, hidden, P)]
        self.n = len(self.chunks) * (2 if gated else 1)
        self.steps = self.n * unroll
        self.up = hidden * (2 if gated else 1)
        self.split = self.up + P * len(self.chunks)
        self.width = self.split + biases
        self.hidden = hidden
        self.total = self.n * experts
        self.bodies = -(-experts // unroll)
        self.loop_end = (experts - 2 * unroll) // unroll + 1

    def run(self, eng, body):
        body(0)
        if self.loop_end > 1:
            with eng.Fori(1, self.loop_end) as it:
                body(it)
        for it in range(max(self.loop_end, 1), self.bodies):
            body(it)


MOES = [
    Moe(0, 8, 512, False, 2, 2, biases=5),
    Moe(1, 8, 352, True, 2, 2),
    Moe(2, 16, 128, True, 4, 4, biases=3),
    Moe(3, 9, 512, False, 2, 2, routed=8),
]


def bcast(ap, dim, count):
    shape = list(ap.shape)
    return ap.unsqueeze(dim).broadcast_to(shape[:dim] + [count] + shape[dim:])


def flamingo(nc, a, out):
    ctx = ExitStack()
    with ctx:
        def sb(name, shape, dt=F32):
            return ctx.enter_context(nc.sbuf_tensor(name, shape, dt))

        def sem(name):
            return ctx.enter_context(nc.semaphore(name))

        x = sb("x", [P, T])
        n = sb("n", [P, T])
        n_hi = sb("n_hi", [P, T], F32R)
        n_lo = sb("n_lo", [P, T], F32R)
        xc = sb("xc", [P, T])
        sq = sb("sq", [P, T])
        diag = sb("diag", [P, T])
        ctxT = sb("ctxT", [P, T])
        kT = [sb("kT1", [P, T]), sb("kT3", [P, T])]
        vblk = [sb("vblk1", [P, B, 8, 18]), sb("vblk3", [P, B, 8, 18])]
        txt = sb("txt", [P, T])
        uv = sb("uv", [P, 2, S])
        work = sb("work", [P, 12 * T])
        wslot = max(m.width * m.unroll for m in MOES)
        w_f32 = sb("w_f32", [P, wslot])
        w_hi = sb("w_hi", [P, wslot], F32R)
        w_lo = sb("w_lo", [P, wslot], F32R)
        w_bias = sb("w_bias", [P, 4, 5])
        h_act = sb("h_act", [P, 2, T])
        h_hi = sb("h_hi", [P, 2, T], F32R)
        h_lo = sb("h_lo", [P, 2, T], F32R)
        g_sb = sb("g_sb", [P, 2, T])
        y_g = sb("y_g", [P, 2, T])

        ident = sb("ident", [P, P])
        ident16 = sb("ident16", [P, P], BF16)
        mean_w = sb("mean_w", [P, P])
        ones_w = sb("ones_w", [P, P])
        minus_half = sb("minus_half", [P, TILES])
        tg = sb("tg", [P, 8])
        rope = sb("rope", [P, 4, S])
        hmask = sb("hmask", [P, HEADS])
        perm = sb("perm", [P, P])
        sel = {8: sb("sel8", [P, 8, P], BF16), 16: sb("sel16", [P, 16, P], BF16)}
        revi = {8: sb("revi8", [P, 8]), 16: sb("revi16", [P, 16]), 4: sb("revi4", [P, 4])}
        wqk = sb("wqk", [P, 12, P])
        abias = sb("abias", [P, 7])
        l2w = sb("l2w", [P, 2, P])
        l2pad = sb("l2pad", [P, 63])
        l2uvpad = sb("l2uvpad", [P, 2, 62])
        l2b = sb("l2b", [P, 3])
        qmask = sb("qmask", [P, S], I32)
        mbias = sb("mbias", [P, 2, S])
        wg = [sb(f"wg{m.layer}", [P, m.routed]) for m in MOES]
        gb0 = sb("gb0", [P, 8])
        var_eps = sb("var_eps", [P, TILES])
        rstd = sb("rstd", [P, TILES])
        rt = {k: sb(f"rt_{k}", [P, TILES, 16]) for k in ("lg", "cur", "e", "a", "c", "s", "sg", "w")}
        rt_m = sb("rt_m", [P, 4, 4 * TILES])
        gsp = sb("gsp", [P, TILES, 3 * 16], BF16)
        gT = sb("gT", [P, T], BF16)
        mx = sb("mx", [P, 2, HEADS])
        rsum = sb("rsum", [P, 2, HEADS])
        ao = sb("ao", [P, 2, P])
        st2 = sb("st2", [P, 6, 8])

        ps = ctx.enter_context(nc.psum_tensor("ps", [P, 8, 512], F32))

        kexp = work[:, 0:8 * T].rearrange("p (r b h k) -> p r b h k", r=4, b=2, h=HEADS)
        s_sub = work[:, 8 * T:10 * T].rearrange("p (r c) -> p r c", r=2)
        p_exp, p_tr = y_g, g_sb
        qT, aoT = xc, sq
        PSUMS = 2 * T
        sums = work[:, 0:6 * T].rearrange("p (r c) -> p r c", r=3)
        tanhs = work[:, 6 * T:12 * T].rearrange("p (r c) -> p r c", r=3)

        in_x, in_ctx, in_small = sem("in_x"), sem("in_ctx"), sem("in_small")
        consts = sem("consts")
        tg_ready = sem("tg_ready")
        dve_link, pool_link, act_link = sem("dve_link"), sem("pool_link"), sem("act_link")
        x_done = [sem("x_done0"), sem("x_done1")]
        ln = {k: sem(f"ln_{k}") for k in ("mean", "xc", "sq", "var", "eps", "rstd", "diag", "bc", "n", "hi", "lo")}
        pre = {k: sem(f"pre_{k}") for k in ("kv", "scan", "proj", "k", "v", "vcp", "txt", "txtcp", "uv", "uvcp", "wo")}
        at = {k: sem(f"at_{k}") for k in ("q", "qT", "kexp", "sc", "max", "sub", "exp", "tr", "trcp", "pv", "ao", "aot", "aocp", "proj")}
        x2 = {k: sem(f"x2_{k}") for k in ("feat", "fb", "sumA", "sumB", "tanh", "dot", "soft", "exp", "wb", "tw", "d", "bc", "mb")}
        once = {k: sem(f"rt_{k}") for k in ("logit", "cur", "e", "w", "gsp", "gtr", "gT")}
        mo = [{k: sem(f"m{m.layer}_{k}") for k in ["g_full", "gcp", "hid", "act", "hi", "h_ready", "h_used", "gate", "acc", "whu", "whd", "wlu", "wld"]
              + ["mul"] * m.gated + ["xn"] * (m.layer == 3)} for m in MOES]
        w_in = [[sem(f"w{m.layer}_in{u}") for u in range(m.unroll)] for m in MOES]
        s_out = sem("s_out")

        def linker(eng, s):
            count = [0]

            def link(ins):
                count[0] += 1
                ins.then_inc(s, 1)
                eng.wait_ge(s, count[0])
            return link

        def half(t):
            return slice(t * HALF, (t + 1) * HALF)

        def sum_of(g):
            b, f = g // 2, (g // 2) * S + 32 * (g % 2)
            return (sums[:, g % 3].rearrange("p (f s) -> p f s", s=S), bcast(xc[:, f:f + 32], 2, S), bcast(txt[:, b * S:(b + 1) * S], 1, 32))

        small = [
            (tg, "g_rows"), (ident, "c_ident"), (ident16, "c_ident16"), (rope, "c_rope"), (hmask, "c_hmask"), (perm, "c_perm"),
            (sel[8], "c_sel8"), (sel[16], "c_sel16"), (revi[8], "c_revi8"), (revi[16], "c_revi16"), (revi[4], "c_revi4"),
            (wqk, "w_attn"), (abias, "b_attn"), (l2w, "w_l2"), (l2pad, "w_l2pad"), (l2uvpad, "w_l2uv"), (l2b, "b_l2"), (qmask, "mask_rows"),
            (wg[0], "wg0"), (wg[1], "wg1"), (wg[2], "wg2"), (wg[3], "wg3"), (gb0, "gb0"),
        ]
        SMALL = 16 * len(small)

        block = ctx.enter_context(nc.Block())

        @block.sync
        def _(sp):
            sp.dma_start(x[:, :], a["xT"]).then_inc(in_x, 16)
            sp.dma_start(ctxT[:, :], a["ctxT"]).then_inc(in_ctx, 16)
            for tile, name in small:
                dst = tile[:] if tile.dtype != BF16 else tile[:].bitcast(mybir.dt.uint16)
                sp.dma_start(dst, a[name]).then_inc(in_small, 16)

            def load(m, u, e, body):
                dst = w_f32[:, u * m.width:(u + 1) * m.width]
                src = a[f"w{m.layer}"][bass.ds(e, 1)].rearrange("e p w -> (e p) w")
                sp.dma_start(dst, src).then_inc(w_in[m.layer][u], 16)

            for m in MOES:
                if m.layer:
                    sp.wait_ge(mo[m.layer - 1]["wld"], MOES[m.layer - 1].experts)
                for u in range(m.unroll):
                    load(m, u, u, 0)

                def body(it):
                    for u in range(m.unroll):
                        if not isinstance(it, int) or (it + 1) * m.unroll + u < m.experts:
                            sp.wait_ge(mo[m.layer]["wld"], it * m.unroll + u + 1)
                            load(m, u, (it + 1) * m.unroll + u, it)
                m.run(sp, body)

            for t in range(2):
                sp.wait_ge(x_done[t], 8)
                sp.dma_start(out[:, half(t)], x[:, half(t)]).then_inc(s_out, 16)
            sp.wait_ge(s_out, 32)

        @block.tensor
        def _(pe):
            def norm(j):
                for t in range(2):
                    if j:
                        pe.wait_ge(x_done[t], j)
                    elif t == 0:
                        pe.wait_ge(in_x, 16)
                        pe.wait_ge(consts, 1)
                    if j == 1 and t == 0:
                        pe.wait_ge(pre["uvcp"], 2)
                        pe.wait_ge(pre["txtcp"], 2)
                        pe.wait_ge(pre["vcp"], 8)
                    pe.matmul(ps[:, t], mean_w[:, :], x[:, half(t)], start=True, stop=True).then_inc(ln["mean"], 1)
                for t in range(2):
                    pe.wait_ge(ln["sq"], 2 * j + t + 1)
                    for i in range(HT):
                        c = t * HT + i
                        mm = pe.matmul(ps[:, 2 + t, i:i + 1], sq[:, c * P:(c + 1) * P], mean_w[:, 0:1], start=True, stop=True)
                    mm.then_inc(ln["var"], 1)
                for t in range(2):
                    pe.wait_ge(ln["diag"], 2 * j + t + 1)
                    pe.matmul(ps[:, 4 + t], ones_w[:, :], diag[:, half(t)], start=True, stop=True).then_inc(ln["bc"], 1)

            def prepare():
                pe.wait_ge(in_ctx, 16)
                pe.wait_ge(in_small, SMALL)
                for i, w0 in enumerate((2, 8)):
                    for t in range(2):
                        if 2 * i + t >= 2:
                            pe.wait_ge(pre["k"], 2 * i + t - 1)
                        slot = 2 * t
                        pe.matmul(ps[:, slot], wqk[:, w0], ctxT[:, half(t)], start=True, stop=True)
                        pe.matmul(ps[:, slot + 1], wqk[:, w0 + 1], ctxT[:, half(t)], start=True, stop=True).then_inc(pre["proj"], 1)
                for i, w0 in enumerate((4, 10)):
                    for q in range(4):
                        r = 4 * i + q
                        if r >= 2:
                            pe.wait_ge(pre["vcp"], r - 1)
                        for b in range(4 * q, 4 * q + 4):
                            for h2 in range(2):
                                mm = pe.matmul(ps[h2 * S:(h2 + 1) * S, 4 + r % 2, (b % 4) * P:(b % 4 + 1) * P],
                                               ctxT[:, b * S:(b + 1) * S], wqk[:, w0], start=True, stop=True)
                        mm.then_inc(pre["v"], 1)
                for t in range(2):
                    pe.matmul(ps[:, 6 + t], l2w[:, 0], ctxT[:, half(t)], start=True, stop=True).then_inc(pre["txt"], 1)
                pe.wait_ge(pre["k"], 4)
                for r in range(2):
                    for b in range(B):
                        for q in range(4):
                            mm = pe.matmul(ps[32 * q:32 * q + 32, r, 0:S], l2uvpad[:, r, 30 - 2 * b:62 - 2 * b],
                                           ctxT[:, b * S:(b + 1) * S], start=(b == 0), stop=(b == B - 1))
                    mm.then_inc(pre["uv"], 1)

            def attention(i):
                w0 = 6 * i
                for t in range(2):
                    pe.wait_ge(ln["n"], 2 * (2, 6)[i] + t + 1)
                    pe.matmul(ps[:, 2 * t], wqk[:, w0], n[:, half(t)], start=True, stop=True)
                    pe.matmul(ps[:, 2 * t + 1], wqk[:, w0 + 1], n[:, half(t)], start=True, stop=True).then_inc(at["q"], 1)
                base = PAIRS * i

                def scores(p):
                    g = base + p
                    pe.wait_ge(at["qT"], 2 * i + p // HT + 1)
                    if p < 2:
                        pe.wait_ge(at["qT"], 2 * i + 2)
                    else:
                        pe.wait_ge(at["sub"], g - 1)
                    pe.wait_ge(at["kexp"], g + 1)
                    for hh in range(2):
                        for b in range(2):
                            c = p * P + b * S
                            mm = pe.matmul(ps[b * S:(b + 1) * S, 2 * (p % 2) + hh], qT[:, c:c + S],
                                           kexp[:, p % 4, b, 8 * hh:8 * hh + 8], start=True, stop=True)
                    mm.then_inc(at["sc"], 1)

                def turn(p):
                    g = base + p
                    pe.wait_ge(at["exp"], g + 1)
                    for hp in range(8):
                        if hp % 4 == 0 and g:
                            pe.wait_ge(at["trcp"], 2 * g - 1 + hp // 4)
                        mm = pe.transpose(ps[:, 4 + hp // 4, (hp % 4) * P:(hp % 4 + 1) * P],
                                          p_exp[:, p % 2, hp * P:(hp + 1) * P], ident[:, :])
                        if hp % 4 == 3:
                            mm.then_inc(at["tr"], 1)

                def values(p):
                    g = base + p
                    if g:
                        pe.wait_ge(at["ao"], g)
                    for hp in range(8):
                        if hp % 4 == 0:
                            pe.wait_ge(at["trcp"], 2 * g + 1 + hp // 4)
                        for b in range(2):
                            mm = pe.matmul(ps[b * S:(b + 1) * S, 6, hp * 18:(hp + 1) * 18],
                                           p_tr[:, p % 2, hp * P + b * S:hp * P + (b + 1) * S],
                                           vblk[i][:, 2 * p + b, hp], start=True, stop=True)
                    mm.then_inc(at["pv"], 1)

                def turn_out(p):
                    g = base + p
                    pe.wait_ge(at["ao"], g + 1)
                    if g:
                        pe.wait_ge(at["aocp"], g)
                    if p == HT:
                        pe.wait_ge(x_done[0], (3, 7)[i])
                    pe.transpose(ps[:, 7, 0:P], ao[:, p % 2], ident[:, :]).then_inc(at["aot"], 1)

                def project(t):
                    pe.wait_ge(at["aocp"], base + HT * (t + 1))
                    pe.wait_ge(pre["wo"], i + 1)
                    pe.matmul(ps[:, 7], wqk[:, w0 + 5], aoT[:, half(t)], start=True, stop=True).then_inc(at["proj"], 1)

                scores(0)
                for p in range(PAIRS):
                    if p + 1 < PAIRS:
                        scores(p + 1)
                    turn(p)
                    if p:
                        turn_out(p - 1)
                    if p == HT:
                        project(0)
                    values(p)
                turn_out(PAIRS - 1)
                project(1)

            def pair_sums():
                for t in range(2):
                    pe.wait_ge(ln["n"], 2 * 4 + t + 1)
                    pe.matmul(ps[:, t], l2w[:, 1], n[:, half(t)], start=True, stop=True).then_inc(x2["feat"], 1)
                for g in range(2 * B):
                    pe.wait_ge(x2["tanh"], g + 1)
                    for q in range(4):
                        mm = pe.matmul(ps[32 * q:32 * q + 32, 6], l2pad[:, 31 - g:63 - g],
                                       tanhs[:, g % 3, q * 512:(q + 1) * 512], start=(g == 0), stop=(g == 2 * B - 1))
                    mm.then_inc(x2["dot"], 1)
                for r in range(2):
                    pe.wait_ge(x2["d"], r + 1)
                    for t in range(2):
                        pe.matmul(ps[:, 2 * r + t], ones_w[:, :], (diag, sq)[r][:, half(t)], start=True, stop=True).then_inc(x2["bc"], 1)

            def moe(m):
                s, L = mo[m.layer], m.layer
                j, N, U, E = 2 * L + 1, m.n, m.unroll, m.routed

                def wap(w, u, lo, size, rows=P):
                    return w[0:rows, u * m.width + lo:u * m.width + lo + size]

                def products(dst, w, u, lo, size, rows, hi, low, first=True, last=True):
                    passes = [(w_hi, hi), (w_hi, low), (w_lo, hi)]
                    for c, (wt, mv) in enumerate(passes):
                        for i in range(len(dst)):
                            mm = pe.matmul(dst[i], wap(wt, u, lo, size, rows), mv[i],
                                           start=(first and c == 0), stop=(last and c == 2))
                    return mm

                def up(it, k):
                    u, sl, step = (k // N) % U, k % 2, it * m.steps + k
                    if k % N == 0:
                        pe.wait_ge(s["wlu"], it * U + k // N + 1)
                    if not (isinstance(it, int) and step < 2):
                        pe.wait_ge(s["mul" if m.gated else "act"], step - 1)
                    if not m.gated:
                        f, size = m.chunks[k % N]
                        mm = products([ps[0:size, 2 * sl + t] for t in range(2)], w_hi, u, f, size, P,
                                      [n_hi[:, half(t)] for t in range(2)], [n_lo[:, half(t)] for t in range(2)])
                    else:
                        f, size = m.chunks[(k % N) // 2]
                        t = k % 2
                        for i in range(2):
                            mm = products([ps[0:size, 2 * sl + i]], w_hi, u, i * m.hidden + f, size, P, [n_hi[:, half(t)]], [n_lo[:, half(t)]])
                    mm.then_inc(s["hid"], 1)

                def down(it, k):
                    u, sl, step = (k // N) % U, k % 2, it * m.steps + k
                    pe.wait_ge(s["h_ready"], step + 1)
                    if k % N == 0:
                        pe.wait_ge(s["wld"], it * U + k // N + 1)
                        if not (isinstance(it, int) and step == 0):
                            pe.wait_ge(s["gate"], it * U + k // N)
                    ci = (k % N) // 2 if m.gated else k % N
                    f, size = m.chunks[ci]
                    ts = [k % 2] if m.gated else [0, 1]
                    hv = [[h[0:size, sl, 0:HALF] if m.gated else h[0:size, sl, half(t)] for t in ts] for h in (h_hi, h_lo)]
                    products([ps[:, 4 + t] for t in ts], w_hi, u, m.up + ci * P, P, size, hv[0], hv[1],
                             first=(ci == 0), last=(ci == len(m.chunks) - 1)).then_inc(s["h_used"], 1)

                def spread(it, k):
                    e = it * U + k // N
                    if isinstance(it, int) and e == 0:
                        pe.wait_ge(once["gT"], m.layer + 1)
                    else:
                        pe.wait_ge(s["gcp"], e)
                    for t in range(2):
                        mm = pe.matmul(ps[:, 6 + t], sel[E][:, bass.ds(e, 1)].rearrange("p a c -> p (a c)"), gT[:, half(t)], start=True, stop=True)
                    mm.then_inc(s["g_full"], 1)

                pe.wait_ge(ln["n"], 2 * j + 2)
                for c in range(TILES):
                    mm = pe.matmul(ps[:, 6, c * E:(c + 1) * E], n[:, c * P:(c + 1) * P], wg[L][:, :], start=True, stop=True)
                mm.then_inc(once["logit"], 1)
                pe.wait_ge(ln["lo"], 2 * L + 2)
                up(0, 0)
                up(0, 1)

                def body(it):
                    for k in range(m.steps):
                        if isinstance(it, int) and it * m.steps + k >= m.total:
                            break
                        if not isinstance(it, int) or it * m.steps + k + 2 < m.total:
                            up(it, k + 2)
                        if isinstance(it, int) and it == 0 and k == max(N - 2, 0):
                            pe.wait_ge(once["gsp"], m.layer + 1)
                            for c in range(TILES):
                                mm = pe.transpose(ps[0:3 * E, 7].bitcast(BF16)[:, c * P:(c + 1) * P], gsp[:, c, 0:3 * E], ident16[:, :])
                            mm.then_inc(once["gtr"], 1)
                        if k % N == N - 1 and not (isinstance(it, int) and it * U + k // N >= E):
                            spread(it, k)
                        down(it, k)
                m.run(pe, body)

            norm(0)
            prepare()
            norm(1)
            moe(MOES[0])
            norm(2)
            attention(0)
            norm(3)
            moe(MOES[1])
            norm(4)
            pair_sums()
            norm(5)
            moe(MOES[2])
            norm(6)
            attention(1)
            norm(7)
            moe(MOES[3])

        @block.scalar
        def _(act):
            link = linker(act, act_link)

            def norm(j):
                for t in range(2):
                    act.wait_ge(ln["xc"], 2 * j + t + 1)
                    act.activation(sq[:, half(t)], xc[:, half(t)], ACT.Square).then_inc(ln["sq"], 1)

            def split_hi(m, it, k):
                s, U = mo[m.layer], m.unroll
                u, e = k % U, it * U + k
                act.wait_ge(w_in[m.layer][u], 16 * (it + k // U + 1))
                if not (isinstance(it, int) and e < U):
                    act.wait_ge(s["h_used"], m.n * (e - U + 1))
                o = u * m.width
                act.copy(w_hi[:, o:o + m.up], w_f32[:, o:o + m.up]).then_inc(s["whu"], 1)
                if m.biases:
                    act.copy(w_hi[:, o + m.up:o + m.split], w_f32[:, o + m.up:o + m.split])
                    if not (isinstance(it, int) and e < U):
                        act.wait_ge(s["gate"], e - U + 1)
                    act.copy(w_bias[:, u, 0:m.biases], w_f32[:, o + m.split:o + m.width]).then_inc(s["whd"], 1)
                else:
                    act.copy(w_hi[:, o + m.up:o + m.split], w_f32[:, o + m.up:o + m.split]).then_inc(s["whd"], 1)

            def first_weights(m):
                if m.layer:
                    act.wait_ge(mo[m.layer - 1]["h_used"], MOES[m.layer - 1].total)
                for u in range(m.unroll):
                    split_hi(m, 0, u)

            def prepare():
                for t in range(2):
                    act.wait_ge(pre["txt"], t + 1)
                    act.copy(txt[:, half(t)], ps[:, 6 + t]).then_inc(pre["txtcp"], 1)
                for r in range(2):
                    act.wait_ge(pre["uv"], r + 1)
                    act.copy(uv[:, r], ps[:, r, 0:S]).then_inc(pre["uvcp"], 1)

            def attention(i):
                base = PAIRS * i

                def out_copy(p):
                    act.wait_ge(at["aot"], base + p + 1)
                    if i == 0:
                        ins = act.activation(aoT[:, p * P:(p + 1) * P], ps[:, 7, 0:P], ACT.Identity, bias=abias[:, 6:7])
                    else:
                        ins = act.copy(aoT[:, p * P:(p + 1) * P], ps[:, 7, 0:P])
                    ins.then_inc(at["aocp"], 1)

                for p in range(PAIRS):
                    act.wait_ge(at["sub"], base + p + 1)
                    if base + p >= 2:
                        act.wait_ge(at["tr"], 2 * (base + p) - 2)
                    act.activation(p_exp[:, p % 2], s_sub[:, p % 2], ACT.Exp).then_inc(at["exp"], 1)
                    for hh in range(2):
                        act.wait_ge(at["tr"], 2 * (base + p) + hh + 1)
                        if base + p >= 2:
                            act.wait_ge(at["pv"], base + p - 1)
                        act.copy(p_tr[:, p % 2, half(hh)], ps[:, 4 + hh]).then_inc(at["trcp"], 1)
                    if p:
                        out_copy(p - 1)
                out_copy(PAIRS - 1)

            def pair_sums():
                for g in range(2 * B):
                    s, v = ("sumB", g // 3 + 1) if g % 3 == 2 else ("sumA", g - g // 3 + 1)
                    act.wait_ge(x2[s], v)
                    if g >= 3:
                        act.wait_ge(x2["dot"], g - 2)
                    act.activation(tanhs[:, g % 3], sums[:, g % 3], ACT.Tanh).then_inc(x2["tanh"], 1)
                act.wait_ge(x2["soft"], 1)
                act.activation(h_act[:, 0, 0:512], h_act[:, 1, 0:512], ACT.Exp).then_inc(x2["exp"], 1)
                act.wait_ge(x2["wb"], 1)
                for r in range(2):
                    act.activation(st2[:, 4 + r], st2[:, 2 + r], ACT.Tanh, bias=l2b[:, 1 + r:2 + r]).then_inc(x2["tw"], 1)

            def moe(m):
                s, L = mo[m.layer], m.layer
                N, U, E = m.n, m.unroll, m.routed
                if L == 2:
                    act.wait_ge(once["logit"], m.layer + 1)
                    act.activation(rt["e"][:, :, 0:E], ps[:, 6, 0:TILES * E].rearrange("p (c e) -> p c e", e=E), ACT.Sigmoid).then_inc(once["e"], 1)
                else:
                    act.wait_ge(once["cur"], (1, 2, 0, 3)[m.layer])
                    act.activation(rt["e"][:, :, 0:E], rt["sg"][:, :, 0:E], ACT.Exp).then_inc(once["e"], 1)

                def hidden(it, k):
                    step, sl = it * m.steps + k, k % 2
                    act.wait_ge(s["hid"], step + 1)
                    if m.biases and k % N == 0:
                        act.wait_ge(s["whd"], it * U + k // N + 1)
                    if not (isinstance(it, int) and step < 2):
                        act.wait_ge(s["h_ready"], step - 1)
                    if m.gated:
                        size = m.chunks[(k % N) // 2][1]
                        kw = {"bias": w_bias[:, (k // N) % U, 0:1]} if L == 2 else {}
                        act.activation(h_act[0:size, sl, 0:HALF], ps[0:size, 2 * sl], ACT.Silu, **kw).then_inc(s["act"], 1)
                    else:
                        kw = {"bias": w_bias[:, (k // N) % U, k % N:k % N + 1]} if L == 0 else {}
                        act.activation(h_act[:, sl], ps[:, 2 * sl:2 * sl + 2].rearrange("p a c -> p (a c)"), ACT.Gelu, **kw).then_inc(s["act"], 1)

                def gates(it, k):
                    e = it * U + k
                    act.wait_ge(s["g_full"], e + 1)
                    if not (isinstance(it, int) and e < 2):
                        act.wait_ge(s["gate"], e - 1)
                    act.copy(g_sb[:, k % 2], ps[:, 6:8].rearrange("p a c -> p (a c)")).then_inc(s["gcp"], 1)

                def after(it, k):
                    if isinstance(it, int) and it == 0 and k == max(N - 2, 0) + 2:
                        act.wait_ge(once["gtr"], m.layer + 1)
                        act.copy(gT[0:3 * E, :], ps[0:3 * E, 7].bitcast(BF16)).then_inc(once["gT"], 1)
                    e = (k - 2) // N if (k - 2) % N == N - 1 else None
                    if e is not None and not (isinstance(it, int) and not 0 <= it * U + e < E):
                        gates(it, e)
                    e = (k - 3) // N if (k - 3) % N == N - 1 else None
                    if e is not None and not (isinstance(it, int) and not U <= it * U + e + U < m.experts):
                        split_hi(m, it, e + U)

                def body(it):
                    for k in range(m.steps):
                        if not isinstance(it, int) or it * m.steps + k < m.total:
                            hidden(it, k)
                        after(it, k)
                m.run(act, body)
                for k in range(2):
                    if m.experts % U == 0:
                        after(m.bodies, k)

            act.wait_ge(in_small, SMALL)
            act.activation(tg[:, :], tg[:, :], ACT.Tanh).then_inc(tg_ready, 1)
            act.wait_ge(in_ctx, 16)
            act.activation(diag[:, :], ctxT[:, :], ACT.Square).then_inc(pre["kv"], 1)
            norm(0)
            prepare()
            first_weights(MOES[0])
            norm(1)
            moe(MOES[0])
            first_weights(MOES[1])
            norm(2)
            attention(0)
            norm(3)
            moe(MOES[1])
            first_weights(MOES[2])
            norm(4)
            pair_sums()
            norm(5)
            moe(MOES[2])
            first_weights(MOES[3])
            norm(6)
            attention(1)
            norm(7)
            moe(MOES[3])

        @block.vector
        def _(dve):
            link = linker(dve, dve_link)

            def norm(j):
                for t in range(2):
                    dve.wait_ge(ln["mean"], 2 * j + t + 1)
                    dve.tensor_tensor(xc[:, half(t)], x[:, half(t)], ps[:, t], ALU.subtract).then_inc(ln["xc"], 1)
                for t in range(2):
                    dve.wait_ge(ln["var"], 2 * j + t + 1)
                    dve.tensor_scalar(var_eps[:, t * HT:(t + 1) * HT], ps[:, 2 + t, 0:HT], EPS, None, ALU.add).then_inc(ln["eps"], 1)
                if j == 0:
                    dve.wait_ge(in_small, SMALL)
                for t in range(2):
                    dve.wait_ge(ln["rstd"], 2 * j + t + 1)
                    dve.tensor_tensor(diag[:, half(t)].rearrange("p (c k) -> p c k", k=P), bcast(ident[:, :], 1, HT),
                                      bcast(rstd[:, t * HT:(t + 1) * HT], 2, P), ALU.mult).then_inc(ln["diag"], 1)
                for t in range(2):
                    dve.wait_ge(ln["bc"], 2 * j + t + 1)
                    dve.tensor_tensor(n[:, half(t)], xc[:, half(t)], ps[:, 4 + t], ALU.mult).then_inc(ln["n"], 1)
                if j % 2:
                    i = j // 2
                    for t in range(2):
                        dve.wait_ge(ln["n"], 2 * j + t + 1)
                        dve.tensor_copy(n_hi[:, half(t)], n[:, half(t)]).then_inc(ln["hi"], 1)
                        dve.wait_ge(ln["hi"], 2 * i + t + 1)
                        dve.tensor_tensor(n_lo[:, half(t)], n[:, half(t)], n_hi[:, half(t)].bitcast(F32), ALU.subtract).then_inc(ln["lo"], 1)

            def rotate(dst, t, banks, tab, bias):
                v = dst[:, half(t)].rearrange("p (b s) -> p b s", s=S)
                tmp = h_act[:, t, 0:HALF].rearrange("p (b s) -> p b s", s=S)
                b0 = abias[:, bias:bias + 1] if bias is not None else 0.0
                b1 = abias[:, bias + 1:bias + 2] if bias is not None else 0.0
                dve.scalar_tensor_tensor(v, ps[:, banks].rearrange("p (b s) -> p b s", s=S), b0, bcast(rope[:, tab], 1, 8), ALU.add, ALU.mult)
                link(dve.scalar_tensor_tensor(tmp, ps[:, banks + 1].rearrange("p (b s) -> p b s", s=S), b1, bcast(rope[:, tab + 1], 1, 8), ALU.add, ALU.mult))
                return dve.tensor_tensor(v, v, tmp, ALU.add)

            def prepare():
                for i in range(2):
                    for t in range(2):
                        dve.wait_ge(pre["proj"], 2 * i + t + 1)
                        rotate(kT[i], t, 2 * t, 2, 2 if i == 0 else None).then_inc(pre["k"], 1)
                for i in range(2):
                    for q in range(4):
                        r = 4 * i + q
                        dve.wait_ge(pre["v"], r + 1)
                        for h2 in range(2):
                            rows = slice(64 * h2, 64 * h2 + 64)
                            src = ps[rows, 4 + r % 2].rearrange("p (b h c d) -> p (b h) c d", b=4, h=8, c=2)[:, :, h2]
                            dst = vblk[i][rows, 4 * q:4 * q + 4].rearrange("p b h (c d) -> p (b h) c d", c=2)[:, :, h2, 0:8]
                            ins = dve.tensor_copy(dst, src)
                        ins.then_inc(pre["vcp"], 1)

            def attention(i):
                base = PAIRS * i
                for t in range(2):
                    dve.wait_ge(at["q"], 2 * i + t + 1)
                    rotate(qT, t, 2 * t, 0, 0 if i == 0 else None).then_inc(at["qT"], 1)

                def soft(p):
                    g = base + p
                    dve.wait_ge(at["sc"], g + 1)
                    sc = ps[:, 2 * (p % 2):2 * (p % 2) + 2].rearrange("p a (h k) -> p (a h) k", k=S)
                    dve.tensor_reduce(mx[:, p % 2], sc, AX, ALU.max).then_inc(at["max"], 1)
                    dve.wait_ge(at["max"], g + 1)
                    if g >= 2:
                        dve.wait_ge(at["exp"], g - 1)
                    dve.tensor_tensor(s_sub[:, p % 2].rearrange("p (h k) -> p h k", k=S), sc, bcast(mx[:, p % 2], 2, S),
                                      ALU.subtract).then_inc(at["sub"], 1)

                def output(p):
                    g = base + p
                    dve.wait_ge(at["pv"], g + 1)
                    o = ps[:, 6, 0:144].rearrange("p (h c) -> p h c", c=9)
                    link(dve.reciprocal(rsum[:, p % 2], o[:, :, 8]))
                    if g >= 2:
                        dve.wait_ge(at["aot"], g - 1)
                    dve.tensor_tensor(ao[:, p % 2].rearrange("p (h d) -> p h d", d=HD), o[:, :, 0:HD], bcast(rsum[:, p % 2], 2, HD),
                                      ALU.mult).then_inc(at["ao"], 1)

                def update(t):
                    dve.wait_ge(at["proj"], 2 * i + t + 1)
                    bo = abias[:, 5:6] if i == 0 else 0.0
                    dve.scalar_tensor_tensor(x[:, half(t)], ps[:, 7], bo, x[:, half(t)], ALU.add, ALU.add).then_inc(x_done[t], 1)

                soft(0)
                for p in range(PAIRS):
                    if p + 1 < PAIRS:
                        soft(p + 1)
                    if p == HT + 1:
                        update(0)
                    output(p)
                update(1)

            def pair_sums():
                for t in range(2):
                    dve.wait_ge(x2["feat"], t + 1)
                    dve.tensor_scalar(xc[:, half(t)], ps[:, t], l2b[:, 0:1], None, ALU.add).then_inc(x2["fb"], 1)
                dve.wait_ge(x2["fb"], 2)
                for g in range(2 * B):
                    if g % 3 == 2:
                        continue
                    if g >= 3:
                        dve.wait_ge(x2["tanh"], g - 2)
                    dve.tensor_tensor(*sum_of(g), ALU.add).then_inc(x2["sumA"], 1)
                dve.wait_ge(x2["dot"], 2 * B)
                r3 = h_act[:, 1, 0:512].rearrange("p (f s) -> p f s", s=S)
                e3 = h_act[:, 0, 0:512].rearrange("p (f s) -> p f s", s=S)
                t3 = h_act[:, 1, 512:1024].rearrange("p (f s) -> p f s", s=S)
                link(dve.tensor_tensor(r3, ps[:, 6].rearrange("p (f s) -> p f s", s=S), bcast(mbias[:, 1], 1, 8), ALU.add))
                link(dve.tensor_reduce(st2[:, 0], r3, AX, ALU.max))
                dve.tensor_tensor(r3, r3, bcast(st2[:, 0], 2, S), ALU.subtract).then_inc(x2["soft"], 1)
                dve.wait_ge(x2["exp"], 1)
                link(dve.tensor_reduce(st2[:, 0], e3, AX, ALU.add))
                link(dve.reciprocal(st2[:, 1], st2[:, 0]))
                for r in range(2):
                    link(dve.tensor_tensor(t3, e3, bcast(uv[:, r], 1, 8), ALU.mult))
                    link(dve.tensor_reduce(st2[:, 2 + r], t3, AX, ALU.add))
                for r in range(2):
                    ins = dve.tensor_tensor(st2[:, 2 + r], st2[:, 2 + r], st2[:, 1], ALU.mult)
                ins.then_inc(x2["wb"], 1)
                dve.wait_ge(x2["tw"], 2)
                for r in range(2):
                    link(dve.tensor_scalar(st2[:, 2 + r], st2[:, 4 + r], tg[:, 2:3], None, ALU.mult))
                    dve.tensor_tensor((diag, sq)[r][:, :].rearrange("p (c f) -> p c f", f=8), bcast(perm[:, :], 2, 8),
                                      bcast(st2[:, 2 + r], 1, P), ALU.mult).then_inc(x2["d"], 1)
                for t in range(2):
                    dve.wait_ge(x2["bc"], t + 1)
                    dve.tensor_tensor(xc[:, half(t)], n[:, half(t)], ps[:, t], ALU.mult).then_inc(x2["mb"], 1)
                for t in range(2):
                    dve.wait_ge(x2["bc"], t + 3)
                    dve.wait_ge(x2["mb"], t + 1)
                    link(dve.tensor_tensor(xc[:, half(t)], xc[:, half(t)], ps[:, 2 + t], ALU.add))
                    dve.tensor_tensor(x[:, half(t)], x[:, half(t)], xc[:, half(t)], ALU.add).then_inc(x_done[t], 1)

            def top(cur, count, width, big, chosen):
                m0, m1 = rt_m[:, 0, 0:TILES], rt_m[:, 1, 0:TILES]
                eq, c = rt["a"][:, :, 0:width], rt["c"][:, :, 0:width]
                for r in range(count):
                    link(dve.tensor_reduce(m0, cur, AX, ALU.max))
                    link(dve.tensor_tensor(eq, cur, bcast(m0, 2, width), ALU.is_equal))
                    link(dve.tensor_tensor(eq, eq, bcast(revi[width][:, :], 1, TILES), ALU.mult))
                    link(dve.tensor_reduce(m1, eq, AX, ALU.max))
                    link(dve.tensor_tensor(c, eq, bcast(m1, 2, width), ALU.is_equal))
                    link(dve.scalar_tensor_tensor(cur, c, -big, cur, ALU.mult, ALU.add))
                link(dve.tensor_scalar(chosen, cur, -big / 2, None, ALU.is_lt))

            def route(m):
                s, L, E = mo[m.layer], m.layer, m.routed
                e, cur, w, chosen = (rt[k][:, :, 0:E] for k in ("e", "cur", "w", "s"))
                if L == 2:
                    dve.wait_ge(once["e"], m.layer + 1)
                    e4 = e.rearrange("p c (g k) -> p c g k", g=4)
                    cur4 = cur.rearrange("p c (g k) -> p c g k", g=4)
                    gm, gs = rt["lg"][:, :, 0:4], rt["sg"][:, :, 0:4]
                    link(dve.tensor_reduce(gm, e4, AX, ALU.max))
                    top(gm, 2, 4, 8.0, gs)
                    link(dve.tensor_tensor(cur4, e4, bcast(gs, 3, 4), ALU.mult))
                    link(dve.tensor_scalar(gs, gs, 1.0, None, ALU.subtract))
                    link(dve.tensor_tensor(cur4, cur4, bcast(gs, 3, 4), ALU.add))
                    top(cur, 4, 16, 8.0, chosen)
                else:
                    top(cur, m.topk, E, 1e30, chosen)
                    dve.wait_ge(once["e"], m.layer + 1)
                total, inv = rt_m[:, 0, 0:TILES], rt_m[:, 1, 0:TILES]
                link(dve.tensor_tensor(w, e, chosen, ALU.mult))
                link(dve.tensor_reduce(total, e if L == 3 else w, AX, ALU.add))
                link(dve.reciprocal(inv, total))
                link(dve.tensor_scalar(inv, inv, tg[:, 4 + L:5 + L], 2.5 if L == 2 else 1.0, ALU.mult, ALU.mult))
                dve.tensor_tensor(w, w, bcast(inv, 2, E), ALU.mult).then_inc(once["w"], 1)

            def moe(m):
                s, L = mo[m.layer], m.layer
                N, U, E = m.n, m.unroll, m.routed
                lg = ps[:, 6, 0:TILES * E].rearrange("p (c e) -> p c e", e=E)
                cur = rt["cur"][:, :, 0:E]
                if L == 0:
                    dve.wait_ge(once["logit"], m.layer + 1)
                    link(dve.tensor_tensor(rt["lg"][:, :, 0:E], lg, bcast(gb0[:, :], 1, TILES), ALU.add))
                    lg = rt["lg"][:, :, 0:E]
                if L != 2:
                    dve.wait_ge(once["logit"], m.layer + 1)
                    link(dve.tensor_reduce(rt_m[:, 3, 0:TILES], lg, AX, ALU.max))
                    dve.tensor_tensor(rt["sg"][:, :, 0:E], lg, bcast(rt_m[:, 3, 0:TILES], 2, E), ALU.subtract).then_inc(once["cur"], 1)
                    dve.wait_ge(once["cur"], (1, 2, 0, 3)[m.layer])
                    link(dve.tensor_copy(cur, rt["sg"][:, :, 0:E]))
                route(m)
                if L == 3:
                    dve.scalar_tensor_tensor(x[:, :], n[:, :], tg[:, 7:8], x[:, :], ALU.mult, ALU.add).then_inc(s["xn"], 1)

                def split(it, k):
                    step, sl = it * m.steps + k, k % 2
                    dve.wait_ge(s["act"], step + 1)
                    if m.gated:
                        size = m.chunks[(k % N) // 2][1]
                        ha = h_act[0:size, sl, 0:HALF]
                        b3 = w_bias[:, k // N, 1:2] if L == 2 else 0.0
                        dve.scalar_tensor_tensor(ha, ps[0:size, 2 * sl + 1], b3, ha, ALU.add, ALU.mult).then_inc(s["mul"], 1)
                        dve.wait_ge(s["mul"], step + 1)
                        hi, lo = h_hi[0:size, sl, 0:HALF], h_lo[0:size, sl, 0:HALF]
                    else:
                        ha, hi, lo = h_act[:, sl], h_hi[:, sl], h_lo[:, sl]
                    if not (isinstance(it, int) and step < 2):
                        dve.wait_ge(s["h_used"], step - 1)
                    dve.tensor_copy(hi, ha).then_inc(s["hi"], 1)
                    dve.wait_ge(s["hi"], step + 1)
                    dve.tensor_tensor(lo, ha, hi.bitcast(F32), ALU.subtract).then_inc(s["h_ready"], 1)

                def gate(it, k):
                    e = it * U + k
                    yy, dst = ps[:, 4:6].rearrange("p a c -> p (a c)"), y_g[:, k % 2]
                    dve.wait_ge(s["h_used"], N * (e + 1))
                    if not (isinstance(it, int) and e < 2):
                        dve.wait_ge(s["acc"], e - 1)
                    if isinstance(it, int) and e >= E:
                        dve.tensor_scalar(dst, yy, tg[:, 4 + L:5 + L], None, ALU.mult).then_inc(s["gate"], 1)
                        return
                    dve.wait_ge(s["gcp"], e + 1)
                    if m.biases:
                        dve.scalar_tensor_tensor(dst, yy, w_bias[:, k % U, m.biases - 1:m.biases], g_sb[:, k % 2], ALU.add, ALU.mult).then_inc(s["gate"], 1)
                    else:
                        dve.tensor_tensor(dst, yy, g_sb[:, k % 2], ALU.mult).then_inc(s["gate"], 1)

                def body(it):
                    for k in range(m.steps):
                        if isinstance(it, int) and it * m.steps + k >= m.total:
                            break
                        split(it, k)
                        if (k - 1) % N == N - 1 and not (isinstance(it, int) and it * m.steps + k < N):
                            gate(it, (k - 1) // N)
                m.run(dve, body)
                gate(m.bodies - 1, (m.experts - 1) % U)

            dve.memset(mean_w[:, :], 1.0 / P)
            dve.memset(ones_w[:, :], 1.0)
            dve.memset(minus_half[:, :], -0.5)
            dve.memset(gT[:, :], 0.0).then_inc(consts, 1)
            for i in range(2):
                vz = vblk[i][:].rearrange("p b h c -> p (b h c)")
                link(dve.memset(vz, 0.0))
                for h2 in range(2):
                    rows = slice(64 * h2, 64 * h2 + 64)
                    ones = vblk[i][rows].rearrange("p b h (c d) -> p (b h) c d", c=2)[:, :, h2, 8]
                    dve.memset(ones, 1.0)
            link(dve.memset(h_act[:, 0], DECAY))
            link(dve.memset(h_act[:, 0].rearrange("p (b s) -> p b s", s=S)[:, :, 0], 0.0))
            dve.wait_ge(pre["kv"], 1)
            dve.tensor_tensor_scan(h_act[:, 1], h_act[:, 0], diag[:, :], 0.0, ALU.mult, ALU.add).then_inc(pre["scan"], 1)
            norm(0)
            dve.wait_ge(pre["scan"], 1)
            dve.wait_ge(tg_ready, 1)
            for t in range(2):
                dve.wait_ge(ln["n"], t + 1)
                link(dve.scalar_tensor_tensor(n[:, half(t)], n[:, half(t)], tg[:, 0:1], h_act[:, 1, half(t)], ALU.mult, ALU.mult))
                dve.tensor_tensor(x[:, half(t)], x[:, half(t)], n[:, half(t)], ALU.add).then_inc(x_done[t], 1)
            dve.tensor_scalar(wqk[:, 5], wqk[:, 5], tg[:, 1:2], None, ALU.mult).then_inc(pre["wo"], 1)
            dve.tensor_scalar(wqk[:, 11], wqk[:, 11], tg[:, 3:4], None, ALU.mult).then_inc(pre["wo"], 1)
            dve.wait_ge(pre["wo"], 2)
            prepare()
            link(dve.tensor_scalar(mbias[:, 0], qmask[:, :], -1.0, 1.0, ALU.mult, ALU.add))
            link(dve.tensor_scalar(mbias[:, 1], mbias[:, 0], NEG, None, ALU.mult))
            link(dve.tensor_scalar(abias[:, 5:6], abias[:, 4:5], tg[:, 1:2], None, ALU.mult))
            norm(1)
            moe(MOES[0])
            norm(2)
            attention(0)
            norm(3)
            moe(MOES[1])
            norm(4)
            pair_sums()
            norm(5)
            moe(MOES[2])
            norm(6)
            attention(1)
            norm(7)
            moe(MOES[3])

        @block.gpsimd
        def _(pool):
            link = linker(pool, pool_link)

            def norm(j):
                for t in range(2):
                    r = slice(t * HT, (t + 1) * HT)
                    pool.wait_ge(ln["eps"], 2 * j + t + 1)
                    pool.tensor_tensor(rstd[:, r], var_eps[:, r], minus_half[:, r], ALU.pow).then_inc(ln["rstd"], 1)

            def split_lo(m, it, k):
                s, U = mo[m.layer], m.unroll
                u, e = k % U, it * U + k
                o = u * m.width
                for hi, lo, c0, c1 in (("whu", "wlu", 0, m.up), ("whd", "wld", m.up, m.split)):
                    pool.wait_ge(s[hi], e + 1)
                    pool.tensor_tensor(w_lo[:, o + c0:o + c1], w_f32[:, o + c0:o + c1], w_hi[:, o + c0:o + c1].bitcast(F32),
                                       ALU.subtract).then_inc(s[lo], 1)

            def first_weights(m):
                for u in range(m.unroll):
                    split_lo(m, 0, u)

            def expand_keys(i, p):
                g = PAIRS * i + p
                if p >= 4:
                    pool.wait_ge(at["sc"], g - 3)
                src = kT[i][:, p * P:(p + 1) * P].rearrange("p (b k) -> p b k", b=2)
                for b in range(2):
                    ins = pool.tensor_tensor(kexp[:, p % 4, b], bcast(src[:, b], 1, HEADS), bcast(hmask[:, :], 2, S), ALU.mult)
                ins.then_inc(at["kexp"], 1)

            def pair_sums():
                pool.wait_ge(x2["fb"], 2)
                for g in range(2, 2 * B, 3):
                    if g >= 3:
                        pool.wait_ge(x2["tanh"], g - 2)
                    pool.tensor_tensor(*sum_of(g), ALU.add).then_inc(x2["sumB"], 1)

            def gate_parts(m):
                s, E = mo[m.layer], m.routed
                w = rt["w"][:, :, 0:E]
                part = [gsp[:, :, r * E:(r + 1) * E] for r in range(3)]
                pool.wait_ge(once["w"], m.layer + 1)
                link(pool.tensor_copy(part[0], w))
                link(pool.tensor_tensor(w, w, part[0], ALU.subtract))
                link(pool.tensor_copy(part[1], w))
                link(pool.tensor_tensor(w, w, part[1], ALU.subtract))
                pool.tensor_copy(part[2], w).then_inc(once["gsp"], 1)

            def moe(m):
                s, U = mo[m.layer], m.unroll
                gate_parts(m)
                if m.layer == 3:
                    pool.wait_ge(s["xn"], 1)

                def accumulate(it, k):
                    e = it * U + k
                    pool.wait_ge(s["gate"], e + 1)
                    if not (isinstance(it, int) and e == 0):
                        pool.wait_ge(s["acc"], e)
                    if isinstance(it, int) and e == m.experts - 1:
                        for t in range(2):
                            pool.tensor_tensor(x[:, half(t)], x[:, half(t)], y_g[:, k % 2, half(t)], ALU.add).then_inc(x_done[t], 1)
                    else:
                        pool.tensor_tensor(x[:, :], x[:, :], y_g[:, k % 2], ALU.add).then_inc(s["acc"], 1)

                def body(it):
                    for k in range(U):
                        if isinstance(it, int) and it * U + k >= m.experts:
                            break
                        accumulate(it, k)
                        if not isinstance(it, int) or it * U + k + U < m.experts:
                            split_lo(m, it, k + U)
                m.run(pool, body)

            pool.wait_ge(consts, 1)
            norm(0)
            first_weights(MOES[0])
            norm(1)
            pool.wait_ge(pre["k"], 4)
            moe(MOES[0])
            for p in range(4):
                expand_keys(0, p)
            first_weights(MOES[1])
            norm(2)
            for p in range(4, PAIRS):
                expand_keys(0, p)
            norm(3)
            moe(MOES[1])
            first_weights(MOES[2])
            norm(4)
            pair_sums()
            norm(5)
            moe(MOES[2])
            for p in range(4):
                expand_keys(1, p)
            first_weights(MOES[3])
            norm(6)
            for p in range(4, PAIRS):
                expand_keys(1, p)
            norm(7)
            moe(MOES[3])


def constants():
    c = {}
    c["c_ident"] = np.eye(P, dtype=np.float32)
    sel_rows = {}
    for e in (8, 16):
        s = np.zeros((P, e, P), np.float32)
        for r in range(3 * e):
            s[r, r % e] = 1.0
        sel_rows[e] = s
        c[f"c_revi{e}"] = np.tile(np.arange(e, 0, -1, dtype=np.float32), (P, 1))
    c["c_revi4"] = np.tile(np.arange(4, 0, -1, dtype=np.float32), (P, 1))
    one16 = np.uint16(0x3F80)
    c["c_ident16"] = np.eye(P, dtype=np.uint16) * one16
    c["c_sel8"], c["c_sel16"] = (sel_rows[e].astype(np.uint16) * one16 for e in (8, 16))
    pair = (np.arange(P) % HD) // 2
    freq = (1.0 / 10000.0 ** (np.arange(0, HD, 2, dtype=np.float64) / HD)).astype(np.float32)[pair]
    ang = (np.arange(S, dtype=np.float32)[None, :] * freq[:, None]).astype(np.float32).astype(np.float64)
    sign = np.where(np.arange(P) % 2 == 0, -1.0, 1.0)[:, None]
    cos, sin = np.cos(ang), np.sin(ang) * sign
    scale = 1.0 / np.sqrt(HD)
    c["c_rope"] = np.stack([cos * scale, sin * scale, cos, sin], axis=1).astype(np.float32)
    c["c_hmask"] = (np.arange(P)[:, None] // HD == np.arange(HEADS)[None, :]).astype(np.float32)
    perm = np.zeros((P, P), np.float32)
    for b in range(B):
        for h in range(2):
            for q in range(4):
                perm[32 * q + 2 * b + h, 8 * b + 4 * h + q] = 1.0
    c["c_perm"] = perm
    return c


def kernel(**inputs):
    import concourse.bacc as bacc
    from concourse.bass_utils import run_bass_kernel_spmd

    i = {k: np.asarray(v) for k, v in inputs.items()}
    f = np.ascontiguousarray
    arr = constants()
    arr["xT"] = f(i["x"].reshape(T, P).T)
    arr["ctxT"] = f(i["ctx_1024"].reshape(T, P).T)
    arr["g_rows"] = f(np.tile(np.concatenate([i["g_xattn"], i["g_ffn"]])[None, :], (P, 1)))

    def chunked(w):
        e, h, d = w.shape
        c = -(-h // P)
        w = np.concatenate([w, np.zeros((e, c * P - h, d), w.dtype)], axis=1)
        return w.reshape(e, c, P, d).transpose(0, 2, 1, 3).reshape(e, P, c * d)

    def tr(w):
        return w.transpose(0, 2, 1)

    def col(v):
        return v.reshape(v.shape[0], -1, P).transpose(0, 2, 1)

    arr["w0"] = f(np.concatenate([i["L0_ffn_w1"], chunked(i["L0_ffn_w2"]), col(i["L0_ffn_b1"]), col(i["L0_ffn_b2"])], axis=2))
    arr["w1"] = f(np.concatenate([tr(i["L1_ffn_W1"]), tr(i["L1_ffn_W3"]), chunked(tr(i["L1_ffn_W2"]))], axis=2))
    arr["w2"] = f(np.concatenate([tr(i["L2_ffn_W1"]), tr(i["L2_ffn_W3"]), chunked(tr(i["L2_ffn_W2"])),
                                 col(i["L2_ffn_b1"]), col(i["L2_ffn_b3"]), col(i["L2_ffn_b2"])], axis=2))
    up3 = np.concatenate([i["L3_ffn_routed_up"], i["L3_ffn_shared_up"]], axis=0)
    dn3 = np.concatenate([i["L3_ffn_routed_down"], i["L3_ffn_shared_down"]], axis=0)
    arr["w3"] = f(np.concatenate([up3, chunked(dn3)], axis=2))
    arr["wg0"], arr["wg1"], arr["wg2"] = f(i["L0_ffn_gate_w"].T), f(i["L1_ffn_Wg"].T), f(i["L2_ffn_Wg"].T)
    arr["wg3"] = f(i["L3_ffn_router_w"])
    arr["gb0"] = f(np.tile(i["L0_ffn_gate_b"][None, :], (P, 1)))

    swap = np.arange(P) ^ 1

    def six(wq, wk, wv, wo):
        return [wq.T, wq[swap].T, wk.T, wk[swap].T, wv.T, wo.T]
    arr["w_attn"] = f(np.stack(six(*(i[f"L1_xattn_{k}"] for k in ("wq", "wk", "wv", "wo")))
                               + six(*(i[f"L3_xattn_W_{k}"] for k in "qkvo")), axis=1))
    bq, bk = i["L1_xattn_bq"], i["L1_xattn_bk"]
    arr["b_attn"] = f(np.stack([bq, bq[swap], bk, bk[swap], i["L1_xattn_bo"], i["L1_xattn_bo"], i["L1_xattn_bv"]], axis=1))
    arr["w_l2"] = f(np.stack([i["L2_xattn_Ws"], i["L2_xattn_W"]], axis=1))
    pad = np.zeros((P, 63), np.float32)
    pad[:, 31] = i["L2_xattn_w"][:, 0]
    arr["w_l2pad"] = pad
    uvp = np.zeros((P, 2, 62), np.float32)
    for r, k in enumerate(("L2_xattn_Wcw", "L2_xattn_Wcb")):
        uvp[:, r, 30:32] = i[k][0][:, None]
    arr["w_l2uv"] = uvp
    one = lambda v: np.broadcast_to(v.reshape(1), (P,))
    arr["b_l2"] = f(np.stack([i["L2_xattn_b"][0], one(i["L2_xattn_bcw"]), one(i["L2_xattn_bcb"])], axis=1))
    mask = i["mask_BxS2_ik0"].astype(np.int32)
    arr["mask_rows"] = f(np.tile(np.repeat(mask, 2, axis=0), (4, 1)))

    nc = bacc.Bacc("TRN2", target_bir_lowering=False, num_devices=1)
    aps = {k: nc.dram_tensor(f"in_{k}", v.shape, mybir.dt.from_np(v.dtype), kind="ExternalInput").ap() for k, v in arr.items()}
    out = nc.dram_tensor("out_xT", (P, T), F32, kind="ExternalOutput").ap()
    flamingo(nc, aps, out)
    r = run_bass_kernel_spmd(nc, [{f"in_{k}": v for k, v in arr.items()}], core_ids=[0])
    return f(r.results[0]["out_xT"].T).reshape(B, S, P)
```

```python
from contextlib import ExitStack

import numpy as np

import concourse.bass as bass
from concourse import mybir

F32 = mybir.dt.float32
F32R = mybir.dt.float32r
BF16 = mybir.dt.bfloat16
I32 = mybir.dt.int32
ACT = mybir.ActivationFunctionType
ALU = mybir.AluOpType
AX = mybir.AxisListType.X

P = 128
B, S = 16, 64
T = B * S
TILES = T // P
HALF = T // 2
HT = TILES // 2
HEADS, HD = 16, 8
PAIRS = B // 2
EPS = 1e-5
DECAY = 0.9
NEG = -1e30


class Moe:

    def __init__(self, layer, experts, hidden, gated, unroll, topk, routed=None, biases=0):
        self.biases = biases
        self.layer, self.experts, self.gated, self.unroll, self.topk = layer, experts, gated, unroll, topk
        self.routed = routed or experts
        self.chunks = [(f, min(P, hidden - f)) for f in range(0, hidden, P)]
        self.n = len(self.chunks) * (2 if gated else 1)
        self.steps = self.n * unroll
        self.up = hidden * (2 if gated else 1)
        self.split = self.up + P * len(self.chunks)
        self.width = self.split + biases
        self.hidden = hidden
        self.total = self.n * experts
        self.down_total = self.total + (not gated)
        self.bodies = -(-experts // unroll)
        self.loop_end = (experts - 2 * unroll) // unroll + 1

    def run(self, eng, body):
        body(0)
        if self.loop_end > 1:
            with eng.Fori(1, self.loop_end) as it:
                body(it)
        for it in range(max(self.loop_end, 1), self.bodies):
            body(it)


MOES = [
    Moe(0, 8, 512, False, 2, 2, biases=5),
    Moe(1, 8, 352, True, 2, 2),
    Moe(2, 16, 128, True, 4, 4, biases=3),
    Moe(3, 9, 512, False, 2, 2, routed=8),
]


PACKS = {
    "p_first": {"gates": (8,), "ident": (P,), "cen": (P,)},
    "p_attn1": {"rope": (4, S), "hmask": (4,), "rmask": (4,), "abias": (7,), "attn1": (6, P), "wg0": (8,), "gb0": (8,)},
    "p_rest": {"attn3": (6, P), "wg1": (8,), "wg2": (16,), "wg3": (8,), "l2w": (2, P), "l2pad": (63,), "l2uv": (2, 158), "l2b": (3,),
               "perm": (P,)},
    "p_bf16": {"ident16": (P,), "sel8": (8, P), "sel16": (16, P)},
}


def bcast(ap, dim, count):
    shape = list(ap.shape)
    return ap.unsqueeze(dim).broadcast_to(shape[:dim] + [count] + shape[dim:])


def flamingo(nc, a, out):
    ctx = ExitStack()
    with ctx:
        def sb(name, shape, dt=F32):
            return ctx.enter_context(nc.sbuf_tensor(name, shape, dt))

        def sem(name):
            return ctx.enter_context(nc.semaphore(name))

        x = sb("x", [P, T])
        n = sb("n", [P, T])
        n_hi = sb("n_hi", [P, T], F32R)
        n_lo = sb("n_lo", [P, T], F32R)
        xc = sb("xc", [P, T])
        sq = sb("sq", [P, T])
        diag = sb("diag", [P, T])
        ctxT = sb("ctxT", [P, T])
        kT = [sb("kT1", [P, T]), sb("kT3", [P, T])]
        vblk = [sb("vblk1", [P, B, 8, 18]), sb("vblk3", [P, B, 8, 18])]
        txt = sb("txt", [P, T])
        uv = sb("uv", [P, 2, S])
        work = sb("work", [P, 12 * T])
        wslot = max(m.width * m.unroll for m in MOES)
        w_f32 = sb("w_f32", [P, wslot])
        w_hi = sb("w_hi", [P, wslot], F32R)
        w_lo = sb("w_lo", [P, wslot], F32R)
        w_bias = sb("w_bias", [P, 4, 5])
        h_act = sb("h_act", [P, 2, T])
        h_hi = sb("h_hi", [P, 2, T], F32R)
        h_lo = sb("h_lo", [P, 2, T], F32R)
        g_sb = sb("g_sb", [P, 2, T])
        y_g = sb("y_g", [P, 2, T])

        packed = {}
        for name, fields in PACKS.items():
            total = sum(int(np.prod(shape)) for shape in fields.values())
            tile = sb(name, [P, total], BF16 if name == "p_bf16" else F32)
            at_col = 0
            for field, shape in fields.items():
                size = int(np.prod(shape))
                view = tile[:, at_col:at_col + size]
                packed[field] = view.rearrange("p (a b) -> p a b", a=shape[0]) if len(shape) == 2 else view
                at_col += size
            packed[name] = tile
        ident, cen_w, tg = packed["ident"], packed["cen"], packed["gates"]
        rope, hmask, rmask, perm = packed["rope"], packed["hmask"], packed["rmask"], packed["perm"]
        wqk1, wqk3, abias, l2w = packed["attn1"], packed["attn3"], packed["abias"], packed["l2w"]
        l2pad, l2uvpad, l2b = packed["l2pad"], packed["l2uv"], packed["l2b"]
        ident16, sel = packed["ident16"], {8: packed["sel8"], 16: packed["sel16"]}
        wg, gb0 = [packed[f"wg{m.layer}"] for m in MOES], packed["gb0"]
        var_w = sb("var_w", [P, 1])
        ones_w = sb("ones_w", [P, P])
        ones_row = sb("ones_row", [P, 16])
        minus_half = sb("minus_half", [P, TILES])
        qmask = sb("qmask", [P, S], I32)
        mbias = sb("mbias", [P, 2, S])
        var_eps = sb("var_eps", [P, TILES])
        rstd = sb("rstd", [P, TILES])
        rt = {k: sb(f"rt_{k}", [P, TILES, 16]) for k in ("lg", "cur", "e", "top8", "above", "equal", "rank", "chosen", "w")}
        groups = sb("groups", [P, 2, TILES, 8])
        rt_m = sb("rt_m", [P, 4, 4 * TILES])
        gsp = sb("gsp", [P, TILES, 3 * 16], BF16)
        gT = sb("gT", [P, T], BF16)
        mx = sb("mx", [P, 2, HEADS])
        rsum = sb("rsum", [P, 2, HEADS])
        ao = sb("ao", [P, 2, P])
        st2 = sb("st2", [P, 6, 8])

        ps = ctx.enter_context(nc.psum_tensor("ps", [P, 8, 512], F32))

        kexp = work[:, 0:4 * T].rearrange("p (b h k) -> p b h k", b=B, h=4)
        q_rows = work[:, 4 * T:8 * T].rearrange("p (r t) -> p r t", r=4)
        s_sub = work[:, 8 * T:10 * T].rearrange("p (r c) -> p r c", r=2)
        p_exp, p_tr = y_g, g_sb
        qT, aoT = xc, sq
        SCB = (2, 0)
        KBANK = ((6, 4), (0, 2))
        VBANK = (6, 0)
        sums = work[:, 0:6 * T].rearrange("p (r c) -> p r c", r=3)
        tanhs = work[:, 6 * T:12 * T].rearrange("p (r c) -> p r c", r=3)

        in_x, in_ctx = sem("in_x"), sem("in_ctx")
        in_pack = {name: sem(f"in_{name}") for name in (*PACKS, "mask")}
        consts = sem("consts")
        tg_ready, zeros = sem("tg_ready"), sem("zeros")
        dve_link, pool_link, act_link = sem("dve_link"), sem("pool_link"), sem("act_link")
        x_done = [sem("x_done0"), sem("x_done1")]
        ln = {k: sem(f"ln_{k}") for k in ("mean", "xc", "sq", "var", "eps", "rstd", "diag", "bc", "n", "hi", "lo")}
        pre = {k: sem(f"pre_{k}") for k in ("kv", "scan", "proj", "k", "v", "vcp", "txt", "txtcp", "uv", "uvcp", "wo")}
        at = {k: sem(f"at_{k}") for k in ("q", "qT", "q_rows", "kexp", "sc", "max", "sub", "exp", "tr", "trcp", "pv", "ao", "aot", "aocp", "proj")}
        x2 = {k: sem(f"x2_{k}") for k in ("feat", "fb", "sumA", "sumB", "tanh", "dot", "soft", "exp", "wb", "tw", "d", "bc", "mb")}
        once = {k: sem(f"rt_{k}") for k in ("logit", "cur", "e", "w", "gsp", "gtr", "gT")}
        mo = [{k: sem(f"m{m.layer}_{k}") for k in ["g_full", "gcp", "hid", "act", "hi", "h_ready", "h_used", "gate", "acc", "whu", "whd", "wlu", "wld"]
              + ["mul"] * m.gated + ["xn"] * (m.layer == 3)} for m in MOES]
        w_in = [[sem(f"w{m.layer}_in{u}") for u in range(m.unroll)] for m in MOES]
        s_out = sem("s_out")

        def linker(eng, s):
            count = [0]

            def link(ins):
                count[0] += 1
                ins.then_inc(s, 1)
                eng.wait_ge(s, count[0])
            return link

        def half(t):
            return slice(t * HALF, (t + 1) * HALF)

        def sum_of(g):
            b, f = g // 2, (g // 2) * S + 32 * (g % 2)
            return (sums[:, g % 3].rearrange("p (f s) -> p f s", s=S), bcast(xc[:, f:f + 32], 2, S), bcast(txt[:, b * S:(b + 1) * S], 1, 32))

        block = ctx.enter_context(nc.Block())

        @block.sync
        def _(sp):
            sp.dma_start(x[:, :], a["xT"]).then_inc(in_x, 16)
            sp.dma_start(packed["p_first"][:, :], a["p_first"]).then_inc(in_pack["p_first"], 16)
            sp.dma_start(ctxT[:, :], a["ctxT"]).then_inc(in_ctx, 16)
            sp.dma_start(packed["p_attn1"][:, :], a["p_attn1"]).then_inc(in_pack["p_attn1"], 16)

            sp.dma_start(packed["p_rest"][:, :], a["p_rest"]).then_inc(in_pack["p_rest"], 16)

            def load(m, u, e, body):
                dst = w_f32[:, u * m.width:(u + 1) * m.width]
                src = a[f"w{m.layer}"][bass.ds(e, 1)].rearrange("e p w -> (e p) w")
                sp.dma_start(dst, src).then_inc(w_in[m.layer][u], 16)

            for m in MOES:
                if m.layer:
                    sp.wait_ge(mo[m.layer - 1]["wld"], MOES[m.layer - 1].experts)
                for u in range(m.unroll):
                    load(m, u, u, 0)
                if m.layer == 0:
                    sp.dma_start(packed["p_bf16"][:, :].bitcast(mybir.dt.uint16), a["p_bf16"]).then_inc(in_pack["p_bf16"], 16)
                    sp.dma_start(qmask[:, :], a["mask_rows"]).then_inc(in_pack["mask"], 16)

                def body(it):
                    for u in range(m.unroll):
                        if not isinstance(it, int) or (it + 1) * m.unroll + u < m.experts:
                            sp.wait_ge(mo[m.layer]["wld"], it * m.unroll + u + 1)
                            load(m, u, (it + 1) * m.unroll + u, it)
                m.run(sp, body)

            for t in range(2):
                sp.wait_ge(x_done[t], 8)
                sp.dma_start(out[:, half(t)], x[:, half(t)]).then_inc(s_out, 16)
            sp.wait_ge(s_out, 32)

        @block.tensor
        def _(pe):
            def norm(j, between=None):
                for t in range(2):
                    if j:
                        pe.wait_ge(x_done[t], j)
                    pe.matmul(ps[:, t], cen_w, x[:, half(t)], start=True, stop=True).then_inc(ln["mean"], 1)
                for t in range(2):
                    pe.wait_ge(ln["sq"], 2 * j + t + 1)
                    if j == 0 and t == 0:
                        pe.wait_ge(consts, 1)
                    for i in range(HT):
                        c = t * HT + i
                        mm = pe.matmul(ps[:, 2 + t, i:i + 1], sq[:, c * P:(c + 1) * P], var_w[:, :], start=True, stop=True)
                    mm.then_inc(ln["var"], 1)
                if between:
                    between()
                for t in range(2):
                    pe.wait_ge(ln["diag"], 2 * j + t + 1)
                    pe.matmul(ps[:, 4 + t], ones_w[:, :], diag[:, half(t)], start=True, stop=True).then_inc(ln["bc"], 1)
                pe.wait_ge(ln["xc"], 2 * j + 2)

            def prepare_keys(i, t):
                w, bank = (wqk1, wqk3)[i], KBANK[i][t]
                pe.matmul(ps[:, bank], w[:, 2], ctxT[:, half(t)], start=True, stop=True)
                pe.matmul(ps[:, bank + 1], w[:, 3], ctxT[:, half(t)], start=True, stop=True).then_inc(pre["proj"], 1)

            def prepare_values(i, q):
                w, r = (wqk1, wqk3)[i], 4 * i + q
                if q >= 2:
                    pe.wait_ge(pre["vcp"], r - 1)
                for b in range(4 * q, 4 * q + 4):
                    for h2 in range(2):
                        mm = pe.matmul(ps[h2 * S:(h2 + 1) * S, VBANK[i] + q % 2, (b % 4) * P:(b % 4 + 1) * P],
                                       ctxT[:, b * S:(b + 1) * S], w[:, 4], start=True, stop=True)
                mm.then_inc(pre["v"], 1)

            def prepare_text():
                for t in range(2):
                    pe.matmul(ps[:, 6 + t], l2w[:, 0], ctxT[:, half(t)], start=True, stop=True).then_inc(pre["txt"], 1)

            def prepare_weighted(r):
                for b in range(B):
                    mm = pe.matmul(ps[:, 7, r * S:(r + 1) * S], l2uvpad[:, r, 30 - 2 * b:30 - 2 * b + P], ctxT[:, b * S:(b + 1) * S],
                                   start=(b == 0), stop=(b == B - 1))
                mm.then_inc(pre["uv"], 1)

            def attention(i):
                w = (wqk1, wqk3)[i]
                for t in range(2):
                    pe.wait_ge(ln["n"], 2 * (2, 6)[i] + t + 1)
                    if t == 1:
                        pe.wait_ge(ln["n"], 2 * (2, 6)[i] + 2)
                    pe.matmul(ps[:, 4 * t], w[:, 0], n[:, half(t)], start=True, stop=True)
                    pe.matmul(ps[:, 4 * t + 1], w[:, 1], n[:, half(t)], start=True, stop=True).then_inc(at["q"], 1)
                if i == 0:
                    prepare_values(0, 2)
                    prepare_values(0, 3)
                base = PAIRS * i

                def scores(p):
                    g = base + p
                    pe.wait_ge(at["q_rows"], 2 * i + p // HT + 1)
                    if p >= 2:
                        pe.wait_ge(at["sub"], g - 1)
                    pe.wait_ge(at["kexp"], g // 2 + 1)
                    for r in range(4):
                        cols = slice(256 * (r % 2), 256 * (r % 2) + 256)
                        for b in range(2):
                            c = p * P + b * S
                            mm = pe.matmul(ps[b * S:(b + 1) * S, SCB[p % 2] + r // 2, cols], q_rows[:, r, c:c + S],
                                           kexp[:, 2 * p + b], start=True, stop=True)
                    mm.then_inc(at["sc"], 1)

                def turn(p):
                    g = base + p
                    pe.wait_ge(at["exp"], g + 1)
                    if p == 0:
                        pe.wait_ge(at["qT"], 2 * i + 2)
                    for hp in range(8):
                        if hp % 4 == 0 and g:
                            pe.wait_ge(at["trcp"], 2 * g - 1 + hp // 4)
                        mm = pe.transpose(ps[:, 4 + hp // 4, (hp % 4) * P:(hp % 4 + 1) * P],
                                          p_exp[:, p % 2, hp * P:(hp + 1) * P], ident)
                        if hp % 4 == 3:
                            mm.then_inc(at["tr"], 1)

                def values(p):
                    g = base + p
                    if g:
                        pe.wait_ge(at["ao"], g)
                    for hp in range(8):
                        if hp % 4 == 0:
                            pe.wait_ge(at["trcp"], 2 * g + 1 + hp // 4)
                        for b in range(2):
                            mm = pe.matmul(ps[b * S:(b + 1) * S, 6, hp * 18:(hp + 1) * 18],
                                           p_tr[:, p % 2, hp * P + b * S:hp * P + (b + 1) * S],
                                           vblk[i][:, 2 * p + b, hp], start=True, stop=True)
                    mm.then_inc(at["pv"], 1)

                def turn_out(p):
                    g = base + p
                    pe.wait_ge(at["ao"], g + 1)
                    if g:
                        pe.wait_ge(at["aocp"], g)
                    if p == HT:
                        pe.wait_ge(x_done[0], (3, 7)[i])
                    pe.transpose(ps[:, 7, 0:P], ao[:, p % 2], ident).then_inc(at["aot"], 1)

                def project(t):
                    pe.wait_ge(at["aocp"], base + HT * (t + 1))
                    pe.wait_ge(pre["wo"], i + 1)
                    pe.matmul(ps[:, 7], w[:, 5], aoT[:, half(t)], start=True, stop=True).then_inc(at["proj"], 1)

                scores(0)
                for p in range(PAIRS):
                    if p + 1 < PAIRS:
                        scores(p + 1)
                    turn(p)
                    if p:
                        turn_out(p - 1)
                    if p == HT:
                        project(0)
                    values(p)
                turn_out(PAIRS - 1)
                project(1)

            def pair_sums():
                for t in range(2):
                    pe.wait_ge(ln["n"], 2 * 4 + t + 1)
                    pe.matmul(ps[:, t], l2w[:, 1], n[:, half(t)], start=True, stop=True).then_inc(x2["feat"], 1)
                for g in range(2 * B):
                    if g == 4:
                        prepare_keys(1, 0)
                        prepare_keys(1, 1)
                    if g in (8, 11, 14, 17):
                        if g == 8:
                            pe.wait_ge(pre["k"], 4)
                        prepare_values(1, (g - 8) // 3)
                    if g in (20, 24):
                        prepare_weighted((g - 20) // 4)
                    pe.wait_ge(x2["tanh"], g + 1)
                    for q in range(4):
                        mm = pe.matmul(ps[32 * q:32 * q + 32, 6], l2pad[:, 31 - g:63 - g],
                                       tanhs[:, g % 3, q * 512:(q + 1) * 512], start=(g == 0), stop=(g == 2 * B - 1))
                    mm.then_inc(x2["dot"], 1)
                pe.wait_ge(pre["vcp"], 8)
                for r in range(2):
                    pe.wait_ge(x2["d"], r + 1)
                    for t in range(2):
                        pe.matmul(ps[:, 2 * r + t], ones_w[:, :], (diag, sq)[r][:, half(t)], start=True, stop=True).then_inc(x2["bc"], 1)

            def moe(m):
                s, L = mo[m.layer], m.layer
                j, N, U, E = 2 * L + 1, m.n, m.unroll, m.routed

                def wap(w, u, lo, size, rows=P):
                    return w[0:rows, u * m.width + lo:u * m.width + lo + size]

                def products(dst, w, u, lo, size, rows, hi, low, first=True, last=True):
                    passes = [(w_hi, hi), (w_hi, low), (w_lo, hi)]
                    for c, (wt, mv) in enumerate(passes):
                        for i in range(len(dst)):
                            mm = pe.matmul(dst[i], wap(wt, u, lo, size, rows), mv[i],
                                           start=(first and c == 0), stop=(last and c == 2))
                    return mm

                def up(it, k):
                    u, sl, step = (k // N) % U, k % 2, it * m.steps + k
                    if k % N == 0:
                        pe.wait_ge(s["wlu"], it * U + k // N + 1)
                    if not (isinstance(it, int) and step < 2):
                        pe.wait_ge(s["mul" if m.gated else "act"], step - 1)
                    if not m.gated:
                        f, size = m.chunks[k % N]
                        mm = products([ps[0:size, 2 * sl + t] for t in range(2)], w_hi, u, f, size, P,
                                      [n_hi[:, half(t)] for t in range(2)], [n_lo[:, half(t)] for t in range(2)])
                    else:
                        f, size = m.chunks[(k % N) // 2]
                        t = k % 2
                        for i in range(2):
                            mm = products([ps[0:size, 2 * sl + i]], w_hi, u, i * m.hidden + f, size, P, [n_hi[:, half(t)]], [n_lo[:, half(t)]])
                    mm.then_inc(s["hid"], 1)

                def down(it, k):
                    u, sl, step = (k // N) % U, k % 2, it * m.steps + k
                    pe.wait_ge(s["h_ready"], step + 1)
                    if k % N == 0:
                        pe.wait_ge(s["wld"], it * U + k // N + 1)
                        if not (isinstance(it, int) and step == 0):
                            pe.wait_ge(s["gate"], it * U + k // N)
                    ci = (k % N) // 2 if m.gated else k % N
                    f, size = m.chunks[ci]
                    ts = [k % 2] if m.gated else [0, 1]
                    hv = [[h[0:size, sl, 0:HALF] if m.gated else h[0:size, sl, half(t)] for t in ts] for h in (h_hi, h_lo)]
                    ends = {"first": ci == 0, "last": ci == len(m.chunks) - 1}
                    if isinstance(it, int) and step == m.total - 1 and not m.gated:
                        for t in ts:
                            products([ps[:, 4 + t]], w_hi, u, m.up + ci * P, P, size, [hv[0][t]], [hv[1][t]], **ends).then_inc(s["h_used"], 1)
                    else:
                        products([ps[:, 4 + t] for t in ts], w_hi, u, m.up + ci * P, P, size, hv[0], hv[1], **ends).then_inc(s["h_used"], 1)

                def spread(it, k):
                    e = it * U + k // N
                    if isinstance(it, int) and e == 0:
                        pe.wait_ge(once["gT"], m.layer + 1)
                    else:
                        pe.wait_ge(s["gcp"], e)
                    for t in range(2):
                        mm = pe.matmul(ps[:, 6 + t], sel[E][:, bass.ds(e, 1)].rearrange("p a c -> p (a c)"), gT[:, half(t)], start=True, stop=True)
                    mm.then_inc(s["g_full"], 1)

                pe.wait_ge(ln["n"], 2 * j + 2)
                for c in range(TILES):
                    mm = pe.matmul(ps[:, 6, c * E:(c + 1) * E], n[:, c * P:(c + 1) * P], wg[L], start=True, stop=True)
                mm.then_inc(once["logit"], 1)
                pe.wait_ge(ln["lo"], 2 * L + 2)
                up(0, 0)
                up(0, 1)

                def body(it):
                    for k in range(m.steps):
                        if isinstance(it, int) and it * m.steps + k >= m.total:
                            break
                        if not isinstance(it, int) or it * m.steps + k + 2 < m.total:
                            up(it, k + 2)
                        first = isinstance(it, int) and it == 0 and k == N - 1
                        if first:
                            if L == 0:
                                pe.wait_ge(in_pack["p_bf16"], 16)
                            pe.wait_ge(once["gsp"], m.layer + 1)
                            for c in range(TILES):
                                mm = pe.transpose(ps[0:3 * E, 7].bitcast(BF16)[:, c * P:(c + 1) * P], gsp[:, c, 0:3 * E], ident16)
                            mm.then_inc(once["gtr"], 1)
                        if k % N == N - 1 and not first and not (isinstance(it, int) and it * U + k // N >= E):
                            spread(it, k)
                        down(it, k)
                        if first:
                            spread(it, k)
                m.run(pe, body)

            pe.wait_ge(in_x, 16)
            pe.wait_ge(in_pack["p_first"], 16)
            norm(0)
            pe.wait_ge(in_ctx, 16)
            pe.wait_ge(in_pack["p_attn1"], 16)
            prepare_keys(0, 0)
            pe.wait_ge(ln["n"], 2)
            prepare_keys(0, 1)
            norm(1, lambda: pe.wait_ge(pre["k"], 2))
            moe(MOES[0])
            norm(2, lambda: (prepare_values(0, 0), prepare_values(0, 1)))
            attention(0)
            norm(3, prepare_text)
            pe.wait_ge(pre["txtcp"], 2)
            moe(MOES[1])
            norm(4)
            pair_sums()
            norm(5)
            moe(MOES[2])
            norm(6)
            attention(1)
            norm(7)
            moe(MOES[3])

        @block.scalar
        def _(act):
            link = linker(act, act_link)

            def norm(j, then=None):
                for t in range(2):
                    act.wait_ge(ln["mean"], 2 * j + t + 1)
                    act.activation(sq[:, half(t)], ps[:, t], ACT.Square).then_inc(ln["sq"], 1)
                for t in range(2):
                    act.copy(xc[:, half(t)], ps[:, t]).then_inc(ln["xc"], 1)
                if then:
                    then()
                if j % 2:
                    for t in range(2):
                        act.wait_ge(ln["n"], 2 * j + t + 1)
                        act.copy(n_hi[:, half(t)], n[:, half(t)]).then_inc(ln["hi"], 1)

            def split_hi(m, it, k):
                s, U = mo[m.layer], m.unroll
                u, e = k % U, it * U + k
                act.wait_ge(w_in[m.layer][u], 16 * (it + k // U + 1))
                if not (isinstance(it, int) and e < U):
                    act.wait_ge(s["h_used"], m.n * (e - U + 1))
                o = u * m.width
                act.copy(w_hi[:, o:o + m.up], w_f32[:, o:o + m.up]).then_inc(s["whu"], 1)
                if m.biases:
                    act.copy(w_hi[:, o + m.up:o + m.split], w_f32[:, o + m.up:o + m.split])
                    if not (isinstance(it, int) and e < U):
                        act.wait_ge(s["gate"], e - U + 1)
                    act.copy(w_bias[:, u, 0:m.biases], w_f32[:, o + m.split:o + m.width]).then_inc(s["whd"], 1)
                else:
                    act.copy(w_hi[:, o + m.up:o + m.split], w_f32[:, o + m.up:o + m.split]).then_inc(s["whd"], 1)

            def first_weights(m):
                if m.layer:
                    act.wait_ge(mo[m.layer - 1]["h_used"], MOES[m.layer - 1].down_total)
                for u in range(m.unroll):
                    split_hi(m, 0, u)

            def prepare_text():
                for t in range(2):
                    act.wait_ge(pre["txt"], t + 1)
                    act.copy(txt[:, half(t)], ps[:, 6 + t]).then_inc(pre["txtcp"], 1)

            def attention(i):
                base = PAIRS * i

                def out_copy(p):
                    act.wait_ge(at["aot"], base + p + 1)
                    if i == 0:
                        ins = act.activation(aoT[:, p * P:(p + 1) * P], ps[:, 7, 0:P], ACT.Identity, bias=abias[:, 6:7])
                    else:
                        ins = act.copy(aoT[:, p * P:(p + 1) * P], ps[:, 7, 0:P])
                    ins.then_inc(at["aocp"], 1)

                for t in range(2):
                    act.wait_ge(at["qT"], 2 * i + t + 1)
                    for r in range(4):
                        ins = act.activation(q_rows[:, r, half(t)], qT[:, half(t)], ACT.Copy, scale=rmask[:, r:r + 1])
                    ins.then_inc(at["q_rows"], 1)
                for p in range(PAIRS):
                    act.wait_ge(at["sub"], base + p + 1)
                    if base + p >= 2:
                        act.wait_ge(at["tr"], 2 * (base + p) - 2)
                    act.activation(p_exp[:, p % 2], s_sub[:, p % 2], ACT.Exp).then_inc(at["exp"], 1)
                    for hh in range(2):
                        act.wait_ge(at["tr"], 2 * (base + p) + hh + 1)
                        if base + p >= 2:
                            act.wait_ge(at["pv"], base + p - 1)
                        act.copy(p_tr[:, p % 2, half(hh)], ps[:, 4 + hh]).then_inc(at["trcp"], 1)
                    if p:
                        out_copy(p - 1)
                out_copy(PAIRS - 1)

            def pair_sums():
                for g in range(2 * B):
                    s, v = ("sumB", g // 3 + 1) if g % 3 == 2 else ("sumA", g - g // 3 + 1)
                    act.wait_ge(x2[s], v)
                    if g >= 3:
                        act.wait_ge(x2["dot"], g - 2)
                    act.activation(tanhs[:, g % 3], sums[:, g % 3], ACT.Tanh).then_inc(x2["tanh"], 1)
                act.wait_ge(x2["soft"], 1)
                act.activation(h_act[:, 0, 0:512], h_act[:, 1, 0:512], ACT.Exp).then_inc(x2["exp"], 1)
                act.wait_ge(x2["wb"], 1)
                for r in range(2):
                    act.activation(st2[:, 4 + r], st2[:, 2 + r], ACT.Tanh, bias=l2b[:, 1 + r:2 + r]).then_inc(x2["tw"], 1)

            def moe(m):
                s, L = mo[m.layer], m.layer
                N, U, E = m.n, m.unroll, m.routed
                if L == 2:
                    act.wait_ge(once["logit"], m.layer + 1)
                    act.activation(rt["e"][:, :, 0:E], ps[:, 6, 0:TILES * E].rearrange("p (c e) -> p c e", e=E), ACT.Sigmoid).then_inc(once["e"], 1)
                else:
                    act.wait_ge(once["cur"], (1, 2, 0, 3)[m.layer])
                    act.activation(rt["e"][:, :, 0:E], rt["cur"][:, :, 0:E], ACT.Exp).then_inc(once["e"], 1)

                def hidden(it, k):
                    step, sl = it * m.steps + k, k % 2
                    act.wait_ge(s["hid"], step + 1)
                    if m.biases and k % N == 0:
                        act.wait_ge(s["whd"], it * U + k // N + 1)
                    if not (isinstance(it, int) and step < 2):
                        act.wait_ge(s["h_ready"], step - 1)
                    if m.gated:
                        size = m.chunks[(k % N) // 2][1]
                        kw = {"bias": w_bias[:, (k // N) % U, 0:1]} if L == 2 else {}
                        act.activation(h_act[0:size, sl, 0:HALF], ps[0:size, 2 * sl], ACT.Silu, **kw).then_inc(s["act"], 1)
                    else:
                        kw = {"bias": w_bias[:, (k // N) % U, k % N:k % N + 1]} if L == 0 else {}
                        act.activation(h_act[:, sl], ps[:, 2 * sl:2 * sl + 2].rearrange("p a c -> p (a c)"), ACT.Gelu, **kw).then_inc(s["act"], 1)

                def gates(it, k):
                    e = it * U + k
                    act.wait_ge(s["g_full"], e + 1)
                    if not (isinstance(it, int) and e < 2):
                        act.wait_ge(s["gate"], e - 1)
                    act.copy(g_sb[:, k % 2], ps[:, 6:8].rearrange("p a c -> p (a c)")).then_inc(s["gcp"], 1)

                def after(it, k):
                    if isinstance(it, int) and it == 0 and k == N:
                        act.wait_ge(once["gtr"], m.layer + 1)
                        act.wait_ge(zeros, 1)
                        act.copy(gT[0:3 * E, :], ps[0:3 * E, 7].bitcast(BF16)).then_inc(once["gT"], 1)
                    e = (k - 2) // N if (k - 2) % N == N - 1 else None
                    if e is not None and not (isinstance(it, int) and not 0 <= it * U + e < E):
                        gates(it, e)
                    e = (k - 3) // N if (k - 3) % N == N - 1 else None
                    if e is not None and not (isinstance(it, int) and not U <= it * U + e + U < m.experts):
                        split_hi(m, it, e + U)

                def body(it):
                    for k in range(m.steps):
                        if not isinstance(it, int) or it * m.steps + k < m.total:
                            hidden(it, k)
                        after(it, k)
                m.run(act, body)
                for k in range(2):
                    if m.experts % U == 0:
                        after(m.bodies, k)

            act.wait_ge(in_pack["p_first"], 16)
            act.activation(tg, tg, ACT.Tanh).then_inc(tg_ready, 1)
            act.wait_ge(in_ctx, 16)
            act.activation(diag[:, :], ctxT[:, :], ACT.Square).then_inc(pre["kv"], 1)
            norm(0)
            first_weights(MOES[0])
            norm(1)
            moe(MOES[0])
            norm(2)
            first_weights(MOES[1])
            attention(0)
            norm(3, prepare_text)
            moe(MOES[1])
            norm(4)
            first_weights(MOES[2])
            pair_sums()
            norm(5)
            moe(MOES[2])
            norm(6)
            first_weights(MOES[3])
            attention(1)
            norm(7)
            moe(MOES[3])

        @block.vector
        def _(dve):
            link = linker(dve, dve_link)

            def norm(j):
                for t in range(2):
                    dve.wait_ge(ln["var"], 2 * j + t + 1)
                    dve.tensor_scalar(var_eps[:, t * HT:(t + 1) * HT], ps[:, 2 + t, 0:HT], EPS, None, ALU.add).then_inc(ln["eps"], 1)
                if j == 0:
                    dve.wait_ge(in_pack["p_first"], 16)
                for t in range(2):
                    dve.wait_ge(ln["rstd"], 2 * j + t + 1)
                    dve.tensor_tensor(diag[:, half(t)].rearrange("p (c k) -> p c k", k=P), bcast(ident, 1, HT),
                                      bcast(rstd[:, t * HT:(t + 1) * HT], 2, P), ALU.mult).then_inc(ln["diag"], 1)
                for t in range(2):
                    dve.wait_ge(ln["bc"], 2 * j + t + 1)
                    dve.wait_ge(ln["xc"], 2 * j + t + 1)
                    dve.tensor_tensor(n[:, half(t)], xc[:, half(t)], ps[:, 4 + t], ALU.mult).then_inc(ln["n"], 1)
                if j % 2:
                    i = j // 2
                    for t in range(2):
                        dve.wait_ge(ln["hi"], 2 * i + t + 1)
                        dve.tensor_tensor(n_lo[:, half(t)], n[:, half(t)], n_hi[:, half(t)].bitcast(F32), ALU.subtract).then_inc(ln["lo"], 1)

            def rotate(dst, t, banks, tab, bias):
                v = dst[:, half(t)].rearrange("p (b s) -> p b s", s=S)
                tmp = y_g[:, t, 0:HALF].rearrange("p (b s) -> p b s", s=S)
                b0 = abias[:, bias:bias + 1] if bias is not None else 0.0
                b1 = abias[:, bias + 1:bias + 2] if bias is not None else 0.0
                dve.scalar_tensor_tensor(v, ps[:, banks].rearrange("p (b s) -> p b s", s=S), b0, bcast(rope[:, tab], 1, 8), ALU.add, ALU.mult)
                link(dve.scalar_tensor_tensor(tmp, ps[:, banks + 1].rearrange("p (b s) -> p b s", s=S), b1, bcast(rope[:, tab + 1], 1, 8), ALU.add, ALU.mult))
                return dve.tensor_tensor(v, v, tmp, ALU.add)

            def prepare_keys(i):
                for t in range(2):
                    dve.wait_ge(pre["proj"], 2 * i + t + 1)
                    rotate(kT[i], t, KBANK[i][t], 2, 2 if i == 0 else None).then_inc(pre["k"], 1)

            def prepare_values(i, q):
                r = 4 * i + q
                dve.wait_ge(pre["v"], r + 1)
                if r == 0:
                    dve.wait_ge(zeros, 1)
                for h2 in range(2):
                    rows = slice(64 * h2, 64 * h2 + 64)
                    src = ps[rows, VBANK[i] + q % 2].rearrange("p (b h c d) -> p (b h) c d", b=4, h=8, c=2)[:, :, h2]
                    dst = vblk[i][rows, 4 * q:4 * q + 4].rearrange("p b h (c d) -> p (b h) c d", c=2)[:, :, h2, 0:8]
                    ins = dve.tensor_copy(dst, src)
                ins.then_inc(pre["vcp"], 1)

            def attention(i):
                base = PAIRS * i
                for t in range(2):
                    dve.wait_ge(at["q"], 2 * i + t + 1)
                    rotate(qT, t, 4 * t, 0, 0 if i == 0 else None).then_inc(at["qT"], 1)

                def soft(p):
                    g = base + p
                    dve.wait_ge(at["sc"], g + 1)
                    sc = ps[:, SCB[p % 2]:SCB[p % 2] + 2].rearrange("p a (h k) -> p (a h) k", k=S)
                    dve.tensor_reduce(mx[:, p % 2], sc, AX, ALU.max).then_inc(at["max"], 1)
                    dve.wait_ge(at["max"], g + 1)
                    if g >= 2:
                        dve.wait_ge(at["exp"], g - 1)
                    dve.tensor_tensor(s_sub[:, p % 2].rearrange("p (h k) -> p h k", k=S), sc, bcast(mx[:, p % 2], 2, S),
                                      ALU.subtract).then_inc(at["sub"], 1)

                def output(p):
                    g = base + p
                    dve.wait_ge(at["pv"], g + 1)
                    o = ps[:, 6, 0:144].rearrange("p (h c) -> p h c", c=9)
                    link(dve.reciprocal(rsum[:, p % 2], o[:, :, 8]))
                    if g >= 2:
                        dve.wait_ge(at["aot"], g - 1)
                    dve.tensor_tensor(ao[:, p % 2].rearrange("p (h d) -> p h d", d=HD), o[:, :, 0:HD], bcast(rsum[:, p % 2], 2, HD),
                                      ALU.mult).then_inc(at["ao"], 1)

                def update(t):
                    dve.wait_ge(at["proj"], 2 * i + t + 1)
                    bo = abias[:, 5:6] if i == 0 else 0.0
                    dve.scalar_tensor_tensor(x[:, half(t)], ps[:, 7], bo, x[:, half(t)], ALU.add, ALU.add).then_inc(x_done[t], 1)

                if i == 0:
                    prepare_values(0, 2)
                    prepare_values(0, 3)
                soft(0)
                for p in range(PAIRS):
                    if p + 1 < PAIRS:
                        soft(p + 1)
                    if p == HT + 1:
                        update(0)
                    output(p)
                update(1)

            def pair_sums():
                for t in range(2):
                    dve.wait_ge(x2["feat"], t + 1)
                    dve.tensor_scalar(xc[:, half(t)], ps[:, t], l2b[:, 0:1], None, ALU.add).then_inc(x2["fb"], 1)
                dve.wait_ge(x2["fb"], 2)
                for g in range(2 * B):
                    if g == 6:
                        prepare_keys(1)
                    if g in (9, 12, 15, 18):
                        prepare_values(1, (g - 9) // 3)
                    if g == 3:
                        dve.tensor_scalar(wqk3[:, 5], wqk3[:, 5], tg[:, 3:4], None, ALU.mult).then_inc(pre["wo"], 1)
                        dve.wait_ge(in_pack["mask"], 16)
                        link(dve.tensor_scalar(mbias[:, 0], qmask[:, :], -1.0, 1.0, ALU.mult, ALU.add))
                        link(dve.tensor_scalar(mbias[:, 1], mbias[:, 0], NEG, None, ALU.mult))
                    if g % 3 == 2:
                        continue
                    if g >= 3:
                        dve.wait_ge(x2["tanh"], g - 2)
                    dve.tensor_tensor(*sum_of(g), ALU.add).then_inc(x2["sumA"], 1)
                dve.wait_ge(pre["uv"], 2)
                dve.tensor_copy(uv[:, :, :], ps[:, 7, 0:2 * S].rearrange("p (r s) -> p r s", r=2)).then_inc(pre["uvcp"], 1)
                dve.wait_ge(x2["dot"], 2 * B)
                r3 = h_act[:, 1, 0:512].rearrange("p (f s) -> p f s", s=S)
                e3 = h_act[:, 0, 0:512].rearrange("p (f s) -> p f s", s=S)
                t3 = h_act[:, 1, 512:1024].rearrange("p (f s) -> p f s", s=S)
                link(dve.tensor_tensor(r3, ps[:, 6].rearrange("p (f s) -> p f s", s=S), bcast(mbias[:, 1], 1, 8), ALU.add))
                link(dve.tensor_reduce(st2[:, 0], r3, AX, ALU.max))
                dve.tensor_tensor(r3, r3, bcast(st2[:, 0], 2, S), ALU.subtract).then_inc(x2["soft"], 1)
                dve.wait_ge(x2["exp"], 1)
                link(dve.tensor_reduce(st2[:, 0], e3, AX, ALU.add))
                link(dve.reciprocal(st2[:, 1], st2[:, 0]))
                for r in range(2):
                    link(dve.tensor_tensor(t3, e3, bcast(uv[:, r], 1, 8), ALU.mult))
                    link(dve.tensor_reduce(st2[:, 2 + r], t3, AX, ALU.add))
                for r in range(2):
                    ins = dve.tensor_tensor(st2[:, 2 + r], st2[:, 2 + r], st2[:, 1], ALU.mult)
                ins.then_inc(x2["wb"], 1)
                dve.wait_ge(x2["tw"], 2)
                for r in range(2):
                    link(dve.tensor_scalar(st2[:, 2 + r], st2[:, 4 + r], tg[:, 2:3], None, ALU.mult))
                    dve.tensor_tensor((diag, sq)[r][:, :].rearrange("p (c f) -> p c f", f=8), bcast(perm, 2, 8),
                                      bcast(st2[:, 2 + r], 1, P), ALU.mult).then_inc(x2["d"], 1)
                for t in range(2):
                    dve.wait_ge(x2["bc"], t + 1)
                    dve.tensor_tensor(xc[:, half(t)], n[:, half(t)], ps[:, t], ALU.mult).then_inc(x2["mb"], 1)
                for t in range(2):
                    dve.wait_ge(x2["bc"], t + 3)
                    dve.wait_ge(x2["mb"], t + 1)
                    link(dve.tensor_tensor(xc[:, half(t)], xc[:, half(t)], ps[:, 2 + t], ALU.add))
                    dve.tensor_tensor(x[:, half(t)], x[:, half(t)], xc[:, half(t)], ALU.add).then_inc(x_done[t], 1)

            def top(cur, count, width, chosen):
                top8, need = rt["top8"][:, :, 0:8], rt_m[:, 1, 0:TILES]
                above, equal, rank = (rt[k][:, :, 0:width] for k in ("above", "equal", "rank"))
                for c in range(TILES):
                    ins = dve.max(top8[:, c], cur[:, c])
                link(ins)
                least = bcast(top8[:, :, count - 1], 2, width)
                dve.tensor_tensor(equal, cur, least, ALU.is_equal)
                link(dve.tensor_tensor(above, cur, least, ALU.is_gt))
                dve.tensor_reduce(need, above, AX, ALU.add)
                for c in range(TILES):
                    ins = dve.tensor_tensor_scan(rank[:, c], ones_row[:, 0:width], equal[:, c], 0.0, ALU.mult, ALU.add)
                link(ins)
                link(dve.tensor_tensor(rank, rank, bcast(need, 2, width), ALU.add))
                link(dve.scalar_tensor_tensor(equal, rank, float(count), equal, ALU.is_le, ALU.mult))
                link(dve.tensor_tensor(chosen, above, equal, ALU.add))

            def route(m):
                s, L, E = mo[m.layer], m.layer, m.routed
                e, cur, w, chosen = (rt[k][:, :, 0:E] for k in ("e", "cur", "w", "chosen"))
                if L == 2:
                    dve.wait_ge(once["e"], m.layer + 1)
                    e4 = e.rearrange("p c (g k) -> p c g k", g=4)
                    cur4 = cur.rearrange("p c (g k) -> p c g k", g=4)
                    gs = groups[:, 1, :, 0:4]
                    link(dve.tensor_reduce(groups[:, 0, :, 0:4], e4, AX, ALU.max))
                    top(groups[:, 0], 2, 8, groups[:, 1])
                    link(dve.tensor_tensor(cur4, e4, bcast(gs, 3, 4), ALU.mult))
                    link(dve.tensor_scalar(gs, gs, 1.0, None, ALU.subtract))
                    link(dve.tensor_tensor(cur4, cur4, bcast(gs, 3, 4), ALU.add))
                    top(cur, 4, 16, chosen)
                else:
                    top(cur, m.topk, E, chosen)
                    dve.wait_ge(once["e"], m.layer + 1)
                total, inv = rt_m[:, 0, 0:TILES], rt_m[:, 1, 0:TILES]
                link(dve.tensor_tensor(w, e, chosen, ALU.mult))
                link(dve.tensor_reduce(total, e if L == 3 else w, AX, ALU.add))
                link(dve.reciprocal(inv, total))
                link(dve.tensor_scalar(inv, inv, tg[:, 4 + L:5 + L], 2.5 if L == 2 else 1.0, ALU.mult, ALU.mult))
                dve.tensor_tensor(w, w, bcast(inv, 2, E), ALU.mult).then_inc(once["w"], 1)

            def moe(m):
                s, L = mo[m.layer], m.layer
                N, U, E = m.n, m.unroll, m.routed
                def split(it, k):
                    step, sl = it * m.steps + k, k % 2
                    dve.wait_ge(s["act"], step + 1)
                    if m.gated:
                        size = m.chunks[(k % N) // 2][1]
                        ha = h_act[0:size, sl, 0:HALF]
                        b3 = w_bias[:, k // N, 1:2] if L == 2 else 0.0
                        dve.scalar_tensor_tensor(ha, ps[0:size, 2 * sl + 1], b3, ha, ALU.add, ALU.mult).then_inc(s["mul"], 1)
                        dve.wait_ge(s["mul"], step + 1)
                        hi, lo = h_hi[0:size, sl, 0:HALF], h_lo[0:size, sl, 0:HALF]
                    else:
                        ha, hi, lo = h_act[:, sl], h_hi[:, sl], h_lo[:, sl]
                    if not (isinstance(it, int) and step < 2):
                        dve.wait_ge(s["h_used"], step - 1)
                    dve.tensor_copy(hi, ha).then_inc(s["hi"], 1)
                    dve.wait_ge(s["hi"], step + 1)
                    dve.tensor_tensor(lo, ha, hi.bitcast(F32), ALU.subtract).then_inc(s["h_ready"], 1)

                lg = ps[:, 6, 0:TILES * E].rearrange("p (c e) -> p c e", e=E)
                cur = rt["cur"][:, :, 0:E]
                if L == 0:
                    dve.wait_ge(once["logit"], m.layer + 1)
                    link(dve.tensor_tensor(rt["lg"][:, :, 0:E], lg, bcast(gb0, 1, TILES), ALU.add))
                    lg = rt["lg"][:, :, 0:E]
                if L != 2:
                    dve.wait_ge(once["logit"], m.layer + 1)
                    link(dve.tensor_reduce(rt_m[:, 3, 0:TILES], lg, AX, ALU.max))
                    dve.tensor_tensor(cur, lg, bcast(rt_m[:, 3, 0:TILES], 2, E), ALU.subtract).then_inc(once["cur"], 1)
                if L == 2:
                    route(m)
                split(0, 0)
                split(0, 1)
                if L != 2:
                    dve.wait_ge(once["cur"], (1, 2, 0, 3)[m.layer])
                    route(m)
                if L == 3:
                    dve.scalar_tensor_tensor(x[:, :], n[:, :], tg[:, 7:8], x[:, :], ALU.mult, ALU.add).then_inc(s["xn"], 1)

                def gate(it, k):
                    e = it * U + k
                    yy, dst = ps[:, 4:6].rearrange("p a c -> p (a c)"), y_g[:, k % 2]
                    dve.wait_ge(s["h_used"], N * (e + 1))
                    if not (isinstance(it, int) and e < 2):
                        dve.wait_ge(s["acc"], e - 1)
                    if isinstance(it, int) and e >= E:
                        dve.tensor_scalar(dst, yy, tg[:, 4 + L:5 + L], None, ALU.mult).then_inc(s["gate"], 1)
                        return
                    dve.wait_ge(s["gcp"], e + 1)
                    if m.biases:
                        dve.scalar_tensor_tensor(dst, yy, w_bias[:, k % U, m.biases - 1:m.biases], g_sb[:, k % 2], ALU.add, ALU.mult).then_inc(s["gate"], 1)
                    else:
                        dve.tensor_tensor(dst, yy, g_sb[:, k % 2], ALU.mult).then_inc(s["gate"], 1)

                def body(it):
                    for k in range(m.steps):
                        if isinstance(it, int) and it * m.steps + k >= m.total:
                            break
                        if not (isinstance(it, int) and it == 0 and k < 2):
                            split(it, k)
                        if (k - 1) % N == N - 1 and not (isinstance(it, int) and it * m.steps + k < N):
                            gate(it, (k - 1) // N)
                m.run(dve, body)
                e, k = m.experts - 1, (m.experts - 1) % U
                dve.wait_ge(s["acc"], e)
                for t in range(2):
                    dve.wait_ge(s["h_used"], m.down_total - 1 + t)
                    yy, xh, dst = ps[:, 4 + t], x[:, half(t)], y_g[:, k % 2, half(t)]
                    if e >= E:
                        dve.scalar_tensor_tensor(xh, yy, tg[:, 4 + L:5 + L], xh, ALU.mult, ALU.add).then_inc(x_done[t], 1)
                        continue
                    dve.wait_ge(s["gcp"], e + 1)
                    if m.biases:
                        link(dve.scalar_tensor_tensor(dst, yy, w_bias[:, k, m.biases - 1:m.biases], g_sb[:, k % 2, half(t)], ALU.add, ALU.mult))
                    else:
                        link(dve.tensor_tensor(dst, yy, g_sb[:, k % 2, half(t)], ALU.mult))
                    dve.tensor_tensor(xh, xh, dst, ALU.add).then_inc(x_done[t], 1)

            dve.memset(var_w[:, :], 1.0 / P)
            dve.memset(ones_w[:, :], 1.0)
            dve.memset(ones_row[:, :], 1.0)
            dve.memset(groups[:, 0], -1.0)
            dve.memset(minus_half[:, :], -0.5).then_inc(consts, 1)
            link(dve.memset(h_act[:, 0], DECAY))
            link(dve.memset(h_act[:, 0].rearrange("p (b s) -> p b s", s=S)[:, :, 0], 0.0))
            dve.wait_ge(pre["kv"], 1)
            dve.tensor_tensor_scan(h_act[:, 1], h_act[:, 0], diag[:, :], 0.0, ALU.mult, ALU.add).then_inc(pre["scan"], 1)
            norm(0)
            dve.wait_ge(pre["scan"], 1)
            dve.wait_ge(tg_ready, 1)
            for t in range(2):
                dve.wait_ge(ln["n"], t + 1)
                link(dve.scalar_tensor_tensor(n[:, half(t)], n[:, half(t)], tg[:, 0:1], h_act[:, 1, half(t)], ALU.mult, ALU.mult))
                dve.tensor_tensor(x[:, half(t)], x[:, half(t)], n[:, half(t)], ALU.add).then_inc(x_done[t], 1)
            dve.wait_ge(in_pack["p_attn1"], 16)
            dve.tensor_scalar(wqk1[:, 5], wqk1[:, 5], tg[:, 1:2], None, ALU.mult).then_inc(pre["wo"], 1)
            link(dve.tensor_scalar(abias[:, 5:6], abias[:, 4:5], tg[:, 1:2], None, ALU.mult))
            prepare_keys(0)
            norm(1)
            moe(MOES[0])
            norm(2)
            for q in range(2):
                prepare_values(0, q)
            attention(0)
            norm(3)
            moe(MOES[1])
            norm(4)
            pair_sums()
            norm(5)
            moe(MOES[2])
            norm(6)
            attention(1)
            norm(7)
            moe(MOES[3])

        @block.gpsimd
        def _(pool):
            link = linker(pool, pool_link)

            def norm(j):
                for t in range(2):
                    r = slice(t * HT, (t + 1) * HT)
                    pool.wait_ge(ln["eps"], 2 * j + t + 1)
                    pool.tensor_tensor(rstd[:, r], var_eps[:, r], minus_half[:, r], ALU.pow).then_inc(ln["rstd"], 1)

            def split_lo(m, it, k):
                s, U = mo[m.layer], m.unroll
                u, e = k % U, it * U + k
                o = u * m.width
                for hi, lo, c0, c1 in (("whu", "wlu", 0, m.up), ("whd", "wld", m.up, m.split)):
                    pool.wait_ge(s[hi], e + 1)
                    pool.tensor_tensor(w_lo[:, o + c0:o + c1], w_f32[:, o + c0:o + c1], w_hi[:, o + c0:o + c1].bitcast(F32),
                                       ALU.subtract).then_inc(s[lo], 1)

            def first_weights(m):
                for u in range(m.unroll):
                    split_lo(m, 0, u)

            def expand_keys(i, q):
                src = kT[i][:, 4 * q * S:4 * (q + 1) * S].rearrange("p (b k) -> p b k", b=4)
                pool.tensor_tensor(kexp[:, 4 * q:4 * q + 4], bcast(src, 2, 4), bcast(bcast(hmask, 2, S), 1, 4), ALU.mult).then_inc(at["kexp"], 1)

            def pair_sums():
                pool.wait_ge(x2["fb"], 2)
                for g in range(2, 2 * B, 3):
                    if g >= 3:
                        pool.wait_ge(x2["tanh"], g - 2)
                    pool.tensor_tensor(*sum_of(g), ALU.add).then_inc(x2["sumB"], 1)

            def gate_parts(m):
                s, E = mo[m.layer], m.routed
                w = rt["w"][:, :, 0:E]
                part = [gsp[:, :, r * E:(r + 1) * E] for r in range(3)]
                pool.wait_ge(once["w"], m.layer + 1)
                link(pool.tensor_copy(part[0], w))
                link(pool.tensor_tensor(w, w, part[0], ALU.subtract))
                link(pool.tensor_copy(part[1], w))
                link(pool.tensor_tensor(w, w, part[1], ALU.subtract))
                pool.tensor_copy(part[2], w).then_inc(once["gsp"], 1)

            def moe(m, then=None):
                s, U = mo[m.layer], m.unroll
                gate_parts(m)
                if then:
                    then()
                if m.layer == 3:
                    pool.wait_ge(s["xn"], 1)

                def accumulate(it, k):
                    e = it * U + k
                    pool.wait_ge(s["gate"], e + 1)
                    if not (isinstance(it, int) and e == 0):
                        pool.wait_ge(s["acc"], e)
                    pool.tensor_tensor(x[:, :], x[:, :], y_g[:, k % 2], ALU.add).then_inc(s["acc"], 1)

                def body(it):
                    for k in range(U):
                        if isinstance(it, int) and it * U + k >= m.experts - 1:
                            break
                        accumulate(it, k)
                        if not isinstance(it, int) or it * U + k + U < m.experts:
                            split_lo(m, it, k + U)
                m.run(pool, body)

            for i in range(2):
                link(pool.memset(vblk[i][:].rearrange("p b h c -> p (b h c)"), 0.0))
                for h2 in range(2):
                    ones = vblk[i][64 * h2:64 * h2 + 64].rearrange("p b h (c d) -> p (b h) c d", c=2)[:, :, h2, 8:9]
                    link(pool.memset(ones, 1.0))
            pool.memset(gT[:, :], 0.0).then_inc(zeros, 1)
            pool.wait_ge(consts, 1)
            norm(0)
            first_weights(MOES[0])
            norm(1)
            pool.wait_ge(in_pack["p_attn1"], 16)
            pool.wait_ge(pre["k"], 2)
            for q in range(2):
                expand_keys(0, q)
            moe(MOES[0], lambda: (expand_keys(0, 2), expand_keys(0, 3)))
            norm(2)
            first_weights(MOES[1])
            norm(3)
            moe(MOES[1])
            norm(4)
            first_weights(MOES[2])
            pair_sums()
            norm(5)
            pool.wait_ge(pre["k"], 4)
            for q in range(2):
                expand_keys(1, q)
            moe(MOES[2], lambda: (expand_keys(1, 2), expand_keys(1, 3)))
            norm(6)
            first_weights(MOES[3])
            norm(7)
            moe(MOES[3])


def constants():
    c = {"ident": np.eye(P, dtype=np.float32)}
    c["cen"] = (np.eye(P) - 1.0 / P).astype(np.float32)
    one16 = np.uint16(0x3F80)
    c["ident16"] = np.eye(P, dtype=np.uint16) * one16
    for e in (8, 16):
        s = np.zeros((P, e, P), np.uint16)
        for r in range(3 * e):
            s[r, r % e] = one16
        c[f"sel{e}"] = s
    pair = (np.arange(P) % HD) // 2
    freq = (1.0 / 10000.0 ** (np.arange(0, HD, 2, dtype=np.float64) / HD)).astype(np.float32)[pair]
    ang = (np.arange(S, dtype=np.float32)[None, :] * freq[:, None]).astype(np.float32).astype(np.float64)
    sign = np.where(np.arange(P) % 2 == 0, -1.0, 1.0)[:, None]
    cos, sin = np.cos(ang), np.sin(ang) * sign
    scale = 1.0 / np.sqrt(HD)
    c["rope"] = np.stack([cos * scale, sin * scale, cos, sin], axis=1).astype(np.float32)
    c["hmask"] = (np.arange(P)[:, None] // HD % 4 == np.arange(4)[None, :]).astype(np.float32)
    c["rmask"] = (np.arange(P)[:, None] // (4 * HD) == np.arange(4)[None, :]).astype(np.float32)
    perm = np.zeros((P, P), np.float32)
    for b in range(B):
        for h in range(2):
            for q in range(4):
                perm[32 * q + 2 * b + h, 8 * b + 4 * h + q] = 1.0
    c["perm"] = perm
    return c


def kernel(**inputs):
    import concourse.bacc as bacc
    from concourse.bass_utils import run_bass_kernel_spmd

    i = {k: np.asarray(v) for k, v in inputs.items()}
    f = np.ascontiguousarray

    def rows(v):
        return np.tile(v.reshape(1, -1), (P, 1))

    def chunked(w):
        e, h, d = w.shape
        c = -(-h // P)
        w = np.concatenate([w, np.zeros((e, c * P - h, d), w.dtype)], axis=1)
        return w.reshape(e, c, P, d).transpose(0, 2, 1, 3).reshape(e, P, c * d)

    def tr(w):
        return w.transpose(0, 2, 1)

    def col(v):
        return v.reshape(v.shape[0], -1, P).transpose(0, 2, 1)

    swap = np.arange(P) ^ 1

    def attention_weights(wq, wk, wv, wo):
        return np.stack([wq.T, wq[swap].T, wk.T, wk[swap].T, wv.T, wo.T], axis=1)

    small = constants()
    small["gates"] = rows(np.concatenate([i["g_xattn"], i["g_ffn"]]))
    small["attn1"] = attention_weights(*(i[f"L1_xattn_{k}"] for k in ("wq", "wk", "wv", "wo")))
    small["attn3"] = attention_weights(*(i[f"L3_xattn_W_{k}"] for k in "qkvo"))
    bq, bk, bo = i["L1_xattn_bq"], i["L1_xattn_bk"], i["L1_xattn_bo"]
    small["abias"] = np.stack([bq, bq[swap], bk, bk[swap], bo, bo, i["L1_xattn_bv"]], axis=1)
    small["wg0"], small["wg1"], small["wg2"] = i["L0_ffn_gate_w"].T, i["L1_ffn_Wg"].T, i["L2_ffn_Wg"].T
    small["wg3"], small["gb0"] = i["L3_ffn_router_w"], rows(i["L0_ffn_gate_b"])
    small["l2w"] = np.stack([i["L2_xattn_Ws"], i["L2_xattn_W"]], axis=1)
    small["l2pad"] = np.zeros((P, 63), np.float32)
    small["l2pad"][:, 31] = i["L2_xattn_w"][:, 0]
    small["l2uv"] = np.zeros((P, 2, 5, 32), np.float32)
    for r, k in enumerate(("L2_xattn_Wcw", "L2_xattn_Wcb")):
        small["l2uv"][:, r, :, 30:32] = i[k][0][:, None, None]
    small["l2uv"] = small["l2uv"].reshape(P, 2, 160)[:, :, 0:158]
    small["l2b"] = np.concatenate([i["L2_xattn_b"].T, rows(i["L2_xattn_bcw"]), rows(i["L2_xattn_bcb"])], axis=1)

    arr = {"xT": f(i["x"].reshape(T, P).T), "ctxT": f(i["ctx_1024"].reshape(T, P).T)}
    for name, fields in PACKS.items():
        arr[name] = f(np.concatenate([small[k].reshape(P, -1) for k in fields], axis=1))
    arr["w0"] = f(np.concatenate([i["L0_ffn_w1"], chunked(i["L0_ffn_w2"]), col(i["L0_ffn_b1"]), col(i["L0_ffn_b2"])], axis=2))
    arr["w1"] = f(np.concatenate([tr(i["L1_ffn_W1"]), tr(i["L1_ffn_W3"]), chunked(tr(i["L1_ffn_W2"]))], axis=2))
    arr["w2"] = f(np.concatenate([tr(i["L2_ffn_W1"]), tr(i["L2_ffn_W3"]), chunked(tr(i["L2_ffn_W2"])),
                                 col(i["L2_ffn_b1"]), col(i["L2_ffn_b3"]), col(i["L2_ffn_b2"])], axis=2))
    up3 = np.concatenate([i["L3_ffn_routed_up"], i["L3_ffn_shared_up"]], axis=0)
    dn3 = np.concatenate([i["L3_ffn_routed_down"], i["L3_ffn_shared_down"]], axis=0)
    arr["w3"] = f(np.concatenate([up3, chunked(dn3)], axis=2))
    arr["mask_rows"] = f(np.tile(np.repeat(i["mask_BxS2_ik0"], 2, axis=0), (4, 1)))

    nc = bacc.Bacc("TRN2", target_bir_lowering=False, num_devices=1)
    aps = {k: nc.dram_tensor(f"in_{k}", v.shape, mybir.dt.from_np(v.dtype), kind="ExternalInput").ap() for k, v in arr.items()}
    out = nc.dram_tensor("out_xT", (P, T), F32, kind="ExternalOutput").ap()
    flamingo(nc, aps, out)
    r = run_bass_kernel_spmd(nc, [{f"in_{k}": v for k, v in arr.items()}], core_ids=[0])
    return f(r.results[0]["out_xT"].T).reshape(B, S, P)
```

```python
from contextlib import ExitStack

import numpy as np

import concourse.bass as bass
from concourse import mybir

F32 = mybir.dt.float32
F32R = mybir.dt.float32r
BF16 = mybir.dt.bfloat16
I32 = mybir.dt.int32
ACT = mybir.ActivationFunctionType
ALU = mybir.AluOpType
AX = mybir.AxisListType.X

P = 128
B, S = 16, 64
T = B * S
TILES = T // P
HALF = T // 2
HT = TILES // 2
HEADS, HD = 16, 8
PAIRS = B // 2
EPS = 1e-5
DECAY = 0.9
NEG = -1e30




class Moe:

    def __init__(self, layer, experts, hidden, gated, unroll, topk, routed=None, biases=0):
        self.biases = biases
        self.layer, self.experts, self.gated, self.unroll, self.topk = layer, experts, gated, unroll, topk
        self.routed = routed or experts
        self.chunks = [(f, min(P, hidden - f)) for f in range(0, hidden, P)]
        self.n = len(self.chunks) * (2 if gated else 1)
        self.steps = self.n * unroll
        self.up = hidden * (2 if gated else 1)
        self.split = self.up + P * len(self.chunks)
        self.width = self.split + biases
        self.hidden = hidden
        self.total = self.n * experts
        self.act_high = layer == 2
        self.gates = 2 if gated else 1
        self.down_total = self.total + (not gated)
        self.bodies = -(-experts // unroll)
        self.loop_end = (experts - 2 * unroll) // unroll + 1

    def run(self, eng, body):
        body(0)
        if self.loop_end > 1:
            with eng.Fori(1, self.loop_end) as it:
                body(it)
        for it in range(max(self.loop_end, 1), self.bodies):
            body(it)


MOES = [
    Moe(0, 8, 512, False, 2, 2, biases=5),
    Moe(1, 8, 352, True, 2, 2),
    Moe(2, 16, 128, True, 4, 4, biases=3),
    Moe(3, 9, 512, False, 2, 2, routed=8),
]


PACKS = {
    "p_first": {"gates": (8,), "ident": (P,), "cen": (P,)},
    "p_attn1": {"rope": (4, S), "hmask": (4,), "rmask": (4,), "abias": (7,), "attn1": (6, P), "wg0": (8,), "gb0": (8,)},
    "p_rest": {"attn3": (6, P), "wg1": (8,), "wg2": (16,), "before": (4, 4), "wg3": (8,), "l2w": (2, P), "l2pad": (63,), "l2uv": (2, 158), "l2b": (3,),
               "perm": (P,)},
    "p_bf16": {"ident16": (P,), "sel8": (8, P), "sel16": (16, P)},
}


def bcast(ap, dim, count):
    shape = list(ap.shape)
    return ap.unsqueeze(dim).broadcast_to(shape[:dim] + [count] + shape[dim:])


def flamingo(nc, a, out):
    ctx = ExitStack()
    with ctx:
        def sb(name, shape, dt=F32):
            return ctx.enter_context(nc.sbuf_tensor(name, shape, dt))

        def sem(name):
            return ctx.enter_context(nc.semaphore(name))

        x = sb("x", [P, T])
        n = sb("n", [P, T])
        n_hi = sb("n_hi", [P, T], F32R)
        n_lo = sb("n_lo", [P, T], F32R)
        xc = sb("xc", [P, T])
        sq = sb("sq", [P, T])
        diag = sb("diag", [P, T])
        ctxT = sb("ctxT", [P, T])
        kT = [sb("kT1", [P, T]), sb("kT3", [P, T])]
        vblk = [sb("vblk1", [P, B, 8, 18]), sb("vblk3", [P, B, 8, 18])]
        txt = sb("txt", [P, T])
        uv = sb("uv", [P, 2, S])
        work = sb("work", [P, 12 * T])
        wslot = max(m.width * m.unroll for m in MOES)
        w_f32 = sb("w_f32", [P, wslot])
        w_hi = sb("w_hi", [P, wslot], F32R)
        w_lo = sb("w_lo", [P, wslot], F32R)
        w_bias = sb("w_bias", [P, 4, 5])
        h_act = sb("h_act", [P, 2, T])
        h_hi = sb("h_hi", [P, 2, T], F32R)
        h_lo = sb("h_lo", [P, 2, T], F32R)
        g_sb = sb("g_sb", [P, 2, T])
        y_g = sb("y_g", [P, 2, T])

        packed = {}
        for name, fields in PACKS.items():
            total = sum(int(np.prod(shape)) for shape in fields.values())
            tile = sb(name, [P, total], BF16 if name == "p_bf16" else F32)
            at_col = 0
            for field, shape in fields.items():
                size = int(np.prod(shape))
                view = tile[:, at_col:at_col + size]
                packed[field] = view.rearrange("p (a b) -> p a b", a=shape[0]) if len(shape) == 2 else view
                at_col += size
            packed[name] = tile
        ident, cen_w, tg = packed["ident"], packed["cen"], packed["gates"]
        rope, hmask, rmask, perm = packed["rope"], packed["hmask"], packed["rmask"], packed["perm"]
        wqk1, wqk3, abias, l2w = packed["attn1"], packed["attn3"], packed["abias"], packed["l2w"]
        l2pad, l2uvpad, l2b = packed["l2pad"], packed["l2uv"], packed["l2b"]
        ident16, sel = packed["ident16"], {8: packed["sel8"], 16: packed["sel16"]}
        wg, gb0 = [packed[f"wg{m.layer}"] for m in MOES], packed["gb0"]
        var_w = sb("var_w", [P, 1])
        ones_w = sb("ones_w", [P, P])
        starts = {e: sb(f"starts{e}", [P, TILES * e]) for e in (8, 16)}
        minus_half = sb("minus_half", [P, TILES])
        qmask = sb("qmask", [P, S], I32)
        mbias = sb("mbias", [P, 2, S])
        var_eps = sb("var_eps", [P, TILES])
        rstd = sb("rstd", [P, TILES])
        rt = {k: sb(f"rt_{k}", [P, TILES * 16]) for k in ("lg", "cur", "e", "top8", "above", "equal", "rank", "chosen", "w")}
        rt_m = sb("rt_m", [P, 4, 4 * TILES])
        gsp = sb("gsp", [P, TILES, 3 * 16], BF16)
        gT = sb("gT", [P, T], BF16)
        mx = sb("mx", [P, 2, HEADS])
        rsum = sb("rsum", [P, 2, HEADS])
        ao = sb("ao", [P, 2, P])
        st2 = sb("st2", [P, 6, 8])

        ps = ctx.enter_context(nc.psum_tensor("ps", [P, 8, 512], F32))

        kexp = work[:, 0:4 * T].rearrange("p (b h k) -> p b h k", b=B, h=4)
        q_rows = work[:, 4 * T:8 * T].rearrange("p (r t) -> p r t", r=4)
        s_sub = work[:, 8 * T:10 * T].rearrange("p (r c) -> p r c", r=2)
        p_exp, p_tr = y_g, g_sb
        qT, aoT = xc, sq
        SCB = (2, 0)
        DOTS = (6, 5)
        KBANK = ((6, 6), (0, 2))
        VBANK = (6, 0)
        sums = work[:, 0:6 * T].rearrange("p (r c) -> p r c", r=3)
        tanhs = work[:, 6 * T:12 * T].rearrange("p (r c) -> p r c", r=3)

        in_x, in_ctx = sem("in_x"), sem("in_ctx")
        in_pack = {name: sem(f"in_{name}") for name in (*PACKS, "mask")}
        consts = sem("consts")
        tg_ready, zeros = sem("tg_ready"), sem("zeros")
        dve_link, pool_link = sem("dve_link"), sem("pool_link")
        x_done = [sem("x_done0"), sem("x_done1")]
        ln = {k: sem(f"ln_{k}") for k in ("mean", "xc", "sq", "var", "eps", "rstd", "diag", "bc", "n", "hi", "lo")}
        pre = {k: sem(f"pre_{k}") for k in ("kv", "scan", "proj", "k", "v", "vcp", "txt", "txtcp", "uv", "uvcp", "wo")}
        at = {k: sem(f"at_{k}") for k in ("q", "qT", "q_rows_lo", "q_rows_hi", "kexp", "sc", "max", "sub", "exp", "tr", "trcp", "pv", "ao", "aot", "aocp", "proj")}
        x2 = {k: sem(f"x2_{k}") for k in ("feat", "fb", "sumA", "sumB", "tanh", "dot", "soft", "exp", "wb", "tw", "d", "bc")}
        once = {k: sem(f"rt_{k}") for k in ("logit", "cur", "e", "w", "gsp", "gtr", "gT")}
        mo = [{k: sem(f"m{m.layer}_{k}") for k in ["g_full", "gcp", "hid", "act", "hi", "h_ready", "h_used", "gate", "acc", "whu", "whd", "wlu", "wld"]
              + ["mul"] * m.gated + ["xn"] * (m.layer == 3)} for m in MOES]
        w_in = [[sem(f"w{m.layer}_in{u}") for u in range(m.unroll)] for m in MOES]
        s_out = sem("s_out")

        def route_view(name, width):
            return rt[name][:, 0:TILES * width].rearrange("p (c e) -> p c e", e=width)

        def linker(eng, s):
            count = [0]

            def link(ins):
                count[0] += 1
                ins.then_inc(s, 1)
                eng.wait_ge(s, count[0])
            return link

        def half(t):
            return slice(t * HALF, (t + 1) * HALF)

        def gate_parts(m, eng, link):
            E = m.routed
            w = route_view("w", E)
            part = [gsp[:, :, r * E:(r + 1) * E] for r in range(3)]
            eng.wait_ge(once["w"], m.layer + 1)
            link(eng.tensor_copy(part[0], w))
            link(eng.tensor_tensor(w, w, part[0], ALU.subtract))
            link(eng.tensor_copy(part[1], w))
            link(eng.tensor_tensor(w, w, part[1], ALU.subtract))
            eng.tensor_copy(part[2], w).then_inc(once["gsp"], 1)

        POOL_SUMS = [g for g in range(2 * B) if (g % 3 == 2 if g < 12 else g % 2 == 1)]

        def sum_of(g):
            b, f = g // 2, (g // 2) * S + 32 * (g % 2)
            return (sums[:, g % 3].rearrange("p (f s) -> p f s", s=S), bcast(xc[:, f:f + 32], 2, S), bcast(txt[:, b * S:(b + 1) * S], 1, 32))

        block = ctx.enter_context(nc.Block())

        @block.sync
        def _(sp):
            sp.dma_start(x[:, :], a["xT"]).then_inc(in_x, 16)
            sp.dma_start(packed["p_first"][:, :], a["p_first"]).then_inc(in_pack["p_first"], 16)
            sp.dma_start(ctxT[:, :], a["ctxT"]).then_inc(in_ctx, 16)
            sp.dma_start(packed["p_attn1"][:, :], a["p_attn1"]).then_inc(in_pack["p_attn1"], 16)

            sp.dma_start(packed["p_rest"][:, :], a["p_rest"]).then_inc(in_pack["p_rest"], 16)

            def load(m, u, e):
                dst = w_f32[:, u * m.width:(u + 1) * m.width]
                src = a[f"w{m.layer}"][bass.ds(e, 1)].rearrange("e p w -> (e p) w")
                sp.dma_start(dst, src).then_inc(w_in[m.layer][u], 16)

            for m in MOES:
                if m.layer:
                    sp.wait_ge(mo[m.layer - 1]["wld"], MOES[m.layer - 1].experts)
                for u in range(m.unroll):
                    load(m, u, u)
                if m.layer == 0:
                    sp.dma_start(packed["p_bf16"][:, :].bitcast(mybir.dt.uint16), a["p_bf16"]).then_inc(in_pack["p_bf16"], 16)
                    sp.dma_start(qmask[:, :], a["mask_rows"]).then_inc(in_pack["mask"], 16)

                def body(it):
                    for u in range(m.unroll):
                        if not isinstance(it, int) or (it + 1) * m.unroll + u < m.experts:
                            sp.wait_ge(mo[m.layer]["wld"], it * m.unroll + u + 1)
                            load(m, u, (it + 1) * m.unroll + u)
                m.run(sp, body)

            for t in range(2):
                sp.wait_ge(x_done[t], 8)
                sp.dma_start(out[:, half(t)], x[:, half(t)]).then_inc(s_out, 16)
            sp.wait_ge(s_out, 32)

        @block.tensor
        def _(pe):
            def keep_busy(count, bank):
                for _ in range(count):
                    pe.matmul(ps[:, bank], ident16, sel[8].rearrange("p e c -> p (e c)")[:, 0:HALF], start=True, stop=True)

            def norm_mean(j, t):
                if j:
                    pe.wait_ge(x_done[t], j)
                pe.matmul(ps[:, t], cen_w, x[:, half(t)], start=True, stop=True).then_inc(ln["mean"], 1)

            def norm_var(j, t):
                pe.wait_ge(ln["sq"], 2 * j + t + 1)
                for i in range(HT):
                    c = t * HT + i
                    mm = pe.matmul(ps[:, 2 + t, i:i + 1], sq[:, c * P:(c + 1) * P], var_w[:, :], start=True, stop=True)
                mm.then_inc(ln["var"], 1)

            def norm_spread(j, t):
                pe.wait_ge(ln["diag"], 2 * j + t + 1)
                pe.matmul(ps[:, 4 + t], ones_w[:, :], diag[:, half(t)], start=True, stop=True).then_inc(ln["bc"], 1)

            def logits(m, t):
                E = m.routed
                pe.wait_ge(ln["n"], 2 * (2 * m.layer + 1) + t + 1)
                for c in range(t * HT, (t + 1) * HT):
                    mm = pe.matmul(ps[:, 6, c * E:(c + 1) * E], n[:, c * P:(c + 1) * P], wg[m.layer], start=True, stop=True)
                mm.then_inc(once["logit"], 1)

            def norm(j, between=None):
                if j >= 2:
                    keep_busy(2, 3)
                for t in range(2):
                    norm_mean(j, t)
                for t in range(2):
                    norm_var(j, t)
                if between:
                    between()
                elif j >= 2:
                    keep_busy(6, 7)
                for t in range(2):
                    norm_spread(j, t)
                pe.wait_ge(ln["xc"], 2 * j + 2)

            def norm_rest(j):
                keep_busy(2, 3)
                norm_mean(j, 1)
                keep_busy(3, 3)
                if j != 5:
                    norm_spread(j, 0)
                norm_var(j, 1)
                logits(MOES[j // 2], 0)
                keep_busy(4, 7)
                norm_spread(j, 1)
                pe.wait_ge(ln["xc"], 2 * j + 2)

            def prepare_keys(i, t):
                w, bank = (wqk1, wqk3)[i], KBANK[i][t]
                pe.matmul(ps[:, bank], w[:, 2], ctxT[:, half(t)], start=True, stop=True)
                pe.matmul(ps[:, bank + 1], w[:, 3], ctxT[:, half(t)], start=True, stop=True).then_inc(pre["proj"], 1)

            def prepare_values(i, q, part=None):
                w, r = (wqk1, wqk3)[i], 4 * i + q
                if q >= 2 and not part:
                    pe.wait_ge(pre["vcp"], r - 1)
                for b in range(4 * q + 2 * (part or 0), 4 * q + (2 if part == 0 else 4)):
                    for h2 in range(2):
                        mm = pe.matmul(ps[h2 * S:(h2 + 1) * S, VBANK[i] + q % 2, (b % 4) * P:(b % 4 + 1) * P],
                                       ctxT[:, b * S:(b + 1) * S], w[:, 4], start=True, stop=True)
                if part != 0:
                    mm.then_inc(pre["v"], 1)

            def prepare_text():
                for t in range(2):
                    pe.matmul(ps[:, 6 + t], l2w[:, 0], ctxT[:, half(t)], start=True, stop=True).then_inc(pre["txt"], 1)

            def prepare_weighted(r, part):
                for b in range(B // 2 * part, B // 2 * (part + 1)):
                    mm = pe.matmul(ps[:, 7, r * S:(r + 1) * S], l2uvpad[:, r, 30 - 2 * b:30 - 2 * b + P], ctxT[:, b * S:(b + 1) * S],
                                   start=(b == 0), stop=(b == B - 1))
                if part:
                    mm.then_inc(pre["uv"], 1)

            def attention(i):
                w = (wqk1, wqk3)[i]
                for t in range(2):
                    pe.wait_ge(ln["n"], 2 * (2, 6)[i] + t + 1)
                    if t == 1:
                        pe.wait_ge(ln["n"], 2 * (2, 6)[i] + 2)
                    pe.matmul(ps[:, 4 * t], w[:, 0], n[:, half(t)], start=True, stop=True)
                    pe.matmul(ps[:, 4 * t + 1], w[:, 1], n[:, half(t)], start=True, stop=True).then_inc(at["q"], 1)
                if i == 0:
                    prepare_values(0, 2)
                    prepare_values(0, 3)
                base = PAIRS * i

                def scores(p):
                    g = base + p
                    pe.wait_ge(at["q_rows_lo"], 2 * i + p // HT + 1)
                    pe.wait_ge(at["q_rows_hi"], 2 * i + p // HT + 1)
                    if p >= 2:
                        pe.wait_ge(at["sub"], g - 1)
                    pe.wait_ge(at["kexp"], g // 2 + 1)
                    for r in range(4):
                        cols = slice(256 * (r % 2), 256 * (r % 2) + 256)
                        for b in range(2):
                            c = p * P + b * S
                            mm = pe.matmul(ps[b * S:(b + 1) * S, SCB[p % 2] + r // 2, cols], q_rows[:, r, c:c + S],
                                           kexp[:, 2 * p + b], start=True, stop=True)
                    mm.then_inc(at["sc"], 1)

                def turn(p):
                    g = base + p
                    pe.wait_ge(at["exp"], g + 1)
                    if p == 0:
                        pe.wait_ge(at["qT"], 2 * i + 2)
                    for hp in range(8):
                        if hp % 4 == 0 and g:
                            pe.wait_ge(at["trcp"], 2 * g - 1 + hp // 4)
                        mm = pe.transpose(ps[:, 4 + hp // 4, (hp % 4) * P:(hp % 4 + 1) * P],
                                          p_exp[:, p % 2, hp * P:(hp + 1) * P], ident)
                        if hp % 4 == 3:
                            mm.then_inc(at["tr"], 1)

                def values(p):
                    g = base + p
                    if g:
                        pe.wait_ge(at["ao"], g)
                    for hp in range(8):
                        if hp % 4 == 0:
                            pe.wait_ge(at["trcp"], 2 * g + 1 + hp // 4)
                        for b in range(2):
                            mm = pe.matmul(ps[b * S:(b + 1) * S, 6, hp * 18:(hp + 1) * 18],
                                           p_tr[:, p % 2, hp * P + b * S:hp * P + (b + 1) * S],
                                           vblk[i][:, 2 * p + b, hp], start=True, stop=True)
                    mm.then_inc(at["pv"], 1)

                def turn_out(p):
                    g = base + p
                    pe.wait_ge(at["ao"], g + 1)
                    if g:
                        pe.wait_ge(at["aocp"], g)
                    if p == HT:
                        pe.wait_ge(x_done[0], (3, 7)[i])
                    pe.transpose(ps[:, 7, 0:P], ao[:, p % 2], ident).then_inc(at["aot"], 1)

                def project(t):
                    pe.wait_ge(at["aocp"], base + HT * (t + 1))
                    pe.wait_ge(pre["wo"], i + 1)
                    pe.matmul(ps[:, 7], w[:, 5], aoT[:, half(t)], start=True, stop=True).then_inc(at["proj"], 1)

                scores(0)
                scores(1)
                for p in range(PAIRS):
                    turn(p)
                    if p + 2 < PAIRS:
                        scores(p + 2)
                    if p == PAIRS - 1:
                        norm_mean((3, 7)[i], 0)
                    if p == HT + 2:
                        turn_out(HT)
                    values(p)
                    if p == HT + 1:
                        project(0)
                    elif p:
                        turn_out(p - 1)
                norm_var((3, 7)[i], 0)
                turn_out(PAIRS - 1)
                project(1)

            def weights_out(t, r):
                pe.wait_ge(x2["d"], 2 * t + r + 1)
                pe.matmul(ps[:, (0, 6)[t] + r], ones_w[:, :], (diag, sq)[r][:, half(t)], start=True, stop=True).then_inc(x2["bc"], 1)

            def pair_sums():
                pe.wait_ge(pre["txtcp"], 2)
                for t in range(2):
                    pe.wait_ge(ln["n"], 2 * 4 + t + 1)
                    pe.matmul(ps[:, t], l2w[:, 1], n[:, half(t)], start=True, stop=True).then_inc(x2["feat"], 1)
                for g in range(2 * B):
                    if g in (4, 5):
                        prepare_keys(1, g - 4)
                    if 8 <= g < 16:
                        if g == 8:
                            pe.wait_ge(pre["k"], 4)
                        prepare_values(1, (g - 8) // 2, g % 2)
                    if 16 <= g < 20:
                        prepare_weighted((g - 16) // 2, g % 2)
                    if g == 29:
                        pe.wait_ge(pre["vcp"], 8)
                    if g in (29, 30):
                        weights_out(0, g - 29)
                    pe.wait_ge(x2["tanh"], g + 1)
                    for q in range(4):
                        mm = pe.matmul(ps[32 * q:32 * q + 32, DOTS[g // B]], l2pad[:, 31 - g:63 - g],
                                       tanhs[:, g % 3, q * 512:(q + 1) * 512], start=(g % B == 0), stop=(g % B == B - 1))
                    mm.then_inc(x2["dot"], 1)
                norm_mean(5, 0)
                norm_var(5, 0)
                keep_busy(8, 3)
                norm_spread(5, 0)
                keep_busy(4, 3)
                for r in range(2):
                    weights_out(1, r)

            def moe(m):
                s, L = mo[m.layer], m.layer
                j, N, U, E = 2 * L + 1, m.n, m.unroll, m.routed

                def wap(w, u, lo, size, rows=P):
                    return w[0:rows, u * m.width + lo:u * m.width + lo + size]

                def products(dst, u, lo, size, rows, hi, low, first=True, last=True):
                    passes = [(w_hi, hi), (w_hi, low), (w_lo, hi)]
                    for c, (wt, mv) in enumerate(passes):
                        for i in range(len(dst)):
                            mm = pe.matmul(dst[i], wap(wt, u, lo, size, rows), mv[i],
                                           start=(first and c == 0), stop=(last and c == 2))
                    return mm

                def up(it, k):
                    u, sl, step = (k // N) % U, k % 2, it * m.steps + k
                    if k % N == 0:
                        pe.wait_ge(s["wlu"], it * U + k // N + 1)
                    if not (isinstance(it, int) and step < 2):
                        pe.wait_ge(s["mul" if m.gated else "act"], step - 1)
                    if not m.gated:
                        f, size = m.chunks[k % N]
                        mm = products([ps[0:size, 2 * sl + t] for t in range(2)], u, f, size, P,
                                      [n_hi[:, half(t)] for t in range(2)], [n_lo[:, half(t)] for t in range(2)])
                    else:
                        f, size = m.chunks[(k % N) // 2]
                        t = k % 2
                        for i in range(2):
                            mm = products([ps[0:size, 2 * sl + i]], u, i * m.hidden + f, size, P, [n_hi[:, half(t)]], [n_lo[:, half(t)]])
                    mm.then_inc(s["hid"], 1)

                def down(it, k):
                    u, sl, step = (k // N) % U, k % 2, it * m.steps + k
                    pe.wait_ge(s["h_ready"], step + 1)
                    if k % N == 0:
                        pe.wait_ge(s["wld"], it * U + k // N + 1)
                    if k % N < m.gates and not (isinstance(it, int) and step < m.gates):
                        pe.wait_ge(s["gate"], m.gates * (it * U + k // N - 1) + k % N + 1)
                    ci = (k % N) // 2 if m.gated else k % N
                    f, size = m.chunks[ci]
                    ts = [k % 2] if m.gated else [0, 1]
                    hv = [[h[0:size, sl, 0:HALF] if m.gated else h[0:size, sl, half(t)] for t in ts] for h in (h_hi, h_lo)]
                    ends = {"first": ci == 0, "last": ci == len(m.chunks) - 1}
                    if isinstance(it, int) and step == m.total - 1 and not m.gated:
                        for t in ts:
                            products([ps[:, 4 + t]], u, m.up + ci * P, P, size, [hv[0][t]], [hv[1][t]], **ends).then_inc(s["h_used"], 1)
                    else:
                        products([ps[:, 4 + t] for t in ts], u, m.up + ci * P, P, size, hv[0], hv[1], **ends).then_inc(s["h_used"], 1)

                def spread(it, k):
                    e = it * U + k // N
                    if isinstance(it, int) and e == 0:
                        pe.wait_ge(once["gT"], m.layer + 1)
                    else:
                        pe.wait_ge(s["gcp"], e)
                    for t in range(2):
                        mm = pe.matmul(ps[:, 6 + t], sel[E][:, bass.ds(e, 1)].rearrange("p a c -> p (a c)"), gT[:, half(t)], start=True, stop=True)
                    mm.then_inc(s["g_full"], 1)

                if L == 0:
                    logits(m, 0)
                if m.gated:
                    pe.wait_ge(ln["lo"], 2 * L + 1)
                    up(0, 0)
                logits(m, 1)
                pe.wait_ge(ln["lo"], 2 * L + 2)
                if not m.gated:
                    up(0, 0)
                up(0, 1)

                def turn_gates():
                    if L == 0:
                        pe.wait_ge(in_pack["p_bf16"], 16)
                    pe.wait_ge(once["gsp"], L + 1)
                    for c in range(TILES):
                        mm = pe.transpose(ps[0:3 * E, 7].bitcast(BF16)[:, c * P:(c + 1) * P], gsp[:, c, 0:3 * E], ident16)
                    mm.then_inc(once["gtr"], 1)

                def body(it):
                    for k in range(m.steps):
                        if isinstance(it, int) and it * m.steps + k >= m.total:
                            break
                        first = isinstance(it, int) and it == 0
                        if first and L == 2 and k == 0:
                            turn_gates()
                        if not isinstance(it, int) or it * m.steps + k + 2 < m.total:
                            up(it, k + 2)
                        if first and L != 2 and k == N - 1:
                            turn_gates()
                        if k % N == N - 2 and not (isinstance(it, int) and not (L != 2) <= it * U + k // N < E):
                            spread(it, k)
                        down(it, k)
                        if first and L != 2 and k == N - 1:
                            spread(it, k)
                m.run(pe, body)

            pe.wait_ge(in_x, 16)
            pe.wait_ge(in_pack["p_first"], 16)
            pe.wait_ge(consts, 1)
            norm(0)
            pe.wait_ge(in_ctx, 16)
            pe.wait_ge(in_pack["p_attn1"], 16)
            prepare_keys(0, 0)

            def second_keys():
                pe.wait_ge(pre["k"], 1)
                prepare_keys(0, 1)

            norm(1, second_keys)
            pe.wait_ge(pre["k"], 2)
            moe(MOES[0])
            norm(2, lambda: (prepare_values(0, 0), prepare_values(0, 1)))
            attention(0)
            norm_rest(3)
            moe(MOES[1])
            norm(4, prepare_text)
            pair_sums()
            norm_rest(5)
            moe(MOES[2])
            norm(6)
            attention(1)
            norm_rest(7)
            moe(MOES[3])

        @block.scalar
        def _(act):

            def norm_square(j, t):
                act.wait_ge(ln["mean"], 2 * j + t + 1)
                act.activation(sq[:, half(t)], ps[:, t], ACT.Square).then_inc(ln["sq"], 1)

            def norm_copy(j, t):
                act.copy(xc[:, half(t)], ps[:, t]).then_inc(ln["xc"], 1)

            def norm_high(j, t):
                act.wait_ge(ln["n"], 2 * j + t + 1)
                act.copy(n_hi[:, half(t)], n[:, half(t)]).then_inc(ln["hi"], 1)

            def norm(j):
                for t in range(2):
                    norm_square(j, t)
                for t in range(2):
                    norm_copy(j, t)
                if j % 2:
                    for t in range(2):
                        norm_high(j, t)

            def norm_rest(j):
                norm_square(j, 1)
                norm_copy(j, 1)
                for t in range(2):
                    norm_high(j, t)

            def split_hi(m, it, k):
                s, U = mo[m.layer], m.unroll
                u, e = k % U, it * U + k
                act.wait_ge(w_in[m.layer][u], 16 * (it + k // U + 1))
                if not (isinstance(it, int) and e < U):
                    act.wait_ge(s["h_used"], m.n * (e - U + 1))
                o = u * m.width
                act.copy(w_hi[:, o:o + m.up], w_f32[:, o:o + m.up]).then_inc(s["whu"], 1)
                if m.biases:
                    act.copy(w_hi[:, o + m.up:o + m.split], w_f32[:, o + m.up:o + m.split])
                    if not (isinstance(it, int) and e < U):
                        act.wait_ge(s["gate"], m.gates * (e - U + 1))
                    act.copy(w_bias[:, u, 0:m.biases], w_f32[:, o + m.split:o + m.width]).then_inc(s["whd"], 1)
                else:
                    act.copy(w_hi[:, o + m.up:o + m.split], w_f32[:, o + m.up:o + m.split]).then_inc(s["whd"], 1)

            def first_weights(m):
                if m.layer:
                    act.wait_ge(mo[m.layer - 1]["h_used"], MOES[m.layer - 1].down_total)
                for u in range(m.unroll):
                    split_hi(m, 0, u)

            def prepare_text():
                for t in range(2):
                    act.wait_ge(pre["txt"], t + 1)
                    act.copy(txt[:, half(t)], ps[:, 6 + t]).then_inc(pre["txtcp"], 1)

            def attention(i):
                base = PAIRS * i

                def out_copy(p):
                    act.wait_ge(at["aot"], base + p + 1)
                    if i == 0:
                        ins = act.activation(aoT[:, p * P:(p + 1) * P], ps[:, 7, 0:P], ACT.Identity, bias=abias[:, 6:7])
                    else:
                        ins = act.copy(aoT[:, p * P:(p + 1) * P], ps[:, 7, 0:P])
                    ins.then_inc(at["aocp"], 1)

                for t in range(2):
                    act.wait_ge(at["qT"], 2 * i + t + 1)
                    for r in range(2, 4):
                        ins = act.activation(q_rows[:, r, half(t)], qT[:, half(t)], ACT.Copy, scale=rmask[:, r:r + 1])
                    ins.then_inc(at["q_rows_hi"], 1)
                for p in range(PAIRS):
                    act.wait_ge(at["sub"], base + p + 1)
                    if base + p >= 2:
                        act.wait_ge(at["tr"], 2 * (base + p) - 2)
                    act.activation(p_exp[:, p % 2], s_sub[:, p % 2], ACT.Exp).then_inc(at["exp"], 1)
                    if p >= 2:
                        out_copy(p - 2)
                    for hh in range(2):
                        act.wait_ge(at["tr"], 2 * (base + p) + hh + 1)
                        if base + p >= 2:
                            act.wait_ge(at["pv"], base + p - 1)
                        act.copy(p_tr[:, p % 2, half(hh)], ps[:, 4 + hh]).then_inc(at["trcp"], 1)
                    if p == PAIRS - 1:
                        norm_square((3, 7)[i], 0)
                out_copy(PAIRS - 2)
                norm_copy((3, 7)[i], 0)
                out_copy(PAIRS - 1)

            def softmax_exp(t):
                act.wait_ge(x2["soft"], t + 1)
                act.activation(h_act[:, 0, 0:512], h_act[:, 1, 0:512], ACT.Exp).then_inc(x2["exp"], 1)

            def weights_tanh(t):
                act.wait_ge(x2["wb"], t + 1)
                for r in range(2):
                    act.activation(st2[:, 4 + r], st2[:, 2 + r], ACT.Tanh, bias=l2b[:, 1 + r:2 + r]).then_inc(x2["tw"], 1)

            def pair_sums():
                for g in range(2 * B):
                    if g == 20:
                        softmax_exp(0)
                    if g == 26:
                        weights_tanh(0)
                    of_pool = len([p for p in POOL_SUMS if p <= g])
                    if g in POOL_SUMS:
                        act.wait_ge(x2["sumB"], of_pool)
                    else:
                        act.wait_ge(x2["sumA"], g + 1 - of_pool)
                    if g >= 3:
                        act.wait_ge(x2["dot"], g - 2)
                    act.activation(tanhs[:, g % 3], sums[:, g % 3], ACT.Tanh).then_inc(x2["tanh"], 1)
                norm_square(5, 0)
                norm_copy(5, 0)
                softmax_exp(1)
                weights_tanh(1)

            def moe(m):
                s, L = mo[m.layer], m.layer
                N, U, E = m.n, m.unroll, m.routed
                if L == 2:
                    act.wait_ge(once["logit"], 2 * (m.layer + 1))
                    act.activation(route_view("e", E), ps[:, 6, 0:TILES * E].rearrange("p (c e) -> p c e", e=E), ACT.Sigmoid).then_inc(once["e"], 1)
                else:
                    act.wait_ge(once["cur"], (1, 2, 0, 3)[m.layer])
                    act.activation(route_view("e", E), route_view("cur", E), ACT.Exp).then_inc(once["e"], 1)

                def hidden(it, k):
                    step, sl = it * m.steps + k, k % 2
                    act.wait_ge(s["hid"], step + 1)
                    if m.biases and k % N == 0:
                        act.wait_ge(s["whd"], it * U + k // N + 1)
                    if not (isinstance(it, int) and step < 2):
                        act.wait_ge(s["h_ready"], step - 1)
                    if m.gated:
                        size = m.chunks[(k % N) // 2][1]
                        kw = {"bias": w_bias[:, (k // N) % U, 0:1]} if L == 2 else {}
                        act.activation(h_act[0:size, sl, 0:HALF], ps[0:size, 2 * sl], ACT.Silu, **kw).then_inc(s["act"], 1)
                    else:
                        kw = {"bias": w_bias[:, (k // N) % U, k % N:k % N + 1]} if L == 0 else {}
                        act.activation(h_act[:, sl], ps[:, 2 * sl:2 * sl + 2].rearrange("p a c -> p (a c)"), ACT.Gelu, **kw).then_inc(s["act"], 1)

                def high(it, k):
                    step, sl, size = it * m.steps + k, k % 2, m.chunks[(k % N) // 2][1]
                    act.wait_ge(s["mul"], step + 1)
                    if not (isinstance(it, int) and step < 2):
                        act.wait_ge(s["h_used"], step - 1)
                    act.copy(h_hi[0:size, sl, 0:HALF], h_act[0:size, sl, 0:HALF]).then_inc(s["hi"], 1)

                def gates(it, k):
                    e = it * U + k
                    act.wait_ge(s["g_full"], e + 1)
                    if not (isinstance(it, int) and e < 2):
                        act.wait_ge(s["gate"], m.gates * (e - 1))
                    act.copy(g_sb[:, k % 2], ps[:, 6:8].rearrange("p a c -> p (a c)")).then_inc(s["gcp"], 1)

                def copy_gates():
                    act.wait_ge(once["gtr"], L + 1)
                    act.wait_ge(zeros, 1)
                    act.copy(gT[0:3 * E, :], ps[0:3 * E, 7].bitcast(BF16)).then_inc(once["gT"], 1)

                lag = 4 if m.act_high else 3

                def after(it, k):
                    if isinstance(it, int) and it == 0 and k == N and L != 2:
                        copy_gates()
                    e = (k - 1) // N if (k - 1) % N == N - 1 else None
                    if e is not None and not (isinstance(it, int) and not 0 <= it * U + e < E):
                        gates(it, e)
                    e = (k - lag) // N if (k - lag) % N == N - 1 else None
                    if e is not None and not (isinstance(it, int) and not U <= it * U + e + U < m.experts):
                        split_hi(m, it, e + U)

                def body(it):
                    for k in range(m.steps):
                        if isinstance(it, int) and it == 0 and k == 2 and L == 2:
                            copy_gates()
                        if not isinstance(it, int) or it * m.steps + k < m.total:
                            hidden(it, k)
                            if m.act_high and not (isinstance(it, int) and it == 0 and k == 0):
                                high(it, k - 1)
                        after(it, k)
                m.run(act, body)
                for k in range(1):
                    if m.experts % U == 0:
                        after(m.bodies, k)
                if m.act_high:
                    high(m.bodies, -1)

            act.wait_ge(in_pack["p_first"], 16)
            act.activation(tg, tg, ACT.Tanh).then_inc(tg_ready, 1)
            act.wait_ge(in_ctx, 16)
            act.activation(diag[:, :], ctxT[:, :], ACT.Square).then_inc(pre["kv"], 1)
            norm(0)
            first_weights(MOES[0])
            norm(1)
            moe(MOES[0])
            norm(2)
            first_weights(MOES[1])
            attention(0)
            norm_rest(3)
            moe(MOES[1])
            norm(4)
            prepare_text()
            first_weights(MOES[2])
            pair_sums()
            norm_rest(5)
            moe(MOES[2])
            norm(6)
            first_weights(MOES[3])
            attention(1)
            norm_rest(7)
            moe(MOES[3])

        @block.vector
        def _(dve):
            link = linker(dve, dve_link)

            def norm_eps(j, t):
                dve.wait_ge(ln["var"], 2 * j + t + 1)
                dve.tensor_scalar(var_eps[:, t * HT:(t + 1) * HT], ps[:, 2 + t, 0:HT], EPS, None, ALU.add).then_inc(ln["eps"], 1)

            def norm_diag(j, t):
                dve.wait_ge(ln["rstd"], 2 * j + t + 1)
                dve.tensor_tensor(diag[:, half(t)].rearrange("p (c k) -> p c k", k=P), bcast(ident, 1, HT),
                                  bcast(rstd[:, t * HT:(t + 1) * HT], 2, P), ALU.mult).then_inc(ln["diag"], 1)

            def norm_out(j, t):
                dve.wait_ge(ln["bc"], 2 * j + t + 1)
                dve.wait_ge(ln["xc"], 2 * j + t + 1)
                dve.tensor_tensor(n[:, half(t)], xc[:, half(t)], ps[:, 4 + t], ALU.mult).then_inc(ln["n"], 1)

            def norm_low(j, t):
                dve.wait_ge(ln["hi"], 2 * (j // 2) + t + 1)
                dve.tensor_tensor(n_lo[:, half(t)], n[:, half(t)], n_hi[:, half(t)].bitcast(F32), ALU.subtract).then_inc(ln["lo"], 1)

            def norm(j, between=None):
                for step in (norm_eps, norm_diag, norm_out) + (norm_low,) * (j % 2):
                    if between and step is norm_out:
                        between()
                    for t in range(2):
                        step(j, t)

            def norm_rest(j):
                if j != 5:
                    norm_diag(j, 0)
                    norm_out(j, 0)
                norm_eps(j, 1)
                norm_low(j, 0)
                norm_diag(j, 1)
                norm_out(j, 1)
                norm_low(j, 1)

            def rotate(dst, t, banks, tab, bias):
                v = dst[:, half(t)].rearrange("p (b s) -> p b s", s=S)
                tmp = y_g[:, t, 0:HALF].rearrange("p (b s) -> p b s", s=S)
                b0 = abias[:, bias:bias + 1] if bias is not None else 0.0
                b1 = abias[:, bias + 1:bias + 2] if bias is not None else 0.0
                dve.scalar_tensor_tensor(v, ps[:, banks].rearrange("p (b s) -> p b s", s=S), b0, bcast(rope[:, tab], 1, 8), ALU.add, ALU.mult)
                link(dve.scalar_tensor_tensor(tmp, ps[:, banks + 1].rearrange("p (b s) -> p b s", s=S), b1, bcast(rope[:, tab + 1], 1, 8), ALU.add, ALU.mult))
                return dve.tensor_tensor(v, v, tmp, ALU.add)

            def prepare_keys(i, t):
                dve.wait_ge(pre["proj"], 2 * i + t + 1)
                rotate(kT[i], t, KBANK[i][t], 2, 2 if i == 0 else None).then_inc(pre["k"], 1)

            def prepare_values(i, q):
                r = 4 * i + q
                dve.wait_ge(pre["v"], r + 1)
                if r == 0:
                    dve.wait_ge(zeros, 1)
                for h2 in range(2):
                    rows = slice(64 * h2, 64 * h2 + 64)
                    src = ps[rows, VBANK[i] + q % 2].rearrange("p (b h c d) -> p (b h) c d", b=4, h=8, c=2)[:, :, h2]
                    dst = vblk[i][rows, 4 * q:4 * q + 4].rearrange("p b h (c d) -> p (b h) c d", c=2)[:, :, h2, 0:8]
                    ins = dve.tensor_copy(dst, src)
                ins.then_inc(pre["vcp"], 1)

            def attention(i):
                base = PAIRS * i
                for t in range(2):
                    dve.wait_ge(at["q"], 2 * i + t + 1)
                    rotate(qT, t, 4 * t, 0, 0 if i == 0 else None).then_inc(at["qT"], 1)
                    dve.wait_ge(at["qT"], 2 * i + t + 1)
                    for r in range(2):
                        ins = dve.tensor_scalar(q_rows[:, r, half(t)], qT[:, half(t)], rmask[:, r:r + 1], None, ALU.mult)
                    ins.then_inc(at["q_rows_lo"], 1)

                def soft(p):
                    g = base + p
                    dve.wait_ge(at["sc"], g + 1)
                    sc = ps[:, SCB[p % 2]:SCB[p % 2] + 2].rearrange("p a (h k) -> p (a h) k", k=S)
                    dve.tensor_reduce(mx[:, p % 2], sc, AX, ALU.max).then_inc(at["max"], 1)
                    dve.wait_ge(at["max"], g + 1)
                    if g >= 2:
                        dve.wait_ge(at["exp"], g - 1)
                    dve.tensor_tensor(s_sub[:, p % 2].rearrange("p (h k) -> p h k", k=S), sc, bcast(mx[:, p % 2], 2, S),
                                      ALU.subtract).then_inc(at["sub"], 1)

                def output(p):
                    g = base + p
                    dve.wait_ge(at["pv"], g + 1)
                    o = ps[:, 6, 0:144].rearrange("p (h c) -> p h c", c=9)
                    link(dve.reciprocal(rsum[:, p % 2], o[:, :, 8]))
                    if g >= 2:
                        dve.wait_ge(at["aot"], g - 1)
                    dve.tensor_tensor(ao[:, p % 2].rearrange("p (h d) -> p h d", d=HD), o[:, :, 0:HD], bcast(rsum[:, p % 2], 2, HD),
                                      ALU.mult).then_inc(at["ao"], 1)

                def update(t):
                    dve.wait_ge(at["proj"], 2 * i + t + 1)
                    bo = abias[:, 5:6] if i == 0 else 0.0
                    dve.scalar_tensor_tensor(x[:, half(t)], ps[:, 7], bo, x[:, half(t)], ALU.add, ALU.add).then_inc(x_done[t], 1)

                if i == 0:
                    prepare_values(0, 2)
                    prepare_values(0, 3)
                soft(0)
                soft(1)
                for p in range(PAIRS):
                    if p + 2 < PAIRS:
                        soft(p + 2)
                    output(p)
                    if p == HT + 1:
                        update(0)
                norm_eps((3, 7)[i], 0)
                update(1)

            raw = h_act[:, 1, 0:512].rearrange("p (f s) -> p f s", s=S)
            e3 = h_act[:, 0, 0:512].rearrange("p (f s) -> p f s", s=S)
            t3 = h_act[:, 1, 512:1024].rearrange("p (f s) -> p f s", s=S)

            def softmax(t):
                dve.wait_ge(x2["dot"], B * (t + 1))
                link(dve.tensor_tensor(raw, ps[:, DOTS[t]].rearrange("p (f s) -> p f s", s=S), bcast(mbias[:, 1], 1, 8), ALU.add))
                link(dve.tensor_reduce(st2[:, 0], raw, AX, ALU.max))
                dve.tensor_tensor(raw, raw, bcast(st2[:, 0], 2, S), ALU.subtract).then_inc(x2["soft"], 1)

            def share(t):
                dve.wait_ge(x2["exp"], t + 1)
                link(dve.tensor_reduce(st2[:, 0], e3, AX, ALU.add))
                link(dve.reciprocal(st2[:, 1], st2[:, 0]))

            def weigh(t, r):
                dve.wait_ge(pre["uvcp"], 1)
                link(dve.tensor_tensor(t3, e3, bcast(uv[:, r], 1, 8), ALU.mult))
                link(dve.tensor_reduce(st2[:, 2 + r], t3, AX, ALU.add))
                if r == 0:
                    return
                for r in range(2):
                    ins = dve.tensor_tensor(st2[:, 2 + r], st2[:, 2 + r], st2[:, 1], ALU.mult)
                ins.then_inc(x2["wb"], 1)

            def scale_rows(t, r):
                dve.wait_ge(x2["tw"], 2 * t + r + 1)
                rows = slice(t * P // 2, (t + 1) * P // 2)
                link(dve.tensor_scalar(st2[:, 2 + r], st2[:, 4 + r], tg[:, 2:3], None, ALU.mult))
                dve.tensor_tensor((diag, sq)[r][:, half(t)].rearrange("p (c f) -> p c f", f=8), bcast(perm[:, rows], 2, 8),
                                  bcast(st2[:, 2 + r], 1, P // 2), ALU.mult).then_inc(x2["d"], 1)

            def update(t):
                dve.wait_ge(x2["bc"], 2 * t + 1)
                link(dve.tensor_tensor(xc[:, half(t)], n[:, half(t)], ps[:, (0, 6)[t]], ALU.mult))
                dve.wait_ge(x2["bc"], 2 * t + 2)
                link(dve.tensor_tensor(xc[:, half(t)], xc[:, half(t)], ps[:, (0, 6)[t] + 1], ALU.add))
                dve.tensor_tensor(x[:, half(t)], x[:, half(t)], xc[:, half(t)], ALU.add).then_inc(x_done[t], 1)

            def pair_sums():
                for t in range(2):
                    dve.wait_ge(x2["feat"], t + 1)
                    dve.tensor_scalar(xc[:, half(t)], ps[:, t], l2b[:, 0:1], None, ALU.add).then_inc(x2["fb"], 1)
                dve.wait_ge(x2["fb"], 2)
                dve.wait_ge(pre["txtcp"], 2)
                for g in range(2 * B):
                    if g in (7, 8):
                        prepare_keys(1, g - 7)
                    if g in (11, 13, 15, 17):
                        prepare_values(1, (g - 11) // 2)
                    if g == 3:
                        dve.tensor_scalar(wqk3[:, 5], wqk3[:, 5], tg[:, 3:4], None, ALU.mult).then_inc(pre["wo"], 1)
                        dve.wait_ge(in_pack["mask"], 16)
                        link(dve.tensor_scalar(mbias[:, 0], qmask[:, :], -1.0, 1.0, ALU.mult, ALU.add))
                        link(dve.tensor_scalar(mbias[:, 1], mbias[:, 0], NEG, None, ALU.mult))
                    if g == 22:
                        dve.wait_ge(pre["uv"], 2)
                        dve.tensor_copy(uv[:, :, :], ps[:, 7, 0:2 * S].rearrange("p (r s) -> p r s", r=2)).then_inc(pre["uvcp"], 1)
                    if g == 19:
                        softmax(0)
                    if g == 22:
                        share(0)
                    if g in (23, 24):
                        weigh(0, g - 23)
                    if g in (27, 28):
                        scale_rows(0, g - 27)
                    if g == 31:
                        update(0)
                    if g in POOL_SUMS:
                        continue
                    if g >= 3:
                        dve.wait_ge(x2["tanh"], g - 2)
                    dve.tensor_tensor(*sum_of(g), ALU.add).then_inc(x2["sumA"], 1)
                softmax(1)
                norm_eps(5, 0)
                share(1)
                for r in range(2):
                    weigh(1, r)
                norm_diag(5, 0)
                for r in range(2):
                    scale_rows(1, r)
                norm_out(5, 0)
                update(1)

            def top(cur, count, width, chosen):
                top8, need = route_view("top8", 8), rt_m[:, 1, 0:TILES]
                above, equal, rank = (route_view(k, width) for k in ("above", "equal", "rank"))
                for c in range(TILES):
                    ins = dve.max(top8[:, c], cur[:, c])
                link(ins)
                least = bcast(top8[:, :, count - 1], 2, width)
                dve.tensor_tensor(equal, cur, least, ALU.is_equal)
                link(dve.tensor_tensor(above, cur, least, ALU.is_gt))
                dve.tensor_reduce(need, above, AX, ALU.add)
                link(dve.tensor_tensor_scan(rt["rank"][:, 0:TILES * width], starts[width][:, :], rt["equal"][:, 0:TILES * width], 0.0, ALU.mult, ALU.add))
                link(dve.tensor_tensor(rank, rank, bcast(need, 2, width), ALU.add))
                link(dve.scalar_tensor_tensor(equal, rank, float(count), equal, ALU.is_le, ALU.mult))
                link(dve.tensor_tensor(chosen, above, equal, ALU.add))

            def route(m):
                s, L, E = mo[m.layer], m.layer, m.routed
                e, cur, w, chosen = (route_view(k, E) for k in ("e", "cur", "w", "chosen"))
                if L == 2:
                    dve.wait_ge(once["e"], m.layer + 1)
                    e4 = e.rearrange("p c (g k) -> p c g k", g=4)
                    cur4 = cur.rearrange("p c (g k) -> p c g k", g=4)
                    best, rank = rt_m[:, 2, 0:4 * TILES], rt_m[:, 3, 0:4 * TILES]
                    best, rank = (v.rearrange("p (c g) -> p c g", g=4) for v in (best, rank))
                    link(dve.tensor_reduce(best, e4, AX, ALU.max))
                    higher, same = (route_view(k, 16).rearrange("p c (g k) -> p c g k", g=4) for k in ("above", "equal"))
                    mine, others = bcast(best, 3, 4), bcast(best, 2, 4)
                    dve.tensor_tensor(higher, others, mine, ALU.is_gt)
                    link(dve.tensor_tensor(same, others, mine, ALU.is_equal))
                    link(dve.tensor_tensor(same, same, bcast(packed["before"], 1, TILES), ALU.mult))
                    link(dve.tensor_tensor(same, same, higher, ALU.add))
                    link(dve.tensor_reduce(rank, same, AX, ALU.add))
                    link(dve.tensor_scalar(rank, rank, 1.5, -4.0, ALU.is_gt, ALU.mult))
                    link(dve.tensor_tensor(cur4, e4, bcast(rank, 3, 4), ALU.add))
                    top(cur, 4, 16, chosen)
                else:
                    top(cur, m.topk, E, chosen)

            def weigh_chosen(m):
                s, L, E = mo[m.layer], m.layer, m.routed
                e, w, chosen = (route_view(k, E) for k in ("e", "w", "chosen"))
                dve.wait_ge(once["e"], m.layer + 1)
                total, inv = rt_m[:, 0, 0:TILES], rt_m[:, 1, 0:TILES]
                link(dve.tensor_tensor(w, e, chosen, ALU.mult))
                link(dve.tensor_reduce(total, e if L == 3 else w, AX, ALU.add))
                link(dve.reciprocal(inv, total))
                link(dve.tensor_scalar(inv, inv, tg[:, 4 + L:5 + L], 2.5 if L == 2 else 1.0, ALU.mult, ALU.mult))
                dve.tensor_tensor(w, w, bcast(inv, 2, E), ALU.mult).then_inc(once["w"], 1)

            def moe(m):
                s, L = mo[m.layer], m.layer
                N, U, E = m.n, m.unroll, m.routed
                def split(it, k, between=None):
                    step, sl = it * m.steps + k, k % 2
                    size, cols = (m.chunks[(k % N) // 2][1], HALF) if m.gated else (P, T)
                    ha, hi, lo = (h[0:size, sl, 0:cols] for h in (h_act, h_hi, h_lo))
                    dve.wait_ge(s["act"], step + 1)
                    if m.gated:
                        b3 = w_bias[:, k // N, 1:2] if L == 2 else 0.0
                        dve.scalar_tensor_tensor(ha, ps[0:size, 2 * sl + 1], b3, ha, ALU.add, ALU.mult).then_inc(s["mul"], 1)
                        if between:
                            between()
                        if not m.act_high:
                            dve.wait_ge(s["mul"], step + 1)
                    if not m.act_high:
                        if not (isinstance(it, int) and step < 2):
                            dve.wait_ge(s["h_used"], step - 1)
                        dve.tensor_copy(hi, ha).then_inc(s["hi"], 1)
                    dve.wait_ge(s["hi"], step + 1)
                    dve.tensor_tensor(lo, ha, hi.bitcast(F32), ALU.subtract).then_inc(s["h_ready"], 1)

                lg = ps[:, 6, 0:TILES * E].rearrange("p (c e) -> p c e", e=E)
                cur = route_view("cur", E)
                if L == 0:
                    dve.wait_ge(once["logit"], 2 * (m.layer + 1))
                    link(dve.tensor_tensor(route_view("lg", E), lg, bcast(gb0, 1, TILES), ALU.add))
                    lg = route_view("lg", E)
                if L != 2:
                    dve.wait_ge(once["logit"], 2 * (m.layer + 1))
                    link(dve.tensor_reduce(rt_m[:, 3, 0:TILES], lg, AX, ALU.max))
                    dve.tensor_tensor(cur, lg, bcast(rt_m[:, 3, 0:TILES], 2, E), ALU.subtract).then_inc(once["cur"], 1)
                if L == 2:
                    route(m)
                    weigh_chosen(m)
                    gate_parts(m, dve, link)
                split(0, 0)
                split(0, 1)

                def gate(it, k, t=None):
                    e = it * U + k
                    toks = slice(0, T) if t is None else half(t)
                    yy = ps[:, 4:6].rearrange("p a c -> p (a c)") if t is None else ps[:, 4 + t]
                    dst, g = y_g[:, k % 2, toks], g_sb[:, k % 2, toks]
                    dve.wait_ge(s["h_used"], N * (e + 1) if t is None else N * e + N - 1 + t)
                    if not t:
                        if not (isinstance(it, int) and e < 2):
                            dve.wait_ge(s["acc"], e - 1)
                        dve.wait_ge(s["gcp"], e + 1)
                    if m.biases:
                        dve.scalar_tensor_tensor(dst, yy, w_bias[:, k % U, m.biases - 1:m.biases], g, ALU.add, ALU.mult).then_inc(s["gate"], 1)
                    else:
                        dve.tensor_tensor(dst, yy, g, ALU.mult).then_inc(s["gate"], 1)

                def body(it):
                    for k in range(m.steps):
                        step = it * m.steps + k
                        if isinstance(it, int) and step >= m.total:
                            break
                        half_due = m.gated and (k - 2) % N >= N - 2 and not (isinstance(it, int) and not 2 <= step < m.total - N + 2)
                        if half_due:
                            split(it, k, lambda: gate(it, (k - 2) // N, (k - 2) % 2))
                        elif not (isinstance(it, int) and step < 2):
                            split(it, k)
                        if isinstance(it, int) and L != 2:
                            if step == N - 3:
                                dve.wait_ge(once["cur"], (1, 2, 0, 3)[L])
                                route(m)
                            if step == N - 2:
                                weigh_chosen(m)
                            if step == N - 1 and L == 3:
                                dve.scalar_tensor_tensor(x[:, :], n[:, :], tg[:, 7:8], x[:, :], ALU.mult, ALU.add).then_inc(s["xn"], 1)
                        if not m.gated and (k - 1) % N == N - 1 and not (isinstance(it, int) and step < N):
                            gate(it, (k - 1) // N)
                m.run(dve, body)
                e, k = m.experts - 1, (m.experts - 1) % U
                dve.wait_ge(s["acc"], e)
                for t in range(2):
                    dve.wait_ge(s["h_used"], m.down_total - 1 + t)
                    yy, xh, dst = ps[:, 4 + t], x[:, half(t)], y_g[:, k % 2, half(t)]
                    if e >= E:
                        dve.scalar_tensor_tensor(xh, yy, tg[:, 4 + L:5 + L], xh, ALU.mult, ALU.add).then_inc(x_done[t], 1)
                        continue
                    dve.wait_ge(s["gcp"], e + 1)
                    if m.biases:
                        link(dve.scalar_tensor_tensor(dst, yy, w_bias[:, k, m.biases - 1:m.biases], g_sb[:, k % 2, half(t)], ALU.add, ALU.mult))
                    else:
                        link(dve.tensor_tensor(dst, yy, g_sb[:, k % 2, half(t)], ALU.mult))
                    dve.tensor_tensor(xh, xh, dst, ALU.add).then_inc(x_done[t], 1)

            dve.memset(var_w[:, :], 1.0 / P)
            dve.memset(ones_w[:, :], 1.0)
            for e, tile in starts.items():
                link(dve.memset(tile[:, :], 1.0))
                dve.memset(tile[:, :].rearrange("p (c e) -> p c e", e=e)[:, :, 0], 0.0)
            dve.memset(minus_half[:, :], -0.5).then_inc(consts, 1)
            link(dve.memset(h_act[:, 0], DECAY))
            link(dve.memset(h_act[:, 0].rearrange("p (b s) -> p b s", s=S)[:, :, 0], 0.0))
            dve.wait_ge(pre["kv"], 1)
            dve.tensor_tensor_scan(h_act[:, 1], h_act[:, 0], diag[:, :], 0.0, ALU.mult, ALU.add).then_inc(pre["scan"], 1)
            dve.wait_ge(in_pack["p_first"], 16)
            norm(0)
            dve.wait_ge(pre["scan"], 1)
            dve.wait_ge(tg_ready, 1)
            for t in range(2):
                dve.wait_ge(ln["n"], t + 1)
                link(dve.scalar_tensor_tensor(n[:, half(t)], n[:, half(t)], tg[:, 0:1], h_act[:, 1, half(t)], ALU.mult, ALU.mult))
                dve.tensor_tensor(x[:, half(t)], x[:, half(t)], n[:, half(t)], ALU.add).then_inc(x_done[t], 1)
            dve.wait_ge(in_pack["p_attn1"], 16)
            dve.tensor_scalar(wqk1[:, 5], wqk1[:, 5], tg[:, 1:2], None, ALU.mult).then_inc(pre["wo"], 1)
            link(dve.tensor_scalar(abias[:, 5:6], abias[:, 4:5], tg[:, 1:2], None, ALU.mult))
            prepare_keys(0, 0)
            norm(1, lambda: prepare_keys(0, 1))
            moe(MOES[0])
            norm(2)
            for q in range(2):
                prepare_values(0, q)
            attention(0)
            norm_rest(3)
            moe(MOES[1])
            norm(4)
            pair_sums()
            norm_rest(5)
            moe(MOES[2])
            norm(6)
            attention(1)
            norm_rest(7)
            moe(MOES[3])

        @block.gpsimd
        def _(pool):
            link = linker(pool, pool_link)

            def norm(j):
                for t in range(2):
                    r = slice(t * HT, (t + 1) * HT)
                    pool.wait_ge(ln["eps"], 2 * j + t + 1)
                    pool.tensor_tensor(rstd[:, r], var_eps[:, r], minus_half[:, r], ALU.pow).then_inc(ln["rstd"], 1)

            def split_lo(m, it, k):
                s, U = mo[m.layer], m.unroll
                u, e = k % U, it * U + k
                o = u * m.width
                for hi, lo, c0, c1 in (("whu", "wlu", 0, m.up), ("whd", "wld", m.up, m.split)):
                    pool.wait_ge(s[hi], e + 1)
                    pool.tensor_tensor(w_lo[:, o + c0:o + c1], w_f32[:, o + c0:o + c1], w_hi[:, o + c0:o + c1].bitcast(F32),
                                       ALU.subtract).then_inc(s[lo], 1)

            def first_weights(m):
                for u in range(m.unroll):
                    split_lo(m, 0, u)

            def expand_keys(i, q):
                src = kT[i][:, 4 * q * S:4 * (q + 1) * S].rearrange("p (b k) -> p b k", b=4)
                pool.tensor_tensor(kexp[:, 4 * q:4 * q + 4], bcast(src, 2, 4), bcast(bcast(hmask, 2, S), 1, 4), ALU.mult).then_inc(at["kexp"], 1)

            def pair_sums():
                pool.wait_ge(x2["fb"], 2)
                pool.wait_ge(pre["txtcp"], 2)
                for g in POOL_SUMS:
                    if g >= 3:
                        pool.wait_ge(x2["tanh"], g - 2)
                    pool.tensor_tensor(*sum_of(g), ALU.add).then_inc(x2["sumB"], 1)

            def moe(m, then=None):
                s, U = mo[m.layer], m.unroll
                if m.layer != 2:
                    gate_parts(m, pool, link)
                if then:
                    then()
                if m.layer == 3:
                    pool.wait_ge(s["xn"], 1)

                def accumulate(it, k):
                    e = it * U + k
                    pool.wait_ge(s["gate"], m.gates * (e + 1))
                    if not (isinstance(it, int) and e == 0):
                        pool.wait_ge(s["acc"], e)
                    pool.tensor_tensor(x[:, :], x[:, :], y_g[:, k % 2], ALU.add).then_inc(s["acc"], 1)

                def body(it):
                    for k in range(U):
                        if isinstance(it, int) and it * U + k >= m.experts - 1:
                            break
                        accumulate(it, k)
                        if not isinstance(it, int) or it * U + k + U < m.experts:
                            split_lo(m, it, k + U)
                m.run(pool, body)

            for i in range(2):
                link(pool.memset(vblk[i][:].rearrange("p b h c -> p (b h c)"), 0.0))
                for h2 in range(2):
                    ones = vblk[i][64 * h2:64 * h2 + 64].rearrange("p b h (c d) -> p (b h) c d", c=2)[:, :, h2, 8:9]
                    link(pool.memset(ones, 1.0))
            pool.memset(gT[:, :], 0.0).then_inc(zeros, 1)
            pool.wait_ge(consts, 1)
            norm(0)
            first_weights(MOES[0])
            norm(1)
            pool.wait_ge(in_pack["p_attn1"], 16)
            pool.wait_ge(pre["k"], 2)
            for q in range(2):
                expand_keys(0, q)
            moe(MOES[0], lambda: (expand_keys(0, 2), expand_keys(0, 3)))
            norm(2)
            first_weights(MOES[1])
            norm(3)
            moe(MOES[1])
            norm(4)
            first_weights(MOES[2])
            pair_sums()
            norm(5)
            pool.wait_ge(pre["k"], 4)
            for q in range(2):
                expand_keys(1, q)
            moe(MOES[2], lambda: (expand_keys(1, 2), expand_keys(1, 3)))
            norm(6)
            first_weights(MOES[3])
            norm(7)
            moe(MOES[3])


def constants():
    c = {"ident": np.eye(P, dtype=np.float32)}
    c["cen"] = (np.eye(P) - 1.0 / P).astype(np.float32)
    one16 = np.uint16(0x3F80)
    c["ident16"] = np.eye(P, dtype=np.uint16) * one16
    for e in (8, 16):
        s = np.zeros((P, e, P), np.uint16)
        for r in range(3 * e):
            s[r, r % e] = one16
        c[f"sel{e}"] = s
    pair = (np.arange(P) % HD) // 2
    freq = (1.0 / 10000.0 ** (np.arange(0, HD, 2, dtype=np.float64) / HD)).astype(np.float32)[pair]
    ang = (np.arange(S, dtype=np.float32)[None, :] * freq[:, None]).astype(np.float32).astype(np.float64)
    sign = np.where(np.arange(P) % 2 == 0, -1.0, 1.0)[:, None]
    cos, sin = np.cos(ang), np.sin(ang) * sign
    scale = 1.0 / np.sqrt(HD)
    c["rope"] = np.stack([cos * scale, sin * scale, cos, sin], axis=1).astype(np.float32)
    c["hmask"] = (np.arange(P)[:, None] // HD % 4 == np.arange(4)[None, :]).astype(np.float32)
    c["rmask"] = (np.arange(P)[:, None] // (4 * HD) == np.arange(4)[None, :]).astype(np.float32)
    c["before"] = np.tile(np.tril(np.ones((4, 4), np.float32), -1).reshape(1, 16), (P, 1))
    perm = np.zeros((P, P), np.float32)
    for b in range(B):
        for h in range(2):
            for q in range(4):
                perm[32 * q + 2 * b + h, 8 * b + 4 * h + q] = 1.0
    c["perm"] = perm
    return c


def kernel(**inputs):
    import concourse.bacc as bacc
    from concourse.bass_utils import run_bass_kernel_spmd

    i = {k: np.asarray(v) for k, v in inputs.items()}
    f = np.ascontiguousarray

    def rows(v):
        return np.tile(v.reshape(1, -1), (P, 1))

    def chunked(w):
        e, h, d = w.shape
        c = -(-h // P)
        w = np.concatenate([w, np.zeros((e, c * P - h, d), w.dtype)], axis=1)
        return w.reshape(e, c, P, d).transpose(0, 2, 1, 3).reshape(e, P, c * d)

    def tr(w):
        return w.transpose(0, 2, 1)

    def col(v):
        return v.reshape(v.shape[0], -1, P).transpose(0, 2, 1)

    swap = np.arange(P) ^ 1

    def attention_weights(wq, wk, wv, wo):
        return np.stack([wq.T, wq[swap].T, wk.T, wk[swap].T, wv.T, wo.T], axis=1)

    small = constants()
    small["gates"] = rows(np.concatenate([i["g_xattn"], i["g_ffn"]]))
    small["attn1"] = attention_weights(*(i[f"L1_xattn_{k}"] for k in ("wq", "wk", "wv", "wo")))
    small["attn3"] = attention_weights(*(i[f"L3_xattn_W_{k}"] for k in "qkvo"))
    bq, bk, bo = i["L1_xattn_bq"], i["L1_xattn_bk"], i["L1_xattn_bo"]
    small["abias"] = np.stack([bq, bq[swap], bk, bk[swap], bo, bo, i["L1_xattn_bv"]], axis=1)
    small["wg0"], small["wg1"], small["wg2"] = i["L0_ffn_gate_w"].T, i["L1_ffn_Wg"].T, i["L2_ffn_Wg"].T
    small["wg3"], small["gb0"] = i["L3_ffn_router_w"], rows(i["L0_ffn_gate_b"])
    small["l2w"] = np.stack([i["L2_xattn_Ws"], i["L2_xattn_W"]], axis=1)
    small["l2pad"] = np.zeros((P, 63), np.float32)
    small["l2pad"][:, 31] = i["L2_xattn_w"][:, 0]
    small["l2uv"] = np.zeros((P, 2, 5, 32), np.float32)
    for r, k in enumerate(("L2_xattn_Wcw", "L2_xattn_Wcb")):
        small["l2uv"][:, r, :, 30:32] = i[k][0][:, None, None]
    small["l2uv"] = small["l2uv"].reshape(P, 2, 160)[:, :, 0:158]
    small["l2b"] = np.concatenate([i["L2_xattn_b"].T, rows(i["L2_xattn_bcw"]), rows(i["L2_xattn_bcb"])], axis=1)

    arr = {"xT": f(i["x"].reshape(T, P).T), "ctxT": f(i["ctx_1024"].reshape(T, P).T)}
    for name, fields in PACKS.items():
        arr[name] = f(np.concatenate([small[k].reshape(P, -1) for k in fields], axis=1))
    arr["w0"] = f(np.concatenate([i["L0_ffn_w1"], chunked(i["L0_ffn_w2"]), col(i["L0_ffn_b1"]), col(i["L0_ffn_b2"])], axis=2))
    arr["w1"] = f(np.concatenate([tr(i["L1_ffn_W1"]), tr(i["L1_ffn_W3"]), chunked(tr(i["L1_ffn_W2"]))], axis=2))
    arr["w2"] = f(np.concatenate([tr(i["L2_ffn_W1"]), tr(i["L2_ffn_W3"]), chunked(tr(i["L2_ffn_W2"])),
                                 col(i["L2_ffn_b1"]), col(i["L2_ffn_b3"]), col(i["L2_ffn_b2"])], axis=2))
    up3 = np.concatenate([i["L3_ffn_routed_up"], i["L3_ffn_shared_up"]], axis=0)
    dn3 = np.concatenate([i["L3_ffn_routed_down"], i["L3_ffn_shared_down"]], axis=0)
    arr["w3"] = f(np.concatenate([up3, chunked(dn3)], axis=2))
    arr["mask_rows"] = f(np.tile(np.repeat(i["mask_BxS2_ik0"], 2, axis=0), (4, 1)))

    nc = bacc.Bacc("TRN2", target_bir_lowering=False, num_devices=1)
    aps = {k: nc.dram_tensor(f"in_{k}", v.shape, mybir.dt.from_np(v.dtype), kind="ExternalInput").ap() for k, v in arr.items()}
    out = nc.dram_tensor("out_xT", (P, T), F32, kind="ExternalOutput").ap()
    flamingo(nc, aps, out)
    r = run_bass_kernel_spmd(nc, [{f"in_{k}": v for k, v in arr.items()}], core_ids=[0])
    return f(r.results[0]["out_xT"].T).reshape(B, S, P)
```
